# Optimizing a Trainium2 kernel written in Bass

```python
import numpy as np
import jax
import jax.numpy as jnp

def _softmax(x, axis=-1):
    return jax.nn.softmax(x, axis=axis)

def _gelu(x):
    return jax.nn.gelu(x, approximate=True)

def _silu(x):
    return jax.nn.silu(x)

def _sigmoid(x):
    return jax.nn.sigmoid(x)

def _layernorm(x, axis=-1, eps=1e-05):
    m = jnp.mean(x, axis=axis, keepdims=True)
    v = jnp.var(x, axis=axis, keepdims=True)
    return (x - m) / jnp.sqrt(v + eps)

def _scatter_add(tgt, idx, src, axis=0):
    return tgt.at[idx].add(src)

def _segment_sum(src, seg, n):
    return jax.ops.segment_sum(src, seg, n)
kernel_name = 'mk_macaron_d1_jaxref_r4_f59096'

def setup_inputs(seed: int=0):
    np.random.seed(seed)
    _w = jnp.asarray

    def _L0_attn_setup():
        import jax, jax.numpy as jnp
        import numpy as np
        B, S, D = (2, 512, 512)
        HQ = 16
        DH = D // HQ
        key = jax.random.key(seed)
        ks = jax.random.split(key, 9)
        sd = 1.0 / np.sqrt(D)
        return {'x': jax.random.normal(ks[0], (B, S, D), jnp.float32), 'Wq': jax.random.normal(ks[1], (D, D), jnp.float32) * sd, 'bq': jnp.zeros((D,), jnp.float32), 'Wk': jax.random.normal(ks[2], (D, DH), jnp.float32) * sd, 'bk': jnp.zeros((DH,), jnp.float32), 'Wv': jax.random.normal(ks[3], (D, DH), jnp.float32) * sd, 'bv': jnp.zeros((DH,), jnp.float32), 'Wo': jax.random.normal(ks[4], (D, D), jnp.float32) * sd, 'bo': jnp.zeros((D,), jnp.float32)}
    _L0_attn_in = _L0_attn_setup()

    def _L0_ffn_setup():
        import jax, jax.numpy as jnp
        import numpy as np
        TOPK = 6
        CAP = 256
        ROUTE_SCALE = 1.0
        key = jax.random.key(seed)
        k = jax.random.split(key, 6)
        B, T, C = (2, 512, 512)
        E, H, HS = (64, 64, 128)
        std = 0.01
        return {'x': jax.random.normal(k[0], (B, T, C), jnp.float32), 'w_gate': jax.random.normal(k[1], (C, E), jnp.float32) * std, 'w_shared_up': jax.random.normal(k[2], (C, 2 * HS), jnp.float32) * std, 'w_shared_down': jax.random.normal(k[3], (HS, C), jnp.float32) * std, 'w_up': jax.random.normal(k[4], (E, C, 2 * H), jnp.float32) * std, 'w_down': jax.random.normal(k[5], (E, H, C), jnp.float32) * std}
    _L0_ffn_in = _L0_ffn_setup()
    _d = {'L0_attn_x': _L0_attn_in['x'], 'L0_attn_Wq': _L0_attn_in['Wq'], 'L0_attn_bq': _L0_attn_in['bq'], 'L0_attn_Wk': _L0_attn_in['Wk'], 'L0_attn_bk': _L0_attn_in['bk'], 'L0_attn_Wv': _L0_attn_in['Wv'], 'L0_attn_bv': _L0_attn_in['bv'], 'L0_attn_Wo': _L0_attn_in['Wo'], 'L0_attn_bo': _L0_attn_in['bo'], 'L0_ffn_w_gate': _L0_ffn_in['w_gate'], 'L0_ffn_w_shared_up': _L0_ffn_in['w_shared_up'], 'L0_ffn_w_shared_down': _L0_ffn_in['w_shared_down'], 'L0_ffn_w_up': _L0_ffn_in['w_up'], 'L0_ffn_w_down': _L0_ffn_in['w_down']}
    _x0 = _d['L0_attn_x']
    _d['L0_attn_x'] = jax.random.normal(jax.random.fold_in(jax.random.key(seed), 1), (2, 2048, 512), dtype=_x0.dtype)
    del _x0
    return _d

def reference(L0_attn_x, L0_attn_Wq, L0_attn_bq, L0_attn_Wk, L0_attn_bk, L0_attn_Wv, L0_attn_bv, L0_attn_Wo, L0_attn_bo, L0_ffn_w_gate, L0_ffn_w_shared_up, L0_ffn_w_shared_down, L0_ffn_w_up, L0_ffn_w_down):

    def _L0_attn_ref(x, Wq, bq, Wk, bk, Wv, bv, Wo, bo):
        import jax, jax.numpy as jnp
        import numpy as np
        B, S, D = (2, 512, 512)
        HQ = 16
        DH = D // HQ
        b, s, d = x.shape
        scale = jnp.sqrt(jnp.asarray(DH, x.dtype))
        q = (x @ Wq + bq).reshape(b, s, HQ, DH).transpose(0, 2, 1, 3)
        k = x @ Wk + bk
        v = x @ Wv + bv
        scores = jnp.einsum('bhsd,btd->bhst', q, k) / scale
        attn = jax.nn.softmax(scores, axis=-1)
        out = jnp.einsum('bhst,btd->bhsd', attn, v)
        out = out.transpose(0, 2, 1, 3).reshape(b, s, HQ * DH)
        return out @ Wo + bo

    def _L0_ffn_ref(x, w_gate, w_shared_up, w_shared_down, w_up, w_down):
        import jax, jax.numpy as jnp
        import numpy as np
        TOPK = 6
        CAP = 256
        ROUTE_SCALE = 1.0
        B, T, C = x.shape
        E = w_gate.shape[1]
        x_flat = x.reshape(-1, C)
        N = x_flat.shape[0]
        su = x_flat @ w_shared_up
        y_s, g_s = jnp.split(su, 2, axis=-1)
        shared = jax.nn.silu(g_s) * y_s @ w_shared_down
        scores = jax.nn.sigmoid(x_flat @ w_gate)
        _, topk_idx = jax.lax.top_k(scores, TOPK)
        w = jnp.take_along_axis(scores, topk_idx, axis=-1)
        w = w / w.sum(-1, keepdims=True) * ROUTE_SCALE
        flat_e = topk_idx.reshape(-1)
        oh = jax.nn.one_hot(flat_e, E, dtype=jnp.int32)
        pos = jnp.take_along_axis(jnp.cumsum(oh, axis=0), flat_e[:, None], axis=1)[:, 0] - 1
        valid = pos < CAP
        pos_c = jnp.where(valid, pos, CAP - 1)
        token_ids = jnp.repeat(jnp.arange(N), TOPK)
        x_disp = jnp.zeros((E, CAP, C), x.dtype).at[flat_e, pos].set(x_flat[token_ids], mode='drop')
        up = jnp.einsum('ecd,edh->ech', x_disp, w_up)
        g_r, v_r = jnp.split(up, 2, axis=-1)
        h_r = jax.nn.silu(g_r) * v_r
        out_r = jnp.einsum('ech,ehd->ecd', h_r, w_down)
        y_ts = out_r[flat_e, pos_c]
        y_ts = jnp.where(valid[:, None], y_ts, 0.0)
        routed = (y_ts.reshape(N, TOPK, C) * w[:, :, None]).sum(axis=1)
        return (shared + routed).reshape(B, T, C)
    x = L0_attn_x
    x = x + 0.5 * _L0_ffn_ref(_layernorm(x, axis=-1), L0_ffn_w_gate, L0_ffn_w_shared_up, L0_ffn_w_shared_down, L0_ffn_w_up, L0_ffn_w_down)
    x = x + _L0_attn_ref(_layernorm(x, axis=-1), L0_attn_Wq, L0_attn_bq, L0_attn_Wk, L0_attn_bk, L0_attn_Wv, L0_attn_bv, L0_attn_Wo, L0_attn_bo)
    x = x + 0.5 * _L0_ffn_ref(_layernorm(x, axis=-1), L0_ffn_w_gate, L0_ffn_w_shared_up, L0_ffn_w_shared_down, L0_ffn_w_up, L0_ffn_w_down)
    return x

_drawn_inputs = setup_inputs


def setup_inputs(seed=0):
    import zlib

    import numpy as np

    out = dict(_drawn_inputs(seed))
    spreads = {'L0_attn_bq': (0.0, 0.8),
     'L0_attn_bk': (0.0, 0.8),
     'L0_attn_bv': (0.0, 0.1),
     'L0_attn_bo': (0.0, 0.1)}
    factors = {'L0_ffn_w_gate': 8.0,
     'L0_ffn_w_shared_up': 8.0,
     'L0_ffn_w_shared_down': 8.0,
     'L0_ffn_w_up': 8.0,
     'L0_ffn_w_down': 8.0}
    for name, (base, spread) in spreads.items():
        noise = np.random.default_rng([zlib.crc32(name.encode()), seed]).standard_normal(out[name].shape)
        drawn = base * np.exp(spread * noise) if base else spread * noise
        out[name] = jnp.asarray(drawn.astype(out[name].dtype))
    for name, factor in factors.items():
        out[name] = (out[name] * factor).astype(out[name].dtype)
    return out
```

```python
from contextlib import ExitStack

import concourse.bass as bass
from concourse import mybir

F32 = mybir.dt.float32
F32R = mybir.dt.float32r
BF16 = mybir.dt.bfloat16
U32 = mybir.dt.uint32
ALU = mybir.AluOpType
ACT = mybir.ActivationFunctionType
X = mybir.AxisListType.X

P = 128
B, S, C = 2, 2048, 512
N = B * S
NT = N // P
CK = C // P
E, H, HS = 64, 64, 128
TOPK, CAP = 6, 256
EPS = 1e-5
SKIP = 65536.0
ROWS = E * CAP
HALVES = CAP // P
TURN = 4
NTURN = NT // TURN


class Flag:

    AHEAD = 16
    passed = {}

    def __init__(self, sem, ahead=AHEAD):
        self.sem, self.ahead = sem, ahead

    def start(self, eng):
        eng.sem_inc(self.sem, self.ahead)

    def wait(self, eng, count, apart=False):
        eng.wait_ge(self.sem, count + self.ahead)
        if apart or eng.engine == mybir.EngineType.Pool:
            eng.sem_inc(self.passed[eng.engine], 1)


class Steps:

    def __init__(self, eng, flag, per_turn=0, before=0):
        self.eng, self.flag, self.per_turn, self.before = eng, flag, per_turn, before
        self.base, self.k = 0, 0

    def turn(self, i):
        self.base, self.k = i * self.per_turn + self.before, 0

    def __call__(self, ins):
        ins.then_inc(self.flag.sem, 1)
        self.k += 1
        return self.k

    def wait(self, k=None, apart=False):
        self.flag.wait(self.eng, self.base + (self.k if k is None else k), apart)

    def end(self):
        assert self.k == self.per_turn, (self.k, self.per_turn)


class Memory:

    def __init__(self, nc, ctx, tag):
        self.nc, self.ctx, self.tag = nc, ctx, tag

    def sb(self, name, shape, dt=F32):
        return self.ctx.enter_context(self.nc.sbuf_tensor(f"{self.tag}_{name}", shape, dt))

    def ps(self, name, shape, dt=F32):
        return self.ctx.enter_context(self.nc.psum_tensor(f"{self.tag}_{name}", shape, dt))

    def flag(self, name):
        return Flag(self.nc.alloc_semaphore(f"{self.tag}_{name}"))

    def flags(self, name, n):
        return [self.flag(f"{name}{i}") for i in range(n)]

    def pool_dmas(self, name):
        return Flag(self.nc.alloc_semaphore(f"{self.tag}_{name}"), ahead=0)


def start(eng, *signals):
    for s in signals:
        s.start(eng)


def setup(nc, ctx, x_in, tables):
    m = Memory(nc, ctx, "c")
    k = {
        "x": m.sb("x", [P, NT, C]),
        "ident": m.sb("ident", [P, P]),
        "tri": m.sb("tri", [P, P], BF16),
        "ones": m.sb("ones", [P, P], BF16),
        "ones32": m.sb("ones32", [P, 32]),
        "half": m.sb("half", [P, TURN]),
        "expert": m.sb("expert", [P, E]),
        "token": m.sb("token", [P, NT], U32),
        "zero": m.sb("zero", [P, P], U32),
    }
    s_load, s_zero, s_set, s_tab = (m.flag(n) for n in ("load", "zero", "set", "tab"))
    x_view = x_in.rearrange("b (i p) c -> p (b i) c", p=P)
    with nc.Block() as block:
        @block.sync
        def _(sp):
            start(sp, s_load, s_tab)
            for q in range(4):
                part = slice(q * NT // 4, (q + 1) * NT // 4)
                sp.dma_start(k["x"][:, part, :], x_view[:, part, :]).then_inc(s_load.sem, 16)
            s_zero.wait(sp, 1)
            for table in tables:
                sp.dma_start(table.rearrange("(p n) a -> p (n a)", p=P), k["zero"][:, :]).then_inc(s_tab.sem, 16)
            s_tab.wait(sp, 16 * len(tables))
            s_load.wait(sp, 4 * 16)

        @block.gpsimd
        def _(pool):
            start(pool, s_zero, s_set)
            pool.memset(k["zero"][:, :], 0).then_inc(s_zero.sem, 1)
            pool.memset(k["ident"][:, :], 0.0).then_inc(s_set.sem, 1)
            pool.memset(k["tri"][:, :], 1.0).then_inc(s_set.sem, 1)
            pool.memset(k["ones"][:, :], 1.0).then_inc(s_set.sem, 1)
            pool.memset(k["ones32"][:, :], 1.0).then_inc(s_set.sem, 1)
            pool.memset(k["half"][:, :], -0.5).then_inc(s_set.sem, 1)
            pool.iota(k["expert"][:, :], pattern=[[1, E]], base=0, channel_multiplier=0,
                      allow_small_or_imprecise_dtypes=True).then_inc(s_set.sem, 1)
            pool.iota(k["token"][:, :], pattern=[[P, NT]], base=0, channel_multiplier=1).then_inc(s_set.sem, 1)
            s_set.wait(pool, 7)
            pool.affine_select(out=k["ident"][:, :], in_=k["ident"][:, :], compare_op=ALU.not_equal, fill=1.0,
                               base=0, pattern=[[-1, P]], channel_multiplier=1).then_inc(s_set.sem, 1)
            pool.affine_select(out=k["tri"][:, :], in_=k["tri"][:, :], compare_op=ALU.is_gt, fill=0.0,
                               base=0, pattern=[[1, P]], channel_multiplier=-1).then_inc(s_set.sem, 1)
            s_set.wait(pool, 9)
    return k


def route(nc, tag, k, wts, xn_d, tab_d, keep):
    w_gate, w_su, w_sd = wts
    with ExitStack() as ctx:
        m = Memory(nc, ctx, tag)
        wg = m.sb("wg", [P, CK, E])
        wsu = m.sb("wsu", [P, CK, 2 * HS])
        wsd = m.sb("wsd", [P, C])
        stats = m.sb("stats", [P, TURN, 6])
        mv = m.sb("mv", [P, TURN, 2])
        ve = m.sb("ve", [P, TURN])
        rstd = m.sb("rstd", [P, TURN])
        xn = m.sb("xn", [P, TURN, C])
        xT = m.sb("xT", [P, 2, CK, P])
        sc = m.sb("sc", [P, TURN, E])
        sg = m.sb("sg", [P, 2, P])
        gs = m.sb("gs", [P, 2, P])
        hs = m.sb("hs", [P, 2, P])
        v8 = m.sb("v8", [P, TURN, 8])
        i8 = m.sb("i8", [P, TURN, 8], U32)
        i8f = m.sb("i8f", [P, TURN, 8])
        eq = m.sb("eq", [P, TURN, TOPK, E])
        eqp = m.sb("eqp", [P, TURN, TOPK, E])
        mask = m.sb("mask", [P, TURN, E], BF16)
        msum = m.sb("msum", [P, E], BF16)
        cum = m.sb("cum", [P, E], BF16)
        pos = m.sb("pos", [P, TURN, TOPK])
        far = m.sb("far", [P, TURN, TOPK])
        addr = m.sb("addr", [P, TURN, TOPK])
        over = m.sb("over", [P, TURN, TOPK])
        live = m.sb("live", [P, TURN, TOPK])
        wsum = m.sb("wsum", [P, TURN])
        wrec = m.sb("wrec", [P, TURN])
        slot = m.sb("slot", [P, TURN, TOPK], U32)
        tok = m.sb("tok", [P, TURN], U32)
        pT = m.ps("pT", [P, 2, CK, P])
        pU = m.ps("pU", [P, 2, 512])
        pD = m.ps("pD", [P, 2, C])
        pP = m.ps("pP", [P, 512])

        s_w = m.flag("w")
        s_dve = m.flag("dve")
        s_ve = m.flag("ve")
        s_rs = m.flag("rs")
        s_xn = m.flag("xn")
        s_st = [m.flag(f"st{j}") for j in range(TURN)]
        s_tr = m.flag("tr")
        s_xT = m.flag("xT")
        s_up = m.flag("up")
        s_sg = m.flag("sg")
        s_hs = m.flag("hs")
        s_dn = m.flag("dn")
        s_rd = m.flag("rd")
        s_mask = m.flag("mask")
        s_pos = m.flag("pos")
        s_slot = m.flag("slot")
        s_tok = m.flag("tok")
        s_sc = m.pool_dmas("sc")
        s_in = m.flag("in")

        with nc.Block() as block:
            @block.sync
            def _(sp):
                start(sp, s_w, *s_st)
                sp.dma_start(wg[:, :, :], w_gate.rearrange("(k p) e -> p k e", p=P)).then_inc(s_w.sem, 16)
                sp.dma_start(wsu[:, :, :], w_su.rearrange("(k p) e -> p k e", p=P)).then_inc(s_w.sem, 16)
                sp.dma_start(wsd[:, :], w_sd).then_inc(s_w.sem, 16)
                with sp.Fori(0, NTURN) as i:
                    for j in range(TURN):
                        s_xn.wait(sp, i * TURN + j + 1)
                        sp.dma_start(xn_d[bass.ds(i * (TURN * P) + j * P, P), :], xn[:, j, :]).then_inc(s_st[j].sem, 16)
                for j in range(TURN):
                    s_st[j].wait(sp, 16 * NTURN)

            @block.gpsimd
            def _(pool):
                start(pool, s_rs, s_tok, s_in)

                def rsqrt(i):
                    s_ve.wait(pool, i + 1)
                    pool.tensor_tensor(rstd[:, :], ve[:, :], k["half"][:, :], ALU.pow).then_inc(s_rs.sem, 1)

                def scatter(i):
                    pool.tensor_copy(tok[:, :], k["token"][:, bass.ds(i * TURN, TURN)]).then_inc(s_tok.sem, 1)
                    s_tok.wait(pool, i + 1)
                    s_slot.wait(pool, i + 1)
                    for j in range(TURN):
                        for q in range(TOPK):
                            pool.indirect_dma_start(
                                tab_d, bass.IndirectOffsetOnAxis(ap=slot[:, j, q:q + 1], axis=0),
                                tok[:, j:j + 1], None, bounds_check=ROWS - 1, oob_is_err=False).then_inc(s_sc.sem, 16)
                    s_sc.wait(pool, (i + 1) * (16 * TURN * TOPK))
                    pool.sem_inc(s_in.sem, 1)

                rsqrt(0)
                with pool.Fori(1, NTURN) as i:
                    rsqrt(i)
                    scatter(i - 1)
                scatter(NTURN - 1)

            @block.tensor
            def _(pe):
                start(pe, s_tr, s_up, s_dn, s_pos)

                def transposes(i, j):
                    s_xn.wait(pe, i * TURN + j + 1)
                    s_xT.wait(pe, i * TURN + j - 1)
                    for c in range(CK):
                        t = pe.transpose(pT[:, j % 2, c, :], xn[:, j, c * P:(c + 1) * P], k["ident"][:, :])
                    t.then_inc(s_tr.sem, 1)

                def products(i, j):
                    s_xT.wait(pe, i * TURN + j + 1)
                    s_hs.wait(pe, i * TURN + j - 1)
                    h = j % 2
                    for o, w, n in ((256, wg[:, :, :], E),):
                        for c in range(CK):
                            pe.matmul(pU[:, h, o:o + n], xT[:, h, c, :], w[:, c, :], start=c == 0, stop=c == CK - 1)
                    for o in (0, HS):
                        for c in range(CK):
                            t = pe.matmul(pU[:, h, o:o + P], wsu[:, c, o:o + HS], xT[:, h, c, :],
                                          start=c == 0, stop=c == CK - 1)
                    t.then_inc(s_up.sem, 1)

                def down(i, j):
                    s_hs.wait(pe, i * TURN + j + 1)
                    s_rd.wait(pe, i * TURN + j - 1)
                    pe.matmul(pD[:, j % 2, :], hs[:, j % 2, :], wsd[:, :], start=True, stop=True).then_inc(s_dn.sem, 1)

                def positions(i):
                    s_mask.wait(pe, i + 1)
                    for j in range(TURN):
                        o = pP[:, j * E:(j + 1) * E]
                        pe.matmul(o, k["tri"][:, :], mask[:, j, :], start=True, stop=False)
                        for q in range(j):
                            pe.matmul(o, k["ones"][:, :], mask[:, q, :], start=False, stop=False)
                        t = pe.matmul(o, k["ones"][:, :], cum[:, :], start=False, stop=True)
                    t.then_inc(s_pos.sem, 1)

                s_w.wait(pe, 3 * 16)
                with pe.Fori(0, NTURN) as i:
                    for f, j in ((transposes, 0), (transposes, 1), (products, 0), (transposes, 2), (products, 1),
                                 (down, 0), (transposes, 3), (products, 2), (down, 1), (products, 3), (down, 2),
                                 (down, 3)):
                        f(i, j)
                    positions(i)

            @block.scalar
            def _(act):
                start(act, s_xT, s_sg)

                def copy_T(i, j):
                    s_tr.wait(act, i * TURN + j + 1)
                    s_up.wait(act, i * TURN + j - 1)
                    act.activation(xT[:, j % 2, :, :], pT[:, j % 2, :, :], ACT.Copy).then_inc(s_xT.sem, 1)

                def sigmoids(i, j):
                    s_up.wait(act, i * TURN + j + 1)
                    s_hs.wait(act, i * TURN + j - 1)
                    act.activation(sc[:, j, :], pU[:, j % 2, 256:256 + E], ACT.Sigmoid)
                    act.activation(sg[:, j % 2, :], pU[:, j % 2, HS:2 * HS], ACT.Sigmoid).then_inc(s_sg.sem, 1)

                with act.Fori(0, NTURN) as i:
                    for f, j in ((copy_T, 0), (copy_T, 1), (sigmoids, 0), (copy_T, 2), (sigmoids, 1), (copy_T, 3),
                                 (sigmoids, 2), (sigmoids, 3)):
                        if j == 0 and f is sigmoids:
                            s_rd.wait(act, i * TURN)
                            s_slot.wait(act, i)
                        f(i, j)

            @block.vector
            def _(dve):
                start(dve, s_dve, s_ve, s_xn, s_hs, s_rd, s_mask, s_slot)
                step = Steps(dve, s_dve, per_turn=36, before=1)

                def hidden(i, j):
                    s_sg.wait(dve, i * TURN + j + 1)
                    s_dn.wait(dve, i * TURN + j - 1)
                    h = j % 2
                    step(dve.tensor_tensor(gs[:, h, :], sg[:, h, :], pU[:, h, HS:2 * HS], ALU.mult))
                    step.wait()
                    dve.tensor_tensor(hs[:, h, :], gs[:, h, :], pU[:, h, 0:HS], ALU.mult).then_inc(s_hs.sem, 1)

                def residual(i, j):
                    s_dn.wait(dve, i * TURN + j + 1)
                    x = k["x"][:, bass.ds(i * TURN + j, 1), :].rearrange("p a c -> p (a c)")
                    dve.scalar_tensor_tensor(x, pD[:, j % 2, :], 0.5, x, ALU.mult, ALU.add).then_inc(s_rd.sem, 1)

                step(dve.memset(cum[:, :], 0.0))
                with dve.Fori(0, NTURN) as i:
                    step.turn(i)
                    for j in range(TURN):
                        x = k["x"][:, bass.ds(i * TURN + j, 1), :].rearrange("p a c -> p (a c)")
                        step(dve.bn_stats(stats[:, j, :], x))
                    for j in range(TURN):
                        step.wait(j + 1, apart=True)
                        step(dve.bn_aggr(mv[:, j, :], stats[:, j, :]))
                    step.wait()
                    dve.tensor_scalar(ve[:, :], mv[:, :, 1], EPS, None, ALU.add).then_inc(s_ve.sem, 1)
                    s_rs.wait(dve, i + 1)
                    for j in range(TURN):
                        s_st[j].wait(dve, i * 16)
                        s_tr.wait(dve, i * TURN)
                        x = k["x"][:, bass.ds(i * TURN + j, 1), :].rearrange("p a c -> p (a c)")
                        dve.tensor_scalar(xn[:, j, :], x, mv[:, j, 0:1], rstd[:, j:j + 1],
                                          ALU.subtract, ALU.mult).then_inc(s_xn.sem, 1)
                    s_xn.wait(dve, (i + 1) * TURN)
                    for f, j in ((hidden, 0), (hidden, 1), (residual, 0), (hidden, 2), (residual, 1), (hidden, 3),
                                 (residual, 2), (residual, 3)):
                        f(i, j)
                    for j in range(TURN):
                        step(dve.max(v8[:, j, :], sc[:, j, :]))
                        step.wait(apart=True)
                        step(dve.max_index(i8[:, j, :], v8[:, j, :], sc[:, j, :]))
                    step.wait()
                    step(dve.tensor_copy(i8f[:, :, :], i8[:, :, :]))
                    step.wait()
                    step(dve.tensor_tensor(
                        eq[:, :, :, :],
                        k["expert"][:, :].unsqueeze(1).unsqueeze(1).to_broadcast([P, TURN, TOPK, E]),
                        i8f[:, :, 0:TOPK].unsqueeze(3).to_broadcast([P, TURN, TOPK, E]), ALU.is_equal))
                    step.wait()
                    s_pos.wait(dve, i)
                    dve.tensor_reduce(mask[:, :, :], eq[:, :, :, :].rearrange("p j q e -> p j e q"), X,
                                      ALU.max).then_inc(s_mask.sem, 1)
                    s_mask.wait(dve, i + 1)
                    step(dve.tensor_reduce(wsum[:, :], v8[:, :, 0:TOPK], X, ALU.add))
                    step.wait()
                    step(dve.reciprocal(wrec[:, :], wsum[:, :]))
                    s_pos.wait(dve, i + 1)
                    step(dve.tensor_tensor(
                        eqp[:, :, :, :], eq[:, :, :, :],
                        pP[:, 0:TURN * E].rearrange("p (j e) -> p j e", e=E).unsqueeze(2)
                        .to_broadcast([P, TURN, TOPK, E]), ALU.mult))
                    with nc.allow_low_precision(reason="counts up to 32 are exact in bfloat16"):
                        step(dve.tensor_reduce(msum[:, :], mask[:, :, :].rearrange("p j e -> p e j"), X, ALU.add))
                    step.wait()
                    step(dve.tensor_reduce(pos[:, :, :], eqp[:, :, :, :], X, ALU.add))
                    step(dve.tensor_tensor(cum[:, :], cum[:, :], msum[:, :], ALU.add))
                    step.wait()
                    step(dve.tensor_scalar(far[:, :, :], pos[:, :, :], float(P), float(1 - P * P), ALU.is_ge, ALU.mult))
                    step(dve.tensor_scalar(over[:, :, :], pos[:, :, :], float(CAP), SKIP, ALU.is_ge, ALU.mult))
                    step(dve.tensor_scalar(live[:, :, :], pos[:, :, :], float(CAP), 0.5, ALU.is_lt, ALU.mult))
                    step.wait()
                    step(dve.scalar_tensor_tensor(addr[:, :, :], i8f[:, :, 0:TOPK], float(HALVES), far[:, :, :],
                                                  ALU.mult, ALU.add))
                    step(dve.tensor_tensor(live[:, :, :], live[:, :, :], v8[:, :, 0:TOPK], ALU.mult))
                    step.wait()
                    step(dve.scalar_tensor_tensor(addr[:, :, :], pos[:, :, :], float(P), addr[:, :, :],
                                                  ALU.mult, ALU.add))
                    step(dve.tensor_tensor(keep["w"][:, bass.ds(i * TURN, TURN), :], live[:, :, :],
                                           wrec[:, :].unsqueeze(2).to_broadcast([P, TURN, TOPK]), ALU.mult))
                    step.wait()
                    s_in.wait(dve, i)
                    dve.tensor_tensor(slot[:, :, :], addr[:, :, :], over[:, :, :], ALU.add).then_inc(s_slot.sem, 1)
                    step(dve.tensor_tensor(keep["slot"][:, bass.ds(i * TURN, TURN), :], addr[:, :, :],
                                           over[:, :, :], ALU.add))
                    step.wait()
                    step.end()


def experts(nc, tag, k, w_up, w_down, xn_d, tab_d, out_d):
    PAIRS = E // 2
    Q = 2 * HALVES
    up_view = w_up.rearrange("(g a) (c p) h -> g p a c h", a=2, p=P)
    down_view = w_down.rearrange("(g a) h c -> g (a h) c", a=2)
    out_view = out_d.rearrange("(p n) c -> p n c", p=P)
    with ExitStack() as ctx:
        m = Memory(nc, ctx, tag)
        table = m.sb("table", [P, P], U32)
        idx = [m.sb(f"idx{b}", [P, Q], U32) for b in range(2)]
        rows = [m.sb(f"rows{b}", [P, Q, C]) for b in range(2)]
        wup = [m.sb(f"wup{b}", [P, 2, CK, 2 * H]) for b in range(2)]
        wdn = [m.sb(f"wdn{b}", [P, C]) for b in range(2)]
        xT = [m.sb(f"xT{b}", [P, CK, 2, CAP]) for b in range(2)]
        sg = m.sb("sg", [P, CAP])
        gs = m.sb("gs", [P, CAP])
        hid = [m.sb(f"hid{a}", [P, CAP]) for a in range(2)]
        res = [m.sb(f"res{b}", [P, Q, C]) for b in range(2)]
        pT = m.ps("pT", [P, 2, 2, 512])
        pU = m.ps("pU", [P, 2, CAP])
        pD = m.ps("pD", [P, 2, C])

        s_tab = m.flag("tab")
        s_idx = m.flag("idx")
        s_g = [m.pool_dmas(f"g{b}") for b in range(2)]
        s_w = m.flags("w", 2)
        s_o = m.flags("o", 2)
        s_tr = m.flag("tr")
        s_ca = m.flag("ca")
        s_cd = m.flag("cd")
        s_up = m.flag("up")
        s_sg = m.flag("sg")
        s_gs = m.flag("gs")
        s_hid = m.flag("hid")
        s_dn = m.flag("dn")
        s_ea = m.flag("ea")
        s_ed = m.flag("ed")
        s_z = m.flag("z")

        def skewed(eng, stage_in, stage_up, stage_down):
            stage_in(0, 0)
            stage_up(0, 0)
            with eng.Fori(0, PAIRS // 2 - 1) as i:
                for b in (1, 0):
                    stage_in(i * 2 + (2 - b), b)
                    stage_down(i * 2 + (1 - b), 1 - b)
                    stage_up(i * 2 + (2 - b), b)
            stage_in(PAIRS - 1, 1)
            stage_down(PAIRS - 2, 0)
            stage_up(PAIRS - 1, 1)
            stage_down(PAIRS - 1, 1)

        with nc.Block() as block:
            @block.sync
            def _(sp):
                start(sp, s_tab, *s_w)
                sp.dma_start(table[:, :], tab_d.rearrange("(p n) a -> p (n a)", p=P)).then_inc(s_tab.sem, 16)
                with sp.Fori(0, PAIRS // 2) as i:
                    for b in range(2):
                        s_up.wait(sp, i * 2 + b - 1)
                        s_w[b].wait(sp, i * 48)
                        for a in range(2):
                            sp.dma_start(wup[b][:, a, :, :], up_view[bass.ds(i * 2 + b, 1), :, a, :, :]
                                         .rearrange("g p c h -> (g p) c h")).then_inc(s_w[b].sem, 16)
                        s_dn.wait(sp, (i * 2 + b - 1) * Q)
                        sp.dma_start(wdn[b][:, :], down_view[bass.ds(i * 2 + b, 1), :, :]
                                     .rearrange("g p c -> (g p) c")).then_inc(s_w[b].sem, 16)
                for b in range(2):
                    s_w[b].wait(sp, 48 * PAIRS // 2)

            @block.gpsimd
            def _(pool):
                start(pool, s_idx)
                s_tab.wait(pool, 16)
                with pool.Fori(0, PAIRS // 2) as i:
                    for b in range(2):
                        s_tr.wait(pool, (i * 2 + b - 1) * 2)
                        pool.tensor_copy(idx[b][:, :], table[:, bass.ds((i * 2 + b) * Q, Q)]).then_inc(s_idx.sem, 1)
                        s_idx.wait(pool, i * 2 + b + 1)
                        for q in range(Q):
                            pool.indirect_dma_start(
                                rows[b][:, q, :], None, xn_d,
                                bass.IndirectOffsetOnAxis(ap=idx[b][:, q:q + 1], axis=0)).then_inc(s_g[b].sem, 16)
                for b in range(2):
                    s_g[b].wait(pool, 16 * Q * PAIRS // 2)

            @block.tensor
            def _(pe):
                start(pe, s_tr, s_up, s_dn)

                def gathered(e, b):
                    s_g[b].wait(pe, (e + (2 - b)) * (8 * Q))
                    for a in range(2):
                        s_ca.wait(pe, e * 2 + a - 1)
                        s_cd.wait(pe, e * 2 + a - 1)
                        for c in range(CK):
                            for h in range(HALVES):
                                o = (c % 2) * CAP + h * P
                                t = pe.transpose(pT[:, a, c // 2, o:o + P],
                                                 rows[b][:, a * HALVES + h, c * P:(c + 1) * P], k["ident"][:, :])
                        t.then_inc(s_tr.sem, 1)

                def up(e, b):
                    s_w[b].wait(pe, (e + (2 - b)) * 24)
                    s_ca.wait(pe, (e + 1) * 2)
                    s_cd.wait(pe, (e + 1) * 2)
                    s_hid.wait(pe, e)
                    for v in range(2):
                        for c in range(CK):
                            for a in range(2):
                                t = pe.matmul(pU[a * H:(a + 1) * H, v, :], wup[b][:, a, c, v * H:(v + 1) * H],
                                              xT[b][:, c, a, :], start=c == 0, stop=c == CK - 1)
                    t.then_inc(s_up.sem, 1)

                def down(e, b):
                    s_hid.wait(pe, e + 1)
                    for q in range(Q):
                        (s_ea, s_ed)[q % 2].wait(pe, e * 2 + q // 2)
                        pe.matmul(pD[:, q % 2, :], hid[q // HALVES][:, (q % HALVES) * P:(q % HALVES + 1) * P],
                                  wdn[b][:, :], start=True, stop=True).then_inc(s_dn.sem, 1)

                skewed(pe, gathered, up, down)

            @block.scalar
            def _(act):
                start(act, s_ca, s_sg, s_ea, *s_o)

                def gathered(e, b):
                    for a in range(2):
                        s_tr.wait(act, e * 2 + a + 1)
                        s_up.wait(act, e - 1)
                        act.activation(xT[b][:, 0:2, a, :], pT[:, a, 0, :].rearrange("p (c n) -> p c n", c=2),
                                       ACT.Copy).then_inc(s_ca.sem, 1)

                def up(e, b):
                    s_up.wait(act, e + 1)
                    s_gs.wait(act, e)
                    act.activation(sg[:, :], pU[:, 0, :], ACT.Sigmoid).then_inc(s_sg.sem, 1)

                def down(e, b):
                    s_o[b].wait(act, (e - b) * 8)
                    for q in (0, 2):
                        s_dn.wait(act, e * Q + q + 1)
                        act.activation(res[b][:, q, :], pD[:, 0, :], ACT.Copy).then_inc(s_ea.sem, 1)
                    s_ea.wait(act, (e + 1) * 2)
                    s_ed.wait(act, (e + 1) * 2)
                    act.dma_start(out_view[:, bass.ds(e * Q, Q), :], res[b][:, :, :]).then_inc(s_o[b].sem, 16)

                skewed(act, gathered, up, down)
                for b in range(2):
                    s_o[b].wait(act, 16 * PAIRS // 2)

            @block.vector
            def _(dve):
                start(dve, s_cd, s_gs, s_hid, s_ed, s_z)
                for a in range(2):
                    dve.memset(hid[a][(1 - a) * H:(2 - a) * H, :], 0.0).then_inc(s_z.sem, 1)
                s_z.wait(dve, 2)

                def gathered(e, b):
                    for a in range(2):
                        s_tr.wait(dve, e * 2 + a + 1)
                        s_up.wait(dve, e - 1)
                        dve.tensor_copy(xT[b][:, 2:4, a, :], pT[:, a, 1, :].rearrange("p (c n) -> p c n", c=2)
                                        ).then_inc(s_cd.sem, 1)

                def up(e, b):
                    s_sg.wait(dve, e + 1)
                    dve.tensor_tensor(gs[:, :], sg[:, :], pU[:, 0, :], ALU.mult).then_inc(s_gs.sem, 1)
                    s_gs.wait(dve, e + 1)
                    s_dn.wait(dve, e * Q)
                    for a in range(2):
                        o = slice(a * H, (a + 1) * H)
                        t = dve.tensor_tensor(hid[a][o, :], gs[o, :], pU[o, 1, :], ALU.mult)
                    t.then_inc(s_hid.sem, 1)

                def down(e, b):
                    s_o[b].wait(dve, (e - b) * 8)
                    for q in (1, 3):
                        s_dn.wait(dve, e * Q + q + 1)
                        dve.tensor_copy(res[b][:, q, :], pD[:, 1, :]).then_inc(s_ed.sem, 1)

                skewed(dve, gathered, up, down)


def combine(nc, tag, k, out_d, keep, out=None):
    with ExitStack() as ctx:
        m = Memory(nc, ctx, tag)
        idx = [m.sb(f"idx{b}", [P, TOPK], U32) for b in range(2)]
        got = [m.sb(f"got{b}", [P, TOPK, C]) for b in range(2)]
        wst = m.sb("wst", [P, 2, TOPK])
        s_z = m.flag("z")
        s_idx = m.flag("idx")
        s_g = [m.pool_dmas(f"g{b}") for b in range(2)]
        s_ws = m.flag("ws")
        s_add = m.flag("add")
        s_out = m.flag("out")
        out_view = out.rearrange("b (i p) c -> p (b i) c", p=P) if out is not None else None

        with nc.Block() as block:
            @block.gpsimd
            def _(pool):
                start(pool, s_idx, s_z)
                for b in range(2):
                    pool.memset(got[b][:, :, :], 0.0).then_inc(s_z.sem, 1)
                s_z.wait(pool, 2)
                with pool.Fori(0, NT // 2) as i:
                    for b in range(2):
                        s_add.wait(pool, (i * 2 + b - 1) * TOPK)
                        pool.tensor_copy(idx[b][:, :], keep["slot"][:, bass.ds(i * 2 + b, 1), :]
                                         .rearrange("p a q -> p (a q)")).then_inc(s_idx.sem, 1)
                        s_idx.wait(pool, i * 2 + b + 1)
                        for q in range(TOPK):
                            pool.indirect_dma_start(
                                got[b][:, q, :], None, out_d,
                                bass.IndirectOffsetOnAxis(ap=idx[b][:, q:q + 1], axis=0),
                                bounds_check=ROWS - 1, oob_is_err=False).then_inc(s_g[b].sem, 16)

            @block.vector
            def _(dve):
                start(dve, s_add, s_ws)
                with dve.Fori(0, NT // 2) as i:
                    for b in range(2):
                        x = k["x"][:, bass.ds(i * 2 + b, 1), :].rearrange("p a c -> p (a c)")
                        s_add.wait(dve, (i * 2 + b - 1) * TOPK)
                        dve.tensor_copy(wst[:, b, :], keep["w"][:, bass.ds(i * 2 + b, 1), :]
                                        .rearrange("p a q -> p (a q)")).then_inc(s_ws.sem, 1)
                        s_ws.wait(dve, i * 2 + b + 1)
                        s_g[b].wait(dve, (i + 1) * (16 * TOPK))
                        for q in range(TOPK):
                            s_add.wait(dve, (i * 2 + b) * TOPK + q)
                            dve.scalar_tensor_tensor(x, got[b][:, q, :], wst[:, b, q:q + 1], x, ALU.mult,
                                                     ALU.add).then_inc(s_add.sem, 1)

            @block.sync
            def _(sp):
                if out is not None:
                    start(sp, s_out)
                    with sp.Fori(0, NT) as i:
                        s_add.wait(sp, (i + 1) * TOPK)
                        sp.dma_start(out_view[:, bass.ds(i, 1), :].rearrange("p a c -> p (a c)"), k["x"][:, bass.ds(i, 1), :].rearrange("p a c -> p (a c)")).then_inc(s_out.sem, 16)
                    s_out.wait(sp, 16 * NT)


DH, HQ = 32, 16
HG = 4
QT = 512
QTILES = QT // P
GROUPS = N // QT * (HQ // HG)
STEPS = S // P
KCH = S // 512
PER_CHUNK = HQ // HG


def project(nc, tag, k, w, q_d, kT, v_sb):
    wq, bq, wk, bk, wv, bv, wo, bo = w
    with ExitStack() as ctx:
        m = Memory(nc, ctx, tag)
        wq_sb = m.sb("wq", [P, CK, C])
        wkv = m.sb("wkv", [P, CK, 2 * DH])
        bq_sb, bo_sb = m.sb("bq", [P, C]), m.sb("bo", [P, C])
        bkv = m.sb("bkv", [P, 2 * DH])
        stats = m.sb("stats", [P, TURN, 6])
        mv = m.sb("mv", [P, TURN, 2])
        ve = m.sb("ve", [P, TURN])
        rstd = m.sb("rstd", [P, TURN])
        xn = m.sb("xn", [P, TURN, C])
        xT = m.sb("xT", [P, 2, CK, P])
        q_sb = m.sb("q", [P, 2, C])
        kb = m.sb("kb", [P, 2, DH])
        kst = m.sb("kst", [P, 2, P])
        pT = m.ps("pT", [P, 2, CK, P])
        pQ = m.ps("pQ", [P, 2, C])
        pK = m.ps("pK", [P, 2, 512])
        pS = m.ps("pS", [P, 2, 512])
        names = "w bias ve rs xn tr xT pr kst kt kc kb xb init qb vb".split()
        (s_w, s_bias, s_ve, s_rs, s_xn, s_tr, s_xT, s_pr, s_kst, s_kt, s_kc, s_kb, s_xb, s_init, s_qb,
         s_vb) = (m.flag(n) for n in names)
        s_dve = m.flag("dve")
        s_q = m.flags("q", 2)
        scale = float(DH) ** -0.5

        with nc.Block() as block:
            @block.sync
            def _(sp):
                start(sp, s_w, *s_q)
                sp.dma_start(wq_sb[:, :, :], wq.rearrange("(k p) n -> p k n", p=P)).then_inc(s_w.sem, 16)
                sp.dma_start(wkv[:, :, 0:DH], wk.rearrange("(k p) n -> p k n", p=P)).then_inc(s_w.sem, 16)
                sp.dma_start(wkv[:, :, DH:2 * DH], wv.rearrange("(k p) n -> p k n", p=P)).then_inc(s_w.sem, 16)
                for dst, src in ((bq_sb[:, :], bq), (bo_sb[:, :], bo), (bkv[:, 0:DH], bk), (bkv[:, DH:2 * DH], bv)):
                    sp.dma_start(dst, src.rearrange("(a n) -> a n", a=1).to_broadcast(list(dst.shape))
                                 ).then_inc(s_w.sem, 16)
                with sp.Fori(0, NTURN) as i:
                    for j in range(TURN):
                        s_qb.wait(sp, i * TURN + j + 1)
                        sp.dma_start(q_d[bass.ds(i * (TURN * P) + j * P, P), :], q_sb[:, j % 2, :]
                                     ).then_inc(s_q[j % 2].sem, 16)
                for b in range(2):
                    s_q[b].wait(sp, 16 * NT // 2)

            @block.gpsimd
            def _(pool):
                start(pool, s_rs)
                with pool.Fori(0, NTURN) as i:
                    s_ve.wait(pool, i + 1)
                    pool.tensor_tensor(rstd[:, :], ve[:, :], k["half"][:, :], ALU.pow).then_inc(s_rs.sem, 1)

            @block.tensor
            def _(pe):
                start(pe, s_tr, s_pr, s_kt)

                def transposes(i, j):
                    s_xn.wait(pe, i * TURN + j + 1)
                    s_xT.wait(pe, i * TURN + j - 1)
                    for c in range(CK):
                        t = pe.transpose(pT[:, j % 2, c, :], xn[:, j, c * P:(c + 1) * P], k["ident"][:, :])
                    t.then_inc(s_tr.sem, 1)

                def products(i, j):
                    s_xT.wait(pe, i * TURN + j + 1)
                    s_qb.wait(pe, i * TURN + j - 1)
                    s_vb.wait(pe, i * TURN + j - 1)
                    h = j % 2
                    for c in range(CK):
                        pe.matmul(pQ[:, h, :], xT[:, h, c, :], wq_sb[:, c, :], start=c == 0, stop=c == CK - 1)
                    for c in range(CK):
                        t = pe.matmul(pK[:, h, 0:2 * DH], xT[:, h, c, :], wkv[:, c, :], start=c == 0,
                                      stop=c == CK - 1)
                    t.then_inc(s_pr.sem, 1)

                def keys(i, j):
                    s_kst.wait(pe, i * TURN + j + 1)
                    s_kc.wait(pe, i * TURN + j - 1)
                    pe.transpose(pS[:, j % 2, 0:P], kst[:, j % 2, :], k["ident"][:, :]).then_inc(s_kt.sem, 1)

                s_w.wait(pe, 7 * 16)
                with pe.Fori(0, NTURN) as i:
                    for f, j in ((transposes, 0), (transposes, 1), (products, 0), (transposes, 2), (products, 1),
                                 (keys, 0), (transposes, 3), (products, 2), (keys, 1), (products, 3), (keys, 2),
                                 (keys, 3)):
                        f(i, j)

            @block.scalar
            def _(act):
                start(act, s_xT, s_kc)

                def copy_T(i, j):
                    s_tr.wait(act, i * TURN + j + 1)
                    s_pr.wait(act, i * TURN + j - 1)
                    act.activation(xT[:, j % 2, :, :], pT[:, j % 2, :, :], ACT.Copy).then_inc(s_xT.sem, 1)

                def keys(i, j):
                    s_kt.wait(act, i * TURN + j + 1)
                    act.activation(kT[:, bass.ds(i * (TURN * P) + j * P, P)], pS[:, j % 2, 0:P], ACT.Copy
                                   ).then_inc(s_kc.sem, 1)

                with act.Fori(0, NTURN) as i:
                    for f, j in ((copy_T, 0), (copy_T, 1), (copy_T, 2), (keys, 0), (copy_T, 3), (keys, 1), (keys, 2),
                                 (keys, 3)):
                        f(i, j)

            @block.vector
            def _(dve):
                start(dve, s_dve, s_bias, s_ve, s_xn, s_kst, s_kb, s_xb, s_init, s_qb, s_vb)
                step = Steps(dve, s_dve, per_turn=2 * TURN + TURN)

                def outputs(i, j):
                    h = j % 2
                    s_pr.wait(dve, i * TURN + j + 1)
                    s_q[h].wait(dve, (i * 2 + j // 2) * 16)
                    dve.scalar_tensor_tensor(q_sb[:, h, :], pQ[:, h, :], scale, bq_sb[:, :], ALU.mult,
                                             ALU.add).then_inc(s_qb.sem, 1)
                    s_kst.wait(dve, i * TURN + j - 1)
                    dve.tensor_tensor(kb[:, h, :], pK[:, h, 0:DH], bkv[:, 0:DH], ALU.add).then_inc(s_kb.sem, 1)
                    dve.tensor_tensor(v_sb[:, bass.ds(i * TURN + j, 1), :].rearrange("p a d -> p (a d)"),
                                      pK[:, h, DH:2 * DH], bkv[:, DH:2 * DH], ALU.add).then_inc(s_vb.sem, 1)
                    s_kb.wait(dve, i * TURN + j + 1)
                    s_kt.wait(dve, i * TURN + j - 1)
                    step(dve.tensor_copy(kst[:, h, 0:2 * DH].rearrange("p (r d) -> p r d", r=2).bitcast(F32R),
                                         kb[:, h, :].unsqueeze(1).to_broadcast([P, 2, DH])))
                    step.wait()
                    dve.tensor_tensor(kst[:, h, 2 * DH:3 * DH], kb[:, h, :], kst[:, h, 0:DH],
                                      ALU.subtract).then_inc(s_kst.sem, 1)

                dve.memset(kst[:, :, :], 0.0).then_inc(s_init.sem, 1)
                s_init.wait(dve, 1)
                dve.memset(kst[:, :, 3 * DH:3 * DH + 2], 1.0).then_inc(s_init.sem, 1)
                s_w.wait(dve, 7 * 16)
                dve.tensor_scalar(bq_sb[:, :], bq_sb[:, :], scale, None, ALU.mult).then_inc(s_bias.sem, 1)
                s_bias.wait(dve, 1)
                s_init.wait(dve, 2)
                with dve.Fori(0, NTURN) as i:
                    step.turn(i)
                    s_xb.wait(dve, i * TURN)
                    for j in range(TURN):
                        x = k["x"][:, bass.ds(i * TURN + j, 1), :].rearrange("p a c -> p (a c)")
                        step(dve.bn_stats(stats[:, j, :], x))
                    for j in range(TURN):
                        step.wait(j + 1, apart=True)
                        step(dve.bn_aggr(mv[:, j, :], stats[:, j, :]))
                    step.wait()
                    dve.tensor_scalar(ve[:, :], mv[:, :, 1], EPS, None, ALU.add).then_inc(s_ve.sem, 1)
                    s_rs.wait(dve, i + 1)
                    for j in range(TURN):
                        s_tr.wait(dve, i * TURN)
                        x = k["x"][:, bass.ds(i * TURN + j, 1), :].rearrange("p a c -> p (a c)")
                        dve.tensor_scalar(xn[:, j, :], x, mv[:, j, 0:1], rstd[:, j:j + 1],
                                          ALU.subtract, ALU.mult).then_inc(s_xn.sem, 1)
                    for j in range(TURN):
                        s_xn.wait(dve, i * TURN + j + 1)
                        x = k["x"][:, bass.ds(i * TURN + j, 1), :].rearrange("p a c -> p (a c)")
                        dve.tensor_tensor(x, x, bo_sb[:, :], ALU.add).then_inc(s_xb.sem, 1)
                    for j in range(TURN):
                        outputs(i, j)
                    step.end()


def attention(nc, tag, k, w, q_d):
    wo = w[6]
    with ExitStack() as ctx:
        m = Memory(nc, ctx, tag)
        kT = m.sb("kT", [P, N], F32R)
        v_sb = m.sb("v", [P, NT, DH])
        project(nc, tag + "p", k, w, q_d, kT, v_sb)

        wo_sb = m.sb("wo", [P, PER_CHUNK, C])
        qc = m.sb("qc", [P, QTILES, C])
        rows = m.sb("rows", [P, QTILES, HG, P])
        qT = m.sb("qT", [P, 2, HG * QT], F32R)
        shift = m.sb("shift", [P, QTILES, HG, DH])
        mx = m.sb("mx", [P, QTILES * HG, KCH])
        nmax = m.sb("nmax", [P, QTILES, HG])
        PR = 4
        prob = [m.sb(f"prob{b}", [P, 2, HG * QT]) for b in range(PR // 2)]
        pair = [m.sb(f"pair{b}", [P, HG * QT]) for b in range(2)]
        quad = m.sb("quad", [P, HG * QT])
        o_sb, d_sb, oT = (m.sb(n, [P, QT]) for n in ("o", "d", "oT"))
        pS = m.ps("pS", [P, HG, 512])
        pO = m.ps("pO", [P, QT])
        pD = m.ps("pD", [P, QT])
        pR = m.ps("pR", [P, 2, 512])

        s_wo = m.flag("wo")
        s_qc = m.flag("qc")
        s_init = m.flag("init")
        s_clear = m.flag("clear")
        s_pool = m.flag("pool")
        s_rows = m.flag("rows")
        s_put = m.flag("put")
        s_dve = m.flag("dve")
        s_act = m.flag("act")
        s_qT = m.flag("qT")
        s_shift = m.flag("shift")
        s_mx = m.flag("mx")
        s_sc = m.flag("sc")
        s_ex = m.flag("ex")
        s_pv = m.flag("pv")
        s_pair = m.flag("pair")
        s_quad = m.flag("quad")
        s_one = m.flag("one")
        s_oc = m.flag("oc")
        s_dc = m.flag("dc")
        s_rec = m.flag("rec")
        s_oT = m.flag("oT")

        N_MAX = QTILES * HG * KCH
        BEFORE_O = 28
        QUADS = STEPS // 4
        last = GROUPS - 1

        def kinds(prepare=True, output=True):
            o = ["o"] * QTILES if output else []
            return ["q"] * HG + ["m"] * BEFORE_O + o + ["m"] * (N_MAX - BEFORE_O) + ["s"] * 2 if prepare else o

        class Ring:

            def __init__(self, G, what):
                prep, full, acts, outs = HG + N_MAX + 2, HG + N_MAX + 2 + QTILES, HG + 2, QTILES
                zero, tail = isinstance(G, int) and G <= 0, isinstance(G, int) and G == GROUPS
                if zero:
                    self.put, self.dve, self.act = prep * (G + 1), N_MAX * (G + 1), acts * (G + 1)
                else:
                    self.put = G * full + (2 * prep - full) - tail * prep
                    self.dve = G * (N_MAX + outs) + (N_MAX - outs) - tail * N_MAX
                    self.act = G * acts + (acts - tail * acts)
                self.tail, self.what = tail, what

            def filled(self, eng, n):
                s_put.wait(eng, self.put + (n + 1))
                return pR[:, n % 2, :]

            def emptied(self, n, apart=False):
                if n < 2:
                    if self.tail:
                        s_dve.wait(pe_, self.dve + (n - 1), apart)
                    else:
                        s_act.wait(pe_, self.act + (n - 1), apart)
                elif self.what[n - 2] in "qs":
                    s_act.wait(pe_, self.act + sum(x in "qs" for x in self.what[:n - 1]), apart)
                else:
                    s_dve.wait(pe_, self.dve + sum(x in "mo" for x in self.what[:n - 1]), apart)
                return pR[:, n % 2, :]

        pe_ = nc.tensor

        with nc.Block() as block:
            @block.sync
            def _(sp):
                start(sp, s_wo, s_qc)
                sp.dma_start(wo_sb[:, :, :], wo.rearrange("(g p) n -> p g n", p=P)).then_inc(s_wo.sem, 16)
                view = q_d.rearrange("(c t p) n -> c p t n", t=QTILES, p=P)
                with sp.Fori(0, N // QT) as c:
                    s_rows.wait(sp, c * PER_CHUNK)
                    sp.dma_start(qc[:, :, :], view[bass.ds(c, 1), :, :, :].rearrange("c p t n -> (c p) t n")
                                 ).then_inc(s_qc.sem, 16)
                s_qc.wait(sp, 16 * (N // QT))
                s_wo.wait(sp, 16)

            @block.gpsimd
            def _(pool):
                start(pool, s_init, s_pool, s_rows, s_pair, s_oT)

                def query_rows(G):
                    s_qc.wait(pool, (G // PER_CHUNK + 1) * 16)
                    s_act.wait(pool, (G - 1) * (HG + 2) + HG)
                    q = qc[:, :, bass.ds(G % PER_CHUNK * P, P)].rearrange("p t (h d) -> p t h d", h=HG)
                    for o in (0, 2 * DH):
                        pool.tensor_copy(rows[:, :, :, o:o + DH].bitcast(F32R), q).then_inc(s_pool.sem, 1)
                    s_pool.wait(pool, (G + 1) * 2)
                    pool.tensor_tensor(rows[:, :, :, DH:2 * DH], q, rows[:, :, :, 0:DH],
                                       ALU.subtract).then_inc(s_rows.sem, 1)

                def add_pair(G, n):
                    s_ex.wait(pool, G * (2 * STEPS) + 4 * (n + 1))
                    s_quad.wait(pool, G * QUADS + n // 2)
                    pool.tensor_tensor(pair[n % 2][:, :], prob[n % 2][:, 0, :], prob[n % 2][:, 1, :],
                                       ALU.add).then_inc(s_pair.sem, 1)

                def normalise(G):
                    s_oc.wait(pool, G + 1)
                    s_rec.wait(pool, G + 1)
                    s_dve.wait(pool, Ring(G, None).dve)
                    pool.tensor_tensor(oT[:, :], o_sb[:, :], d_sb[:, :], ALU.mult).then_inc(s_oT.sem, 1)

                def body(G, before=True, ahead=True):
                    add_pair(G, 0)
                    if ahead:
                        query_rows(G + 2)
                    add_pair(G, 1)
                    if before:
                        normalise(G - 1)
                    for n in range(2, STEPS // 2):
                        add_pair(G, n)

                pool.memset(rows[:, :, :, :], 0.0).then_inc(s_init.sem, 1)
                s_init.wait(pool, 1)
                query_rows(0)
                query_rows(1)
                body(0, before=False)
                with pool.Fori(1, GROUPS - 2) as G:
                    body(G)
                body(last - 1, ahead=False)
                body(last, ahead=False)
                normalise(last)

            @block.scalar
            def _(act):
                start(act, s_ex, s_oc, s_dc, s_act, s_qT)

                def exps(G, t):
                    for h in range(2):
                        s_sc.wait(act, G * (2 * STEPS) + (2 * t + h + 1))
                        if h == 0:
                            s_pv.wait(act, G * STEPS + (t - PR + 1))
                            s_pair.wait(act, G * (STEPS // 2) + ((t - PR) // 2 + 1))
                        act.activation(prob[t // 2 % 2][:, t % 2, 2 * h * QT:2 * (h + 1) * QT], pS[:, 2 * h:2 * h + 2, :],
                                       ACT.Exp).then_inc(s_ex.sem, 1)

                def query_rows(r, G):
                    for n in range(HG):
                        bank = r.filled(act, n)
                        act.activation(qT[:, bass.ds(G % 2, 1), n * QT:(n + 1) * QT].rearrange("p a n -> p (a n)"),
                                       bank, ACT.Copy).then_inc(s_act.sem, 1)

                def shifts(r, G):
                    n0 = len(r.what) - 2
                    for n in range(2):
                        bank = r.filled(act, n0 + n)
                        for h in range(2):
                            o = (2 * n + h) * QT
                            ins = act.activation(
                                qT[3 * DH:4 * DH, bass.ds(G % 2, 1), o:o + QT].rearrange("p a n -> p (a n)"),
                                bank[h * DH:(h + 1) * DH, :], ACT.Copy)
                            if h:
                                ins.then_inc(s_act.sem, 1)
                    s_act.wait(act, r.act + (HG + 2))
                    act.sem_inc(s_qT.sem, 1)

                def copy_o(G):
                    s_pv.wait(act, (G + 1) * STEPS)
                    s_oT.wait(act, G)
                    act.activation(o_sb[:, :], pO[:, :], ACT.Copy).then_inc(s_oc.sem, 1)

                def copy_d(G):
                    s_one.wait(act, (G + 1) * QUADS)
                    s_oT.wait(act, G)
                    act.activation(d_sb[:, :], pD[:, :], ACT.Copy).then_inc(s_dc.sem, 1)

                def body(G, before=True, prepare=True):
                    r = Ring(G, kinds(prepare, before))
                    if before:
                        copy_o(G - 1)
                    for t in range(1, STEPS):
                        exps(G, t)
                        if t == 1 and prepare:
                            query_rows(r, G + 1)
                        if t == 5 and before:
                            copy_d(G - 1)
                    if prepare:
                        shifts(r, G + 1)
                        exps(G + 1, 0)

                r = Ring(-1, kinds(output=False))
                query_rows(r, 0)
                shifts(r, 0)
                exps(0, 0)
                body(0, before=False)
                with act.Fori(1, last) as G:
                    body(G)
                body(last, prepare=False)
                copy_o(last)
                copy_d(last)

            @block.tensor
            def _(pe):
                start(pe, s_put, s_sc, s_pv, s_one)

                def query_rows(r, n, G, h):
                    if h == 0:
                        s_rows.wait(pe, G + 1)
                    bank = r.emptied(n)
                    for t in range(QTILES):
                        ins = pe.transpose(bank[:, t * P:(t + 1) * P], rows[:, t, h, :], k["ident"][:, :])
                    ins.then_inc(s_put.sem, 1)

                def max_scores(r, n, at, b, batch):
                    if at == 0:
                        s_act.wait(pe, r.act + HG)
                    t, h, c = at // (HG * KCH), at // KCH % HG, at % KCH
                    pe.matmul(r.emptied(n), qT[:, b, h * QT + t * P:h * QT + (t + 1) * P],
                              kT[:, batch * S + c * 512:batch * S + (c + 1) * 512],
                              start=True, stop=True).then_inc(s_put.sem, 1)

                def shifts(r, n, G, at):
                    if at == 0:
                        s_shift.wait(pe, G + 1)
                    bank = r.emptied(n, apart=True)
                    for t in range(QTILES):
                        ins = pe.transpose(bank[0:2 * DH, t * P:(t + 1) * P],
                                           shift[:, t, 2 * at:2 * at + 2, :].rearrange("p h d -> p (h d)"),
                                           k["ident"][:, :])
                    ins.then_inc(s_put.sem, 1)

                def output(r, n, G, g, t):
                    if t == 0:
                        s_oT.wait(pe, G + 1)
                    w_g = wo_sb[:, bass.ds(g, 1), :].rearrange("p g n -> p (g n)")
                    pe.matmul(r.emptied(n), oT[:, t * P:(t + 1) * P], w_g, start=True, stop=True
                              ).then_inc(s_put.sem, 1)

                def scores(G, t, half, b, batch):
                    if t == 0 and half == 0:
                        s_qT.wait(pe, G + 1)
                    s_ex.wait(pe, G * (2 * STEPS) + (2 * t + half - 1))
                    key = batch * S + t * P
                    for h in (2 * half, 2 * half + 1):
                        ins = pe.matmul(pS[:, h, :], kT[:, key:key + P], qT[:, b, h * QT:(h + 1) * QT],
                                        start=True, stop=True)
                    ins.then_inc(s_sc.sem, 1)

                def values(G, t, batch):
                    s_ex.wait(pe, G * (2 * STEPS) + 2 * (t + 1))
                    if t == 0:
                        s_oc.wait(pe, G)
                    for h in range(HG):
                        ins = pe.matmul(pO[h * DH:(h + 1) * DH, :], v_sb[:, batch * STEPS + t, :],
                                        prob[t // 2 % 2][:, t % 2, h * QT:(h + 1) * QT],
                                        start=t == 0, stop=t == STEPS - 1)
                    ins.then_inc(s_pv.sem, 1)

                def denominators(G, n):
                    s_quad.wait(pe, G * QUADS + (n + 1))
                    if n == 0:
                        s_dc.wait(pe, G)
                    for h in range(HG):
                        ins = pe.matmul(pD[h * DH:(h + 1) * DH, :], k["ones32"][:, :], quad[:, h * QT:(h + 1) * QT],
                                        start=n == 0, stop=n == QUADS - 1)
                    ins.then_inc(s_one.sem, 1)

                def body(G, b, batch, g_before=None, after=None):
                    what = kinds(after is not None, g_before is not None)
                    r = Ring(G, what)
                    done = {"q": 0, "m": 0, "o": 0, "s": 0, "all": 0}

                    def item(shift_items=False):
                        n = done["all"]
                        if n == len(what) or (what[n] == "s" and not shift_items) or (after is None and t < 6):
                            return
                        kind = what[n]
                        at = done[kind]
                        if kind == "q":
                            query_rows(r, n, G + 1, at)
                        elif kind == "m":
                            max_scores(r, n, at, 1 - b, after)
                        elif kind == "o":
                            output(r, n, G - 1, g_before, at)
                        else:
                            shifts(r, n, G + 1, at)
                        done[kind] += 1
                        done["all"] += 1

                    for t in range(STEPS):
                        if t < STEPS - 1:
                            for half in range(2):
                                scores(G, t + 1, half, b, batch)
                                item()
                        elif after is not None:
                            values(G, t, batch)
                            item(True)
                            item(True)
                            for half in range(2):
                                scores(G + 1, 0, half, 1 - b, after)
                        if t < STEPS - 1 or after is None:
                            values(G, t, batch)
                            for _ in range(3):
                                item()
                        if t == 3 and g_before is not None:
                            denominators(G - 1, QUADS - 1)
                        if t in (7, 11, 15):
                            denominators(G, t // 4 - 1)
                    assert done["all"] == len(what)

                r = Ring(-1, kinds(output=False))
                for h in range(HG):
                    query_rows(r, h, 0, h)
                for n in range(N_MAX):
                    max_scores(r, HG + n, n, 0, 0)
                for n in range(2):
                    shifts(r, HG + N_MAX + n, 0, n)
                for h in range(2):
                    scores(0, 0, h, 0, 0)
                s_wo.wait(pe, 16)
                half = GROUPS // B
                for batch in range(B):
                    first = batch * half
                    body(first, 0, batch, None if batch == 0 else PER_CHUNK - 1, batch)
                    with pe.Fori(batch * (half // 2), (batch + 1) * (half // 2) - 1) as i:
                        for b in (1, 0):
                            body(i * 2 + (2 - b), b, batch, (i % 2) * 2 + (1 - b), batch)
                    body(first + half - 1, 1, batch, PER_CHUNK - 2, batch + 1 if batch + 1 < B else None)
                denominators(last, QUADS - 1)
                r = Ring(GROUPS, kinds(prepare=False))
                for t in range(QTILES):
                    output(r, t, last, PER_CHUNK - 1, t)

            @block.vector
            def _(dve):
                start(dve, s_dve, s_shift, s_mx, s_clear, s_quad, s_rec)

                def max_scores(r, n, at):
                    bank = r.filled(dve, n)
                    dve.tensor_reduce(mx[:, at // KCH, at % KCH:at % KCH + 1], bank, X, ALU.max
                                      ).then_inc(s_dve.sem, 1)

                def make_shifts(r, G):
                    s_dve.wait(dve, r.dve + sum(x in "mo" for x in r.what))
                    s_shift.wait(dve, G)
                    dve.tensor_reduce(nmax[:, :, :].rearrange("p t h -> p (t h)"), mx[:, :, :], X, ALU.max,
                                      negate=True).then_inc(s_mx.sem, 1)
                    s_mx.wait(dve, G * 2 + 1)
                    dve.tensor_copy(shift[:, :, :, 0].bitcast(F32R), nmax[:, :, :]).then_inc(s_mx.sem, 1)
                    s_mx.wait(dve, G * 2 + 2)
                    dve.tensor_tensor(shift[:, :, :, 1], nmax[:, :, :], shift[:, :, :, 0], ALU.subtract
                                      ).then_inc(s_shift.sem, 1)

                def output(r, n, chunk, t):
                    bank = r.filled(dve, n)
                    x = k["x"][:, bass.ds(chunk * QTILES + t, 1), :].rearrange("p a c -> p (a c)")
                    s_dve.wait(dve, r.dve)
                    dve.tensor_tensor(x, x, bank, ALU.add).then_inc(s_dve.sem, 1)

                def reciprocals(G):
                    s_dc.wait(dve, G + 1)
                    dve.reciprocal(d_sb[:, :], d_sb[:, :]).then_inc(s_rec.sem, 1)

                def add_quad(G, n):
                    s_pair.wait(dve, G * (2 * QUADS) + 2 * (n + 1))
                    s_one.wait(dve, G * QUADS + n)
                    dve.tensor_tensor(quad[:, :], pair[0][:, :], pair[1][:, :], ALU.add).then_inc(s_quad.sem, 1)

                def body(G, before=True, prepare=True):
                    what = kinds(prepare, before)
                    r = Ring(G, what)
                    if prepare:
                        s_mx.wait(dve, (G + 1) * 2)
                    quads = {8: (G - 1, QUADS - 1), 28: (G, 0), 48: (G, 1), 67: (G, 2)}
                    m = o = 0
                    ahead = 0 if prepare else HG + BEFORE_O
                    for n in range(HG + N_MAX + QTILES):
                        if n in quads and (before or n != 8):
                            add_quad(*quads[n])
                        if n == 24 and before:
                            reciprocals(G - 1)
                        if 0 <= n - ahead < len(what):
                            if what[n - ahead] == "m":
                                max_scores(r, n, m)
                                m += 1
                            elif what[n - ahead] == "o":
                                output(r, n - ahead, (G - 1) // PER_CHUNK, o)
                                o += 1
                    if prepare:
                        make_shifts(r, G + 1)

                dve.memset(shift[:, :, :, :], 0.0).then_inc(s_clear.sem, 1)
                s_clear.wait(dve, 1)
                r = Ring(-1, kinds(output=False))
                for n in range(N_MAX):
                    max_scores(r, HG + n, n)
                make_shifts(r, 0)
                body(0, before=False)
                with dve.Fori(1, last) as G:
                    body(G)
                body(last, prepare=False)
                add_quad(last, QUADS - 1)
                reciprocals(last)
                r = Ring(GROUPS, kinds(prepare=False))
                for t in range(QTILES):
                    output(r, t, last // PER_CHUNK, t)


def store(nc, tag, k, out):
    m = Memory(nc, None, tag)
    s = m.flag("st")
    with nc.Block() as block:
        @block.sync
        def _(sp):
            start(sp, s)
            sp.dma_start(out.rearrange("b (i p) c -> p (b i) c", p=P), k["x"][:, :, :]).then_inc(s.sem, 16)
            s.wait(sp, 16)


def program(nc, x_in, wq, bq, wk, bk, wv, bv, wo, bo, w_gate, w_su, w_sd, w_up, w_down, out, stages="faf"):
    with ExitStack() as ctx:
        m = Memory(nc, ctx, "g")
        for eng in (nc.gpsimd, nc.tensor, nc.vector):
            Flag.passed[eng.engine] = m.flag(f"passed_{eng.engine.name}").sem
        xn_d = nc.dram_tensor("xn_rows", (N, C), F32).ap()
        out_d = nc.dram_tensor("expert_rows", (ROWS, C), F32).ap()
        q_d = nc.dram_tensor("q_rows", (N, C), F32).ap()
        tables = [nc.dram_tensor(f"slot_table{n}", (ROWS, 1), U32).ap() for n in range(stages.count("f"))]
        k = setup(nc, ctx, x_in, tables)
        keep = {"slot": m.sb("slot", [P, NT, TOPK], U32), "w": m.sb("w", [P, NT, TOPK])}
        for n, stage in enumerate(stages):
            last = n == len(stages) - 1
            if stage == "f":
                tab_d = tables.pop(0)
                route(nc, f"r{n}", k, (w_gate, w_su, w_sd), xn_d, tab_d, keep)
                experts(nc, f"e{n}", k, w_up, w_down, xn_d, tab_d, out_d)
                combine(nc, f"m{n}", k, out_d, keep, out if last else None)
            else:
                attention(nc, f"a{n}", k, (wq, bq, wk, bk, wv, bv, wo, bo), q_d)
                if last:
                    store(nc, f"s{n}", k, out)


_INS = ['L0_attn_x', 'L0_attn_Wq', 'L0_attn_bq', 'L0_attn_Wk', 'L0_attn_bk', 'L0_attn_Wv', 'L0_attn_bv', 'L0_attn_Wo', 'L0_attn_bo', 'L0_ffn_w_gate', 'L0_ffn_w_shared_up', 'L0_ffn_w_shared_down', 'L0_ffn_w_up', 'L0_ffn_w_down']
_OUTS = [((B, S, C), 'float32')]


def kernel(**inputs):
    import numpy as _np
    import concourse.bacc as _bacc
    from concourse import mybir as _mybir
    from concourse.bass_utils import run_bass_kernel_spmd as _run

    nc = _bacc.Bacc("TRN2", target_bir_lowering=False, num_devices=1)
    arrays, args = {}, []
    for name in _INS:
        a = _np.ascontiguousarray(inputs[name])
        arrays[f"in_{name}_dram"] = a
        args.append(nc.dram_tensor(f"in_{name}_dram", a.shape, _mybir.dt.from_np(a.dtype), kind="ExternalInput").ap())
    for i, (shape, dtype) in enumerate(_OUTS):
        dt = _mybir.dt.from_np(_np.dtype(dtype))
        args.append(nc.dram_tensor(f"out_{i}_dram", shape, dt, kind="ExternalOutput").ap())
    program(nc, *args)
    r = _run(nc, [arrays], core_ids=[0])
    got = tuple(r.results[0][f"out_{i}_dram"] for i in range(len(_OUTS)))
    return got[0]
```

```python
from contextlib import ExitStack

import concourse.bass as bass
from concourse import mybir

F32 = mybir.dt.float32
F32R = mybir.dt.float32r
BF16 = mybir.dt.bfloat16
U32 = mybir.dt.uint32
ALU = mybir.AluOpType
ACT = mybir.ActivationFunctionType
X = mybir.AxisListType.X

P = 128
B, S, C = 2, 2048, 512
N = B * S
NT = N // P
CK = C // P
E, H, HS = 64, 64, 128
TOPK, CAP = 6, 256
EPS = 1e-5
SKIP = 65536.0
ROWS = E * CAP
HALVES = CAP // P
TURN = 4
NTURN = NT // TURN


class Flag:

    AHEAD = 16
    passed = {}

    def __init__(self, sem, ahead=AHEAD):
        self.sem, self.ahead = sem, ahead

    def start(self, eng):
        eng.sem_inc(self.sem, self.ahead)

    def wait(self, eng, count, apart=False):
        eng.wait_ge(self.sem, count + self.ahead)
        if apart or eng.engine == mybir.EngineType.Pool:
            eng.sem_inc(self.passed[eng.engine], 1)


class Steps:

    def __init__(self, eng, flag, per_turn=0, before=0):
        self.eng, self.flag, self.per_turn, self.before = eng, flag, per_turn, before
        self.base, self.k = 0, 0

    def turn(self, i):
        self.base, self.k = i * self.per_turn + self.before, 0

    def __call__(self, ins):
        ins.then_inc(self.flag.sem, 1)
        self.k += 1
        return self.k

    def wait(self, k=None, apart=False):
        self.flag.wait(self.eng, self.base + (self.k if k is None else k), apart)

    def end(self):
        assert self.k == self.per_turn, (self.k, self.per_turn)


class Memory:

    def __init__(self, nc, ctx, tag):
        self.nc, self.ctx, self.tag = nc, ctx, tag

    def sb(self, name, shape, dt=F32):
        return self.ctx.enter_context(self.nc.sbuf_tensor(f"{self.tag}_{name}", shape, dt))

    def ps(self, name, shape, dt=F32):
        return self.ctx.enter_context(self.nc.psum_tensor(f"{self.tag}_{name}", shape, dt))

    def flag(self, name):
        return Flag(self.nc.alloc_semaphore(f"{self.tag}_{name}"))

    def flags(self, name, n):
        return [self.flag(f"{name}{i}") for i in range(n)]

    def pool_dmas(self, name):
        return Flag(self.nc.alloc_semaphore(f"{self.tag}_{name}"), ahead=0)


def start(eng, *signals):
    for s in signals:
        s.start(eng)


def setup(nc, ctx, x_in, tables):
    m = Memory(nc, ctx, "c")
    k = {
        "x": m.sb("x", [P, NT, C]),
        "ident": m.sb("ident", [P, P]),
        "tri": m.sb("tri", [P, P], BF16),
        "ones": m.sb("ones", [P, P], BF16),
        "ones32": m.sb("ones32", [P, 32]),
        "half": m.sb("half", [P, TURN]),
        "expert": m.sb("expert", [P, E]),
        "token": m.sb("token", [P, NT], U32),
        "zero": m.sb("zero", [P, P], U32),
    }
    s_load, s_zero, s_set, s_tab = (m.flag(n) for n in ("load", "zero", "set", "tab"))
    x_view = x_in.rearrange("b (i p) c -> p (b i) c", p=P)
    with nc.Block() as block:
        @block.sync
        def _(sp):
            start(sp, s_load, s_tab)
            for q in range(4):
                part = slice(q * NT // 4, (q + 1) * NT // 4)
                sp.dma_start(k["x"][:, part, :], x_view[:, part, :]).then_inc(s_load.sem, 16)
            s_zero.wait(sp, 1)
            for table in tables:
                sp.dma_start(table.rearrange("(p n) a -> p (n a)", p=P), k["zero"][:, :]).then_inc(s_tab.sem, 16)
            s_tab.wait(sp, 16 * len(tables))
            s_load.wait(sp, 4 * 16)

        @block.gpsimd
        def _(pool):
            start(pool, s_zero, s_set)
            pool.memset(k["zero"][:, :], 0).then_inc(s_zero.sem, 1)
            pool.memset(k["ident"][:, :], 0.0).then_inc(s_set.sem, 1)
            pool.memset(k["tri"][:, :], 1.0).then_inc(s_set.sem, 1)
            pool.memset(k["ones"][:, :], 1.0).then_inc(s_set.sem, 1)
            pool.memset(k["ones32"][:, :], 1.0).then_inc(s_set.sem, 1)
            pool.memset(k["half"][:, :], -0.5).then_inc(s_set.sem, 1)
            pool.iota(k["expert"][:, :], pattern=[[1, E]], base=0, channel_multiplier=0,
                      allow_small_or_imprecise_dtypes=True).then_inc(s_set.sem, 1)
            pool.iota(k["token"][:, :], pattern=[[P, NT]], base=0, channel_multiplier=1).then_inc(s_set.sem, 1)
            s_set.wait(pool, 7)
            pool.affine_select(out=k["ident"][:, :], in_=k["ident"][:, :], compare_op=ALU.not_equal, fill=1.0,
                               base=0, pattern=[[-1, P]], channel_multiplier=1).then_inc(s_set.sem, 1)
            pool.affine_select(out=k["tri"][:, :], in_=k["tri"][:, :], compare_op=ALU.is_gt, fill=0.0,
                               base=0, pattern=[[1, P]], channel_multiplier=-1).then_inc(s_set.sem, 1)
            s_set.wait(pool, 9)
    return k


def route(nc, tag, k, wts, xn_d, tab_d, keep):
    w_gate, w_su, w_sd = wts
    with ExitStack() as ctx:
        m = Memory(nc, ctx, tag)
        wg = m.sb("wg", [P, CK, E])
        wsu = m.sb("wsu", [P, CK, 2 * HS])
        wsd = m.sb("wsd", [P, C])
        stats = m.sb("stats", [P, TURN, 6])
        mv = m.sb("mv", [P, TURN, 2])
        ve = m.sb("ve", [P, TURN])
        rstd = m.sb("rstd", [P, TURN])
        xn = m.sb("xn", [P, TURN, C])
        xT = m.sb("xT", [P, 2, CK, P])
        sc = m.sb("sc", [P, TURN, E])
        sg = m.sb("sg", [P, 2, P])
        gs = m.sb("gs", [P, 2, P])
        hs = m.sb("hs", [P, 2, P])
        v8 = m.sb("v8", [P, TURN, 8])
        i8 = m.sb("i8", [P, TURN, 8], U32)
        i8f = m.sb("i8f", [P, TURN, 8])
        eq = m.sb("eq", [P, TURN, TOPK, E])
        eqp = m.sb("eqp", [P, TURN, TOPK, E])
        mask = m.sb("mask", [P, TURN, E], BF16)
        msum = m.sb("msum", [P, E], BF16)
        cum = m.sb("cum", [P, E], BF16)
        pos = m.sb("pos", [P, TURN, TOPK])
        far = m.sb("far", [P, TURN, TOPK])
        addr = m.sb("addr", [P, TURN, TOPK])
        over = m.sb("over", [P, TURN, TOPK])
        live = m.sb("live", [P, TURN, TOPK])
        wsum = m.sb("wsum", [P, TURN])
        wrec = m.sb("wrec", [P, TURN])
        slot = m.sb("slot", [P, TURN, TOPK], U32)
        tok = m.sb("tok", [P, TURN], U32)
        pT = m.ps("pT", [P, 2, CK, P])
        pU = m.ps("pU", [P, 2, 512])
        pD = m.ps("pD", [P, 2, C])
        pP = m.ps("pP", [P, 512])

        s_w = m.flag("w")
        s_dve = m.flag("dve")
        s_ve = m.flag("ve")
        s_rs = m.flag("rs")
        s_xn = m.flag("xn")
        s_st = [m.flag(f"st{j}") for j in range(TURN)]
        s_tr = m.flag("tr")
        s_xT = m.flag("xT")
        s_up = m.flag("up")
        s_sg = m.flag("sg")
        s_hs = m.flag("hs")
        s_dn = m.flag("dn")
        s_rd = m.flag("rd")
        s_mask = m.flag("mask")
        s_pos = m.flag("pos")
        s_slot = m.flag("slot")
        s_tok = m.flag("tok")
        s_sc = m.pool_dmas("sc")
        s_in = m.flag("in")

        with nc.Block() as block:
            @block.sync
            def _(sp):
                start(sp, s_w, *s_st)
                sp.dma_start(wg[:, :, :], w_gate.rearrange("(k p) e -> p k e", p=P)).then_inc(s_w.sem, 16)
                sp.dma_start(wsu[:, :, :], w_su.rearrange("(k p) e -> p k e", p=P)).then_inc(s_w.sem, 16)
                sp.dma_start(wsd[:, :], w_sd).then_inc(s_w.sem, 16)
                with sp.Fori(0, NTURN) as i:
                    for j in range(TURN):
                        s_xn.wait(sp, i * TURN + j + 1)
                        sp.dma_start(xn_d[bass.ds(i * (TURN * P) + j * P, P), :], xn[:, j, :]).then_inc(s_st[j].sem, 16)
                for j in range(TURN):
                    s_st[j].wait(sp, 16 * NTURN)

            @block.gpsimd
            def _(pool):
                start(pool, s_rs, s_tok, s_in)

                def rsqrt(i):
                    s_ve.wait(pool, i + 1)
                    pool.tensor_tensor(rstd[:, :], ve[:, :], k["half"][:, :], ALU.pow).then_inc(s_rs.sem, 1)

                def scatter(i):
                    pool.tensor_copy(tok[:, :], k["token"][:, bass.ds(i * TURN, TURN)]).then_inc(s_tok.sem, 1)
                    s_tok.wait(pool, i + 1)
                    s_slot.wait(pool, i + 1)
                    for j in range(TURN):
                        for q in range(TOPK):
                            pool.indirect_dma_start(
                                tab_d, bass.IndirectOffsetOnAxis(ap=slot[:, j, q:q + 1], axis=0),
                                tok[:, j:j + 1], None, bounds_check=ROWS - 1, oob_is_err=False).then_inc(s_sc.sem, 16)
                    s_sc.wait(pool, (i + 1) * (16 * TURN * TOPK))
                    pool.sem_inc(s_in.sem, 1)

                rsqrt(0)
                with pool.Fori(1, NTURN) as i:
                    rsqrt(i)
                    scatter(i - 1)
                scatter(NTURN - 1)

            @block.tensor
            def _(pe):
                start(pe, s_tr, s_up, s_dn, s_pos)

                def transposes(i, j):
                    s_xn.wait(pe, i * TURN + j + 1)
                    s_xT.wait(pe, i * TURN + j - 1)
                    for c in range(CK):
                        t = pe.transpose(pT[:, j % 2, c, :], xn[:, j, c * P:(c + 1) * P], k["ident"][:, :])
                    t.then_inc(s_tr.sem, 1)

                def products(i, j):
                    s_xT.wait(pe, i * TURN + j + 1)
                    s_hs.wait(pe, i * TURN + j - 1)
                    h = j % 2
                    for o, w, n in ((256, wg[:, :, :], E),):
                        for c in range(CK):
                            pe.matmul(pU[:, h, o:o + n], xT[:, h, c, :], w[:, c, :], start=c == 0, stop=c == CK - 1)
                    for o in (0, HS):
                        for c in range(CK):
                            t = pe.matmul(pU[:, h, o:o + P], wsu[:, c, o:o + HS], xT[:, h, c, :],
                                          start=c == 0, stop=c == CK - 1)
                    t.then_inc(s_up.sem, 1)

                def down(i, j):
                    s_hs.wait(pe, i * TURN + j + 1)
                    s_rd.wait(pe, i * TURN + j - 1)
                    pe.matmul(pD[:, j % 2, :], hs[:, j % 2, :], wsd[:, :], start=True, stop=True).then_inc(s_dn.sem, 1)

                def positions(i):
                    s_mask.wait(pe, i + 1)
                    for j in range(TURN):
                        o = pP[:, j * E:(j + 1) * E]
                        pe.matmul(o, k["tri"][:, :], mask[:, j, :], start=True, stop=False)
                        for q in range(j):
                            pe.matmul(o, k["ones"][:, :], mask[:, q, :], start=False, stop=False)
                        t = pe.matmul(o, k["ones"][:, :], cum[:, :], start=False, stop=True)
                    t.then_inc(s_pos.sem, 1)

                s_w.wait(pe, 3 * 16)
                with pe.Fori(0, NTURN) as i:
                    for f, j in ((transposes, 0), (transposes, 1), (products, 0), (transposes, 2), (products, 1),
                                 (down, 0), (transposes, 3), (products, 2), (down, 1), (products, 3), (down, 2),
                                 (down, 3)):
                        f(i, j)
                    positions(i)

            @block.scalar
            def _(act):
                start(act, s_xT, s_sg)

                def copy_T(i, j):
                    s_tr.wait(act, i * TURN + j + 1)
                    s_up.wait(act, i * TURN + j - 1)
                    act.activation(xT[:, j % 2, :, :], pT[:, j % 2, :, :], ACT.Copy).then_inc(s_xT.sem, 1)

                def sigmoids(i, j):
                    s_up.wait(act, i * TURN + j + 1)
                    s_hs.wait(act, i * TURN + j - 1)
                    act.activation(sc[:, j, :], pU[:, j % 2, 256:256 + E], ACT.Sigmoid)
                    act.activation(sg[:, j % 2, :], pU[:, j % 2, HS:2 * HS], ACT.Sigmoid).then_inc(s_sg.sem, 1)

                with act.Fori(0, NTURN) as i:
                    for f, j in ((copy_T, 0), (copy_T, 1), (sigmoids, 0), (copy_T, 2), (sigmoids, 1), (copy_T, 3),
                                 (sigmoids, 2), (sigmoids, 3)):
                        if j == 0 and f is sigmoids:
                            s_rd.wait(act, i * TURN)
                            s_slot.wait(act, i)
                        f(i, j)

            @block.vector
            def _(dve):
                start(dve, s_dve, s_ve, s_xn, s_hs, s_rd, s_mask, s_slot)
                step = Steps(dve, s_dve, per_turn=36, before=1)

                def hidden(i, j):
                    s_sg.wait(dve, i * TURN + j + 1)
                    s_dn.wait(dve, i * TURN + j - 1)
                    h = j % 2
                    step(dve.tensor_tensor(gs[:, h, :], sg[:, h, :], pU[:, h, HS:2 * HS], ALU.mult))
                    step.wait()
                    dve.tensor_tensor(hs[:, h, :], gs[:, h, :], pU[:, h, 0:HS], ALU.mult).then_inc(s_hs.sem, 1)

                def residual(i, j):
                    s_dn.wait(dve, i * TURN + j + 1)
                    x = k["x"][:, bass.ds(i * TURN + j, 1), :].rearrange("p a c -> p (a c)")
                    dve.scalar_tensor_tensor(x, pD[:, j % 2, :], 0.5, x, ALU.mult, ALU.add).then_inc(s_rd.sem, 1)

                step(dve.memset(cum[:, :], 0.0))
                with dve.Fori(0, NTURN) as i:
                    step.turn(i)
                    for j in range(TURN):
                        x = k["x"][:, bass.ds(i * TURN + j, 1), :].rearrange("p a c -> p (a c)")
                        step(dve.bn_stats(stats[:, j, :], x))
                    for j in range(TURN):
                        step.wait(j + 1, apart=True)
                        step(dve.bn_aggr(mv[:, j, :], stats[:, j, :]))
                    step.wait()
                    dve.tensor_scalar(ve[:, :], mv[:, :, 1], EPS, None, ALU.add).then_inc(s_ve.sem, 1)
                    s_rs.wait(dve, i + 1)
                    for j in range(TURN):
                        s_st[j].wait(dve, i * 16)
                        s_tr.wait(dve, i * TURN)
                        x = k["x"][:, bass.ds(i * TURN + j, 1), :].rearrange("p a c -> p (a c)")
                        dve.tensor_scalar(xn[:, j, :], x, mv[:, j, 0:1], rstd[:, j:j + 1],
                                          ALU.subtract, ALU.mult).then_inc(s_xn.sem, 1)
                    s_xn.wait(dve, (i + 1) * TURN)
                    for f, j in ((hidden, 0), (hidden, 1), (residual, 0), (hidden, 2), (residual, 1), (hidden, 3),
                                 (residual, 2), (residual, 3)):
                        f(i, j)
                    for j in range(TURN):
                        step(dve.max(v8[:, j, :], sc[:, j, :]))
                        step.wait(apart=True)
                        step(dve.max_index(i8[:, j, :], v8[:, j, :], sc[:, j, :]))
                    step.wait()
                    step(dve.tensor_copy(i8f[:, :, :], i8[:, :, :]))
                    step.wait()
                    step(dve.tensor_tensor(
                        eq[:, :, :, :],
                        k["expert"][:, :].unsqueeze(1).unsqueeze(1).to_broadcast([P, TURN, TOPK, E]),
                        i8f[:, :, 0:TOPK].unsqueeze(3).to_broadcast([P, TURN, TOPK, E]), ALU.is_equal))
                    step.wait()
                    s_pos.wait(dve, i)
                    dve.tensor_reduce(mask[:, :, :], eq[:, :, :, :].rearrange("p j q e -> p j e q"), X,
                                      ALU.max).then_inc(s_mask.sem, 1)
                    s_mask.wait(dve, i + 1)
                    step(dve.tensor_reduce(wsum[:, :], v8[:, :, 0:TOPK], X, ALU.add))
                    step.wait()
                    step(dve.reciprocal(wrec[:, :], wsum[:, :]))
                    s_pos.wait(dve, i + 1)
                    step(dve.tensor_tensor(
                        eqp[:, :, :, :], eq[:, :, :, :],
                        pP[:, 0:TURN * E].rearrange("p (j e) -> p j e", e=E).unsqueeze(2)
                        .to_broadcast([P, TURN, TOPK, E]), ALU.mult))
                    with nc.allow_low_precision(reason="counts up to 32 are exact in bfloat16"):
                        step(dve.tensor_reduce(msum[:, :], mask[:, :, :].rearrange("p j e -> p e j"), X, ALU.add))
                    step.wait()
                    step(dve.tensor_reduce(pos[:, :, :], eqp[:, :, :, :], X, ALU.add))
                    step(dve.tensor_tensor(cum[:, :], cum[:, :], msum[:, :], ALU.add))
                    step.wait()
                    step(dve.tensor_scalar(far[:, :, :], pos[:, :, :], float(P), float(1 - P * P), ALU.is_ge, ALU.mult))
                    step(dve.tensor_scalar(over[:, :, :], pos[:, :, :], float(CAP), SKIP, ALU.is_ge, ALU.mult))
                    step(dve.tensor_scalar(live[:, :, :], pos[:, :, :], float(CAP), 0.5, ALU.is_lt, ALU.mult))
                    step.wait()
                    step(dve.scalar_tensor_tensor(addr[:, :, :], i8f[:, :, 0:TOPK], float(HALVES), far[:, :, :],
                                                  ALU.mult, ALU.add))
                    step(dve.tensor_tensor(live[:, :, :], live[:, :, :], v8[:, :, 0:TOPK], ALU.mult))
                    step.wait()
                    step(dve.scalar_tensor_tensor(addr[:, :, :], pos[:, :, :], float(P), addr[:, :, :],
                                                  ALU.mult, ALU.add))
                    step(dve.tensor_tensor(keep["w"][:, bass.ds(i * TURN, TURN), :], live[:, :, :],
                                           wrec[:, :].unsqueeze(2).to_broadcast([P, TURN, TOPK]), ALU.mult))
                    step.wait()
                    s_in.wait(dve, i)
                    dve.tensor_tensor(slot[:, :, :], addr[:, :, :], over[:, :, :], ALU.add).then_inc(s_slot.sem, 1)
                    step(dve.tensor_tensor(keep["slot"][:, bass.ds(i * TURN, TURN), :], addr[:, :, :],
                                           over[:, :, :], ALU.add))
                    step.wait()
                    step.end()


def experts(nc, tag, k, w_up, w_down, xn_d, tab_d, out_d):
    PAIRS = E // 2
    Q = 2 * HALVES
    up_view = w_up.rearrange("(g a) (c p) h -> g p a c h", a=2, p=P)
    down_view = w_down.rearrange("(g a) h c -> g (a h) c", a=2)
    out_view = out_d.rearrange("(p n) c -> p n c", p=P)
    with ExitStack() as ctx:
        m = Memory(nc, ctx, tag)
        table = m.sb("table", [P, P], U32)
        idx = [m.sb(f"idx{b}", [P, Q], U32) for b in range(2)]
        rows = [m.sb(f"rows{b}", [P, Q, C]) for b in range(2)]
        wup = [m.sb(f"wup{b}", [P, 2, CK, 2 * H]) for b in range(2)]
        wdn = [m.sb(f"wdn{b}", [P, C]) for b in range(2)]
        xT = [m.sb(f"xT{b}", [P, CK, 2, CAP]) for b in range(2)]
        sg = m.sb("sg", [P, CAP])
        gs = m.sb("gs", [P, CAP])
        hid = [m.sb(f"hid{a}", [P, CAP]) for a in range(2)]
        res = [m.sb(f"res{b}", [P, Q, C]) for b in range(2)]
        pT = m.ps("pT", [P, 2, 2, 512])
        pU = m.ps("pU", [P, 2, CAP])
        pD = m.ps("pD", [P, 2, C])

        s_tab = m.flag("tab")
        s_idx = m.flag("idx")
        s_g = [m.pool_dmas(f"g{b}") for b in range(2)]
        s_w = m.flags("w", 2)
        s_o = m.flags("o", 2)
        s_tr = m.flag("tr")
        s_ca = m.flag("ca")
        s_cd = m.flag("cd")
        s_up = m.flag("up")
        s_sg = m.flag("sg")
        s_gs = m.flag("gs")
        s_hid = m.flag("hid")
        s_dn = m.flag("dn")
        s_ea = m.flag("ea")
        s_ed = m.flag("ed")
        s_z = m.flag("z")

        def skewed(eng, stage_in, stage_up, stage_down):
            stage_in(0, 0)
            stage_up(0, 0)
            with eng.Fori(0, PAIRS // 2 - 1) as i:
                for b in (1, 0):
                    stage_in(i * 2 + (2 - b), b)
                    stage_down(i * 2 + (1 - b), 1 - b)
                    stage_up(i * 2 + (2 - b), b)
            stage_in(PAIRS - 1, 1)
            stage_down(PAIRS - 2, 0)
            stage_up(PAIRS - 1, 1)
            stage_down(PAIRS - 1, 1)

        with nc.Block() as block:
            @block.sync
            def _(sp):
                start(sp, s_tab, *s_w)
                sp.dma_start(table[:, :], tab_d.rearrange("(p n) a -> p (n a)", p=P)).then_inc(s_tab.sem, 16)
                with sp.Fori(0, PAIRS // 2) as i:
                    for b in range(2):
                        s_up.wait(sp, i * 2 + b - 1)
                        s_w[b].wait(sp, i * 48)
                        for a in range(2):
                            sp.dma_start(wup[b][:, a, :, :], up_view[bass.ds(i * 2 + b, 1), :, a, :, :]
                                         .rearrange("g p c h -> (g p) c h")).then_inc(s_w[b].sem, 16)
                        s_dn.wait(sp, (i * 2 + b - 1) * Q)
                        sp.dma_start(wdn[b][:, :], down_view[bass.ds(i * 2 + b, 1), :, :]
                                     .rearrange("g p c -> (g p) c")).then_inc(s_w[b].sem, 16)
                for b in range(2):
                    s_w[b].wait(sp, 48 * PAIRS // 2)

            @block.gpsimd
            def _(pool):
                start(pool, s_idx)
                s_tab.wait(pool, 16)
                with pool.Fori(0, PAIRS // 2) as i:
                    for b in range(2):
                        s_tr.wait(pool, (i * 2 + b - 1) * 2)
                        pool.tensor_copy(idx[b][:, :], table[:, bass.ds((i * 2 + b) * Q, Q)]).then_inc(s_idx.sem, 1)
                        s_idx.wait(pool, i * 2 + b + 1)
                        for q in range(Q):
                            pool.indirect_dma_start(
                                rows[b][:, q, :], None, xn_d,
                                bass.IndirectOffsetOnAxis(ap=idx[b][:, q:q + 1], axis=0)).then_inc(s_g[b].sem, 16)
                for b in range(2):
                    s_g[b].wait(pool, 16 * Q * PAIRS // 2)

            @block.tensor
            def _(pe):
                start(pe, s_tr, s_up, s_dn)

                def gathered(e, b):
                    s_g[b].wait(pe, (e + (2 - b)) * (8 * Q))
                    for a in range(2):
                        s_ca.wait(pe, e * 2 + a - 1)
                        s_cd.wait(pe, e * 2 + a - 1)
                        for c in range(CK):
                            for h in range(HALVES):
                                o = (c % 2) * CAP + h * P
                                t = pe.transpose(pT[:, a, c // 2, o:o + P],
                                                 rows[b][:, a * HALVES + h, c * P:(c + 1) * P], k["ident"][:, :])
                        t.then_inc(s_tr.sem, 1)

                def up(e, b):
                    s_w[b].wait(pe, (e + (2 - b)) * 24)
                    s_ca.wait(pe, (e + 1) * 2)
                    s_cd.wait(pe, (e + 1) * 2)
                    s_hid.wait(pe, e)
                    for v in range(2):
                        for c in range(CK):
                            for a in range(2):
                                t = pe.matmul(pU[a * H:(a + 1) * H, v, :], wup[b][:, a, c, v * H:(v + 1) * H],
                                              xT[b][:, c, a, :], start=c == 0, stop=c == CK - 1)
                    t.then_inc(s_up.sem, 1)

                def down(e, b):
                    s_hid.wait(pe, e + 1)
                    for q in range(Q):
                        (s_ea, s_ed)[q % 2].wait(pe, e * 2 + q // 2)
                        pe.matmul(pD[:, q % 2, :], hid[q // HALVES][:, (q % HALVES) * P:(q % HALVES + 1) * P],
                                  wdn[b][:, :], start=True, stop=True).then_inc(s_dn.sem, 1)

                skewed(pe, gathered, up, down)

            @block.scalar
            def _(act):
                start(act, s_ca, s_sg, s_ea, *s_o)

                def gathered(e, b):
                    for a in range(2):
                        s_tr.wait(act, e * 2 + a + 1)
                        s_up.wait(act, e - 1)
                        act.activation(xT[b][:, 0:2, a, :], pT[:, a, 0, :].rearrange("p (c n) -> p c n", c=2),
                                       ACT.Copy).then_inc(s_ca.sem, 1)

                def up(e, b):
                    s_up.wait(act, e + 1)
                    s_gs.wait(act, e)
                    act.activation(sg[:, :], pU[:, 0, :], ACT.Sigmoid).then_inc(s_sg.sem, 1)

                def down(e, b):
                    s_o[b].wait(act, (e - b) * 8)
                    for q in (0, 2):
                        s_dn.wait(act, e * Q + q + 1)
                        act.activation(res[b][:, q, :], pD[:, 0, :], ACT.Copy).then_inc(s_ea.sem, 1)
                    s_ea.wait(act, (e + 1) * 2)
                    s_ed.wait(act, (e + 1) * 2)
                    act.dma_start(out_view[:, bass.ds(e * Q, Q), :], res[b][:, :, :]).then_inc(s_o[b].sem, 16)

                skewed(act, gathered, up, down)
                for b in range(2):
                    s_o[b].wait(act, 16 * PAIRS // 2)

            @block.vector
            def _(dve):
                start(dve, s_cd, s_gs, s_hid, s_ed, s_z)
                for a in range(2):
                    dve.memset(hid[a][(1 - a) * H:(2 - a) * H, :], 0.0).then_inc(s_z.sem, 1)
                s_z.wait(dve, 2)

                def gathered(e, b):
                    for a in range(2):
                        s_tr.wait(dve, e * 2 + a + 1)
                        s_up.wait(dve, e - 1)
                        dve.tensor_copy(xT[b][:, 2:4, a, :], pT[:, a, 1, :].rearrange("p (c n) -> p c n", c=2)
                                        ).then_inc(s_cd.sem, 1)

                def up(e, b):
                    s_sg.wait(dve, e + 1)
                    dve.tensor_tensor(gs[:, :], sg[:, :], pU[:, 0, :], ALU.mult).then_inc(s_gs.sem, 1)
                    s_gs.wait(dve, e + 1)
                    s_dn.wait(dve, e * Q)
                    for a in range(2):
                        o = slice(a * H, (a + 1) * H)
                        t = dve.tensor_tensor(hid[a][o, :], gs[o, :], pU[o, 1, :], ALU.mult)
                    t.then_inc(s_hid.sem, 1)

                def down(e, b):
                    s_o[b].wait(dve, (e - b) * 8)
                    for q in (1, 3):
                        s_dn.wait(dve, e * Q + q + 1)
                        dve.tensor_copy(res[b][:, q, :], pD[:, 1, :]).then_inc(s_ed.sem, 1)

                skewed(dve, gathered, up, down)


def combine(nc, tag, k, out_d, keep, out=None):
    with ExitStack() as ctx:
        m = Memory(nc, ctx, tag)
        idx = [m.sb(f"idx{b}", [P, TOPK], U32) for b in range(2)]
        got = [m.sb(f"got{b}", [P, TOPK, C]) for b in range(2)]
        wst = m.sb("wst", [P, 2, TOPK])
        s_z = m.flag("z")
        s_idx = m.flag("idx")
        s_g = [m.pool_dmas(f"g{b}") for b in range(2)]
        s_ws = m.flag("ws")
        s_add = m.flag("add")
        s_out = m.flag("out")
        out_view = out.rearrange("b (i p) c -> p (b i) c", p=P) if out is not None else None

        with nc.Block() as block:
            @block.gpsimd
            def _(pool):
                start(pool, s_idx, s_z)
                for b in range(2):
                    pool.memset(got[b][:, :, :], 0.0).then_inc(s_z.sem, 1)
                s_z.wait(pool, 2)
                with pool.Fori(0, NT // 2) as i:
                    for b in range(2):
                        s_add.wait(pool, (i * 2 + b - 1) * TOPK)
                        pool.tensor_copy(idx[b][:, :], keep["slot"][:, bass.ds(i * 2 + b, 1), :]
                                         .rearrange("p a q -> p (a q)")).then_inc(s_idx.sem, 1)
                        s_idx.wait(pool, i * 2 + b + 1)
                        for q in range(TOPK):
                            pool.indirect_dma_start(
                                got[b][:, q, :], None, out_d,
                                bass.IndirectOffsetOnAxis(ap=idx[b][:, q:q + 1], axis=0),
                                bounds_check=ROWS - 1, oob_is_err=False).then_inc(s_g[b].sem, 16)

            @block.vector
            def _(dve):
                start(dve, s_add, s_ws)
                with dve.Fori(0, NT // 2) as i:
                    for b in range(2):
                        x = k["x"][:, bass.ds(i * 2 + b, 1), :].rearrange("p a c -> p (a c)")
                        s_add.wait(dve, (i * 2 + b - 1) * TOPK)
                        dve.tensor_copy(wst[:, b, :], keep["w"][:, bass.ds(i * 2 + b, 1), :]
                                        .rearrange("p a q -> p (a q)")).then_inc(s_ws.sem, 1)
                        s_ws.wait(dve, i * 2 + b + 1)
                        s_g[b].wait(dve, (i + 1) * (16 * TOPK))
                        for q in range(TOPK):
                            s_add.wait(dve, (i * 2 + b) * TOPK + q)
                            dve.scalar_tensor_tensor(x, got[b][:, q, :], wst[:, b, q:q + 1], x, ALU.mult,
                                                     ALU.add).then_inc(s_add.sem, 1)

            @block.sync
            def _(sp):
                if out is not None:
                    start(sp, s_out)
                    with sp.Fori(0, NT) as i:
                        s_add.wait(sp, (i + 1) * TOPK)
                        sp.dma_start(out_view[:, bass.ds(i, 1), :].rearrange("p a c -> p (a c)"), k["x"][:, bass.ds(i, 1), :].rearrange("p a c -> p (a c)")).then_inc(s_out.sem, 16)
                    s_out.wait(sp, 16 * NT)


DH, HQ = 32, 16
HG = 4
QT = 512
QTILES = QT // P
GROUPS = N // QT * (HQ // HG)
STEPS = S // P
KCH = S // 512
PER_CHUNK = HQ // HG
DIFF_STEPS = 5
LOWEST = -3.4e38


def project(nc, tag, k, w, q_d, kT, v_sb):
    wq, bq, wk, bk, wv, bv, wo, bo = w
    with ExitStack() as ctx:
        m = Memory(nc, ctx, tag)
        wq_sb = m.sb("wq", [P, CK, C])
        wkv = m.sb("wkv", [P, CK, 2 * DH])
        bq_sb, bo_sb = m.sb("bq", [P, C]), m.sb("bo", [P, C])
        bkv = m.sb("bkv", [P, 2 * DH])
        stats = m.sb("stats", [P, TURN, 6])
        mv = m.sb("mv", [P, TURN, 2])
        ve = m.sb("ve", [P, TURN])
        rstd = m.sb("rstd", [P, TURN])
        xn = m.sb("xn", [P, TURN, C])
        xT = m.sb("xT", [P, 2, CK, P])
        q_sb = m.sb("q", [P, 2, C])
        kb = m.sb("kb", [P, 2, DH])
        kst = m.sb("kst", [P, 2, P])
        pT = m.ps("pT", [P, 2, CK, P])
        pQ = m.ps("pQ", [P, 2, C])
        pK = m.ps("pK", [P, 2, 512])
        pS = m.ps("pS", [P, 2, 512])
        names = "w bias ve rs xn tr xT pr kst kt kc kb xb init qb vb".split()
        (s_w, s_bias, s_ve, s_rs, s_xn, s_tr, s_xT, s_pr, s_kst, s_kt, s_kc, s_kb, s_xb, s_init, s_qb,
         s_vb) = (m.flag(n) for n in names)
        s_dve = m.flag("dve")
        s_q = m.flags("q", 2)
        scale = float(DH) ** -0.5

        with nc.Block() as block:
            @block.sync
            def _(sp):
                start(sp, s_w, *s_q)
                sp.dma_start(wq_sb[:, :, :], wq.rearrange("(k p) n -> p k n", p=P)).then_inc(s_w.sem, 16)
                sp.dma_start(wkv[:, :, 0:DH], wk.rearrange("(k p) n -> p k n", p=P)).then_inc(s_w.sem, 16)
                sp.dma_start(wkv[:, :, DH:2 * DH], wv.rearrange("(k p) n -> p k n", p=P)).then_inc(s_w.sem, 16)
                for dst, src in ((bq_sb[:, :], bq), (bo_sb[:, :], bo), (bkv[:, 0:DH], bk), (bkv[:, DH:2 * DH], bv)):
                    sp.dma_start(dst, src.rearrange("(a n) -> a n", a=1).to_broadcast(list(dst.shape))
                                 ).then_inc(s_w.sem, 16)
                with sp.Fori(0, NTURN) as i:
                    for j in range(TURN):
                        s_qb.wait(sp, i * TURN + j + 1)
                        sp.dma_start(q_d[bass.ds(i * (TURN * P) + j * P, P), :], q_sb[:, j % 2, :]
                                     ).then_inc(s_q[j % 2].sem, 16)
                for b in range(2):
                    s_q[b].wait(sp, 16 * NT // 2)

            @block.gpsimd
            def _(pool):
                start(pool, s_rs)
                with pool.Fori(0, NTURN) as i:
                    s_ve.wait(pool, i + 1)
                    pool.tensor_tensor(rstd[:, :], ve[:, :], k["half"][:, :], ALU.pow).then_inc(s_rs.sem, 1)

            @block.tensor
            def _(pe):
                start(pe, s_tr, s_pr, s_kt)

                def transposes(i, j):
                    s_xn.wait(pe, i * TURN + j + 1)
                    s_xT.wait(pe, i * TURN + j - 1)
                    for c in range(CK):
                        t = pe.transpose(pT[:, j % 2, c, :], xn[:, j, c * P:(c + 1) * P], k["ident"][:, :])
                    t.then_inc(s_tr.sem, 1)

                def products(i, j):
                    s_xT.wait(pe, i * TURN + j + 1)
                    s_qb.wait(pe, i * TURN + j - 1)
                    s_vb.wait(pe, i * TURN + j - 1)
                    h = j % 2
                    for c in range(CK):
                        pe.matmul(pQ[:, h, :], xT[:, h, c, :], wq_sb[:, c, :], start=c == 0, stop=c == CK - 1)
                    for c in range(CK):
                        t = pe.matmul(pK[:, h, 0:2 * DH], xT[:, h, c, :], wkv[:, c, :], start=c == 0,
                                      stop=c == CK - 1)
                    t.then_inc(s_pr.sem, 1)

                def keys(i, j):
                    s_kst.wait(pe, i * TURN + j + 1)
                    s_kc.wait(pe, i * TURN + j - 1)
                    pe.transpose(pS[:, j % 2, 0:P], kst[:, j % 2, :], k["ident"][:, :]).then_inc(s_kt.sem, 1)

                s_w.wait(pe, 7 * 16)
                with pe.Fori(0, NTURN) as i:
                    for f, j in ((transposes, 0), (transposes, 1), (products, 0), (transposes, 2), (products, 1),
                                 (keys, 0), (transposes, 3), (products, 2), (keys, 1), (products, 3), (keys, 2),
                                 (keys, 3)):
                        f(i, j)

            @block.scalar
            def _(act):
                start(act, s_xT, s_kc)

                def copy_T(i, j):
                    s_tr.wait(act, i * TURN + j + 1)
                    s_pr.wait(act, i * TURN + j - 1)
                    act.activation(xT[:, j % 2, :, :], pT[:, j % 2, :, :], ACT.Copy).then_inc(s_xT.sem, 1)

                def keys(i, j):
                    s_kt.wait(act, i * TURN + j + 1)
                    act.activation(kT[:, bass.ds(i * (TURN * P) + j * P, P)], pS[:, j % 2, 0:P], ACT.Copy
                                   ).then_inc(s_kc.sem, 1)

                with act.Fori(0, NTURN) as i:
                    for f, j in ((copy_T, 0), (copy_T, 1), (copy_T, 2), (keys, 0), (copy_T, 3), (keys, 1), (keys, 2),
                                 (keys, 3)):
                        f(i, j)

            @block.vector
            def _(dve):
                start(dve, s_dve, s_bias, s_ve, s_xn, s_kst, s_kb, s_xb, s_init, s_qb, s_vb)
                step = Steps(dve, s_dve, per_turn=2 * TURN + TURN)

                def outputs(i, j):
                    h = j % 2
                    s_pr.wait(dve, i * TURN + j + 1)
                    s_q[h].wait(dve, (i * 2 + j // 2) * 16)
                    dve.scalar_tensor_tensor(q_sb[:, h, :], pQ[:, h, :], scale, bq_sb[:, :], ALU.mult,
                                             ALU.add).then_inc(s_qb.sem, 1)
                    s_kst.wait(dve, i * TURN + j - 1)
                    dve.tensor_tensor(kb[:, h, :], pK[:, h, 0:DH], bkv[:, 0:DH], ALU.add).then_inc(s_kb.sem, 1)
                    dve.tensor_tensor(v_sb[:, bass.ds(i * TURN + j, 1), :].rearrange("p a d -> p (a d)"),
                                      pK[:, h, DH:2 * DH], bkv[:, DH:2 * DH], ALU.add).then_inc(s_vb.sem, 1)
                    s_kb.wait(dve, i * TURN + j + 1)
                    s_kt.wait(dve, i * TURN + j - 1)
                    step(dve.tensor_copy(kst[:, h, 0:2 * DH].rearrange("p (r d) -> p r d", r=2).bitcast(F32R),
                                         kb[:, h, :].unsqueeze(1).to_broadcast([P, 2, DH])))
                    step.wait()
                    dve.tensor_tensor(kst[:, h, 2 * DH:3 * DH], kb[:, h, :], kst[:, h, 0:DH],
                                      ALU.subtract).then_inc(s_kst.sem, 1)

                dve.memset(kst[:, :, :], 0.0).then_inc(s_init.sem, 1)
                s_init.wait(dve, 1)
                dve.memset(kst[:, :, 3 * DH:3 * DH + 2], 1.0).then_inc(s_init.sem, 1)
                s_w.wait(dve, 7 * 16)
                dve.tensor_scalar(bq_sb[:, :], bq_sb[:, :], scale, None, ALU.mult).then_inc(s_bias.sem, 1)
                s_bias.wait(dve, 1)
                s_init.wait(dve, 2)
                with dve.Fori(0, NTURN) as i:
                    step.turn(i)
                    s_xb.wait(dve, i * TURN)
                    for j in range(TURN):
                        x = k["x"][:, bass.ds(i * TURN + j, 1), :].rearrange("p a c -> p (a c)")
                        step(dve.bn_stats(stats[:, j, :], x))
                    for j in range(TURN):
                        step.wait(j + 1, apart=True)
                        step(dve.bn_aggr(mv[:, j, :], stats[:, j, :]))
                    step.wait()
                    dve.tensor_scalar(ve[:, :], mv[:, :, 1], EPS, None, ALU.add).then_inc(s_ve.sem, 1)
                    s_rs.wait(dve, i + 1)
                    for j in range(TURN):
                        s_tr.wait(dve, i * TURN)
                        x = k["x"][:, bass.ds(i * TURN + j, 1), :].rearrange("p a c -> p (a c)")
                        dve.tensor_scalar(xn[:, j, :], x, mv[:, j, 0:1], rstd[:, j:j + 1],
                                          ALU.subtract, ALU.mult).then_inc(s_xn.sem, 1)
                    for j in range(TURN):
                        s_xn.wait(dve, i * TURN + j + 1)
                        x = k["x"][:, bass.ds(i * TURN + j, 1), :].rearrange("p a c -> p (a c)")
                        dve.tensor_tensor(x, x, bo_sb[:, :], ALU.add).then_inc(s_xb.sem, 1)
                    for j in range(TURN):
                        outputs(i, j)
                    step.end()


def attention(nc, tag, k, w, q_d):
    wo = w[6]
    with ExitStack() as ctx:
        m = Memory(nc, ctx, tag)
        kT = m.sb("kT", [P, N], F32R)
        kdiff = m.sb("kdiff", [P, N // 1024, 512], F32R)
        v_sb = m.sb("v", [P, NT, DH])
        project(nc, tag + "p", k, w, q_d, kT, v_sb)

        RING = 3
        PR = 4
        PAIRS = 4
        QUADS = STEPS // 4
        RELUS = 2
        CHUNK_PAIRS = KCH // 2
        last = GROUPS - 1

        wo_sb = m.sb("wo", [P, PER_CHUNK, C])
        qc = [m.sb(f"qc{b}", [P, QTILES, P]) for b in range(2)]
        rows = m.sb("rows", [P, QTILES, HG, P])
        qT = m.sb("qT", [P, 2, HG * QT], F32R)
        relus = [m.sb(f"relu{b}", [P, 512]) for b in range(RELUS)]
        shift = m.sb("shift", [P, QTILES, HG, DH])
        mx = m.sb("mx", [P, QTILES * HG, CHUNK_PAIRS])
        nmax = m.sb("nmax", [P, QTILES, HG])
        prob = [m.sb(f"prob{b}", [P, 2, HG * QT]) for b in range(PR // 2)]
        pair = [m.sb(f"pair{b}", [P, HG * QT]) for b in range(PAIRS)]
        o_sb, d_sb = (m.sb(n, [P, QT]) for n in ("o", "d"))
        pS = m.ps("pS", [P, HG, 512])
        pO = m.ps("pO", [P, QT])
        pR = m.ps("pR", [P, RING, 512])

        s_wo = m.flag("wo")
        s_qc = m.flags("qc", 2)
        s_init = m.flag("init")
        s_diff = m.flag("diff")
        s_clear = m.flag("clear")
        s_pool = m.flag("pool")
        s_rows = m.flag("rows")
        s_put = m.flag("put")
        s_dve = m.flag("dve")
        s_act = m.flag("act")
        s_qT = m.flag("qT")
        s_shift = m.flag("shift")
        s_mx = m.flag("mx")
        s_sc = m.flag("sc")
        s_ex = m.flag("ex")
        s_pv = m.flag("pv")
        s_pair = m.flag("pair")
        s_quad = m.flag("quad")
        s_oc = m.flag("oc")
        s_rec = m.flag("rec")
        s_oT = m.flag("oT")

        def items(G):
            if G == -1:
                return [("q", 0)] * HG + [("a", 0), ("b", 0)] * (QTILES * HG * CHUNK_PAIRS) + [("s", 0)] * 2 + [("q", 0)] * HG
            if G == GROUPS:
                return [("d", 0)] + [("o", 0)] * QTILES
            before, after = G > 0, G < last
            if not after:
                return [("d", 3)] + [("o", 7)] * QTILES + [("d", 8), ("d", 12), ("d", 15)]
            what = ["a", "b"] * (QTILES * HG * CHUNK_PAIRS)
            for kind, at in ([("d", 12)] if before else []) + [("d", 32)] + [("o", 40)] * (QTILES * before) + [
                    ("d", 52), ("d", 72)]:
                what.insert(at, kind)
            steps = STEPS - 2
            placed = [(x, n * steps // len(what)) for n, x in enumerate(what)]
            return placed + [("s", steps)] * 2 + [("q", steps + 1)] * (HG * (G < last - 1))

        LISTS = {G: items(G) for G in range(-1, GROUPS + 1)}
        WHO = {"p": "abcdoqs", "d": "bdo", "a": "qas"}

        def number(what, who):
            return sum(x in WHO[who] for x, _ in what)

        class Ring:

            def __init__(self, G):
                static = isinstance(G, int)
                at = G if static else 1
                self.list, self.prev = LISTS[at], LISTS.get(at - 1 if static else at, [])
                self.what = [x for x, _ in self.list]
                base = {who: sum(number(LISTS[g], who) for g in range(-1, at)) for who in WHO}
                self.bank0 = base["p"] % RING
                full = {who: number(LISTS[1], who) for who in WHO}
                assert full["p"] % RING == 0
                self.base = base if static else {who: G * full[who] + (base[who] - full[who]) for who in WHO}

            def upto(self, who, n):
                if n >= 0:
                    return self.base[who] + number(self.list[:n + 1], who)
                rest = number(self.prev[len(self.prev) + n + 1:], who)
                return self.base[who] - rest if rest else self.base[who]

            def find(self, kind, at, prev=False):
                what = [x for x, _ in (self.prev if prev else self.list)]
                where = [n for n, x in enumerate(what) if x == kind]
                return where[at] - (len(what) if prev else 0)

            def bank(self, n):
                return pR[:, (self.bank0 + n) % RING, :]

            def filled(self, eng, n, apart=False):
                s_put.wait(eng, self.upto("p", n), apart)
                return self.bank(n)

            def emptied(self, pe, n, apart=False):
                at = n - RING
                if at >= 0 or self.prev:
                    by_dve = (self.list if at >= 0 else self.prev)[at][0] in WHO["d"]
                    if by_dve:
                        s_dve.wait(pe, self.upto("d", at), apart)
                    else:
                        s_act.wait(pe, self.upto("a", at), apart)
                return self.bank(n)

        def events(G):
            placed = LISTS[G if isinstance(G, int) else 1]
            before, after = not isinstance(G, int) or G > 0, not isinstance(G, int) or G < last
            for t in range(STEPS):
                mine = [("item", n) for n, (_, step) in enumerate(placed) if step == t]
                more = t < STEPS - 1 or after
                sc = [("scores", t + 1, 0), ("scores", t + 1, 1)] if more else [None, None]
                if t < STEPS - 2:
                    out = [sc[0]] + mine[0:2] + [sc[1]] + mine[2:3] + [("values", t)] + mine[3:]
                elif t == STEPS - 2:
                    out = sc + [("values", t)] + mine
                else:
                    out = mine[0:2] + [("values", t)] + [sc[0]] + mine[2:3] + [sc[1]] + mine[3:]
                yield from (e for e in out if e is not None)

        with nc.Block() as block:
            @block.sync
            def _(sp):
                start(sp, s_wo, *s_qc)
                sp.dma_start(wo_sb[:, :, :], wo.rearrange("(g p) n -> p g n", p=P)).then_inc(s_wo.sem, 16)
                view = q_d.rearrange("(c t p) (g n) -> c g p t n", t=QTILES, p=P, g=PER_CHUNK)
                with sp.Fori(0, GROUPS // 2) as i:
                    for b in range(2):
                        s_rows.wait(sp, i * 2 + (b - 1))
                        sp.dma_start(qc[b][:, :, :], view[bass.ds(i // (PER_CHUNK // 2), 1), bass.ds(i % (PER_CHUNK // 2) * 2 + b, 1), :, :, :]
                                     .rearrange("c g p t n -> (c g p) t n")).then_inc(s_qc[b].sem, 16)
                for b in range(2):
                    s_qc[b].wait(sp, 16 * (GROUPS // 2))
                s_wo.wait(sp, 16)

            @block.gpsimd
            def _(pool):
                start(pool, s_init, s_pool, s_rows, s_pair, s_oT)

                def query_rows(G, b, part):
                    q = qc[b][:, :, :].rearrange("p t (h d) -> p t h d", h=HG)
                    if part < 2:
                        if part == 0:
                            s_qc[b].wait(pool, (G - b) * 8 + 16)
                            if not (isinstance(G, int) and G == 0):
                                s_act.wait(pool, HG if isinstance(G, int) and G == 1 else
                                           Ring(G - 2).upto("a", -1))
                        o = part * 2 * DH
                        pool.tensor_copy(rows[:, :, :, o:o + DH].bitcast(F32R), q).then_inc(s_pool.sem, 1)
                    else:
                        s_pool.wait(pool, (G + 1) * 2)
                        pool.tensor_tensor(rows[:, :, :, DH:2 * DH], q, rows[:, :, :, 0:DH],
                                           ALU.subtract).then_inc(s_rows.sem, 1)

                def add_pair(r, G, n):
                    s_ex.wait(pool, G * (2 * STEPS) + 4 * (n + 1))
                    if n % 2 == 0 and (n >= PAIRS or r.prev is not LISTS[-1]):
                        quad = n // 2 - PAIRS // 2
                        before = isinstance(G, int) and G == 0
                        if quad >= 0:
                            at = r.find("d", quad + (not before))
                        else:
                            at = r.find("d", 0) if quad == -1 else r.find("d", -1, prev=True)
                        s_put.wait(pool, r.upto("p", at))
                    pool.tensor_tensor(pair[n % PAIRS][:, :], prob[n % 2][:, 0, :], prob[n % 2][:, 1, :],
                                       ALU.add).then_inc(s_pair.sem, 1)

                def normalise(G):
                    s_oc.wait(pool, G + 1)
                    s_rec.wait(pool, (G + 1) * 2)
                    pool.tensor_tensor(o_sb[:, :], o_sb[:, :], d_sb[:, :], ALU.mult).then_inc(s_oT.sem, 1)

                def body(G, b, before=True, ahead=True):
                    r = Ring(G)
                    for n in range(STEPS // 2):
                        add_pair(r, G, n)
                        if n == 1 and before:
                            normalise(G - 1)
                        if ahead and n in (0, 2, 3):
                            query_rows(G + 2, b, (0, 2, 3).index(n))

                pool.memset(rows[:, :, :, :], 0.0).then_inc(s_init.sem, 1)
                s_init.wait(pool, 1)
                for part in range(3):
                    query_rows(0, 0, part)
                for part in range(3):
                    query_rows(1, 1, part)
                body(0, 0, before=False)
                with pool.Fori(0, (GROUPS - 4) // 2) as i:
                    for b in (1, 0):
                        body(i * 2 + (2 - b), b)
                body(last - 2, 1)
                body(last - 1, 0, ahead=False)
                body(last, 1, ahead=False)
                normalise(last)

            @block.scalar
            def _(act):
                start(act, s_ex, s_oc, s_act, s_qT)

                def exps(G, t, h):
                    s_sc.wait(act, G * (2 * STEPS) + (2 * t + h + 1))
                    if h == 0:
                        s_pv.wait(act, G * STEPS + (t - PR + 1))
                        s_pair.wait(act, G * (STEPS // 2) + ((t - PR) // 2 + 1))
                    act.activation(prob[t // 2 % 2][:, t % 2, 2 * h * QT:2 * (h + 1) * QT], pS[:, 2 * h:2 * h + 2, :],
                                   ACT.Exp).then_inc(s_ex.sem, 1)

                def query_rows(r, n, G, h):
                    act.activation(qT[:, bass.ds(G % 2, 1), h * QT:(h + 1) * QT].rearrange("p a n -> p (a n)"),
                                   r.filled(act, n), ACT.Copy).then_inc(s_act.sem, 1)

                def relu(r, n, at):
                    bank = r.filled(act, n)
                    if at >= RELUS:
                        s_dve.wait(act, r.upto("d", r.find("b", at - RELUS)))
                    elif r.prev and "b" in [x for x, _ in r.prev]:
                        s_dve.wait(act, r.upto("d", r.find("b", at - RELUS, prev=True)))
                    act.activation(relus[at % RELUS][:, :], bank, ACT.Relu).then_inc(s_act.sem, 1)

                def shifts(r, n, G, at):
                    bank = r.filled(act, n)
                    for h in range(2):
                        o = (2 * at + h) * QT
                        ins = act.activation(
                            qT[3 * DH:4 * DH, bass.ds(G % 2, 1), o:o + QT].rearrange("p a n -> p (a n)"),
                            bank[h * DH:(h + 1) * DH, :], ACT.Copy)
                        if h:
                            ins.then_inc(s_act.sem, 1)
                    if at == 1:
                        s_act.wait(act, r.upto("a", n))
                        act.sem_inc(s_qT.sem, 1)

                def copy_o(G):
                    s_pv.wait(act, (G + 1) * STEPS)
                    if not (isinstance(G, int) and G == 0):
                        r = Ring(G + 1)
                        s_put.wait(act, r.upto("p", r.find("o", -1, prev=True)))
                    act.activation(o_sb[:, :], pO[:, :], ACT.Copy).then_inc(s_oc.sem, 1)

                def emptying(r, G, n, seen):
                    kind = r.what[n]
                    at = seen.get(kind, 0)
                    seen[kind] = at + 1
                    if kind == "q":
                        query_rows(r, n, G + 2, at)
                    elif kind == "a":
                        relu(r, n, at)
                    elif kind == "s":
                        shifts(r, n, G + 1, at)

                def body(G, before=True):
                    r, seen = Ring(G), {}
                    if before:
                        copy_o(G - 1)
                    for what, *at in events(G):
                        if what == "scores":
                            t, h = at
                            exps(G + t // STEPS, t % STEPS, h)
                        elif what == "item":
                            emptying(r, G, at[0], seen)

                r, seen = Ring(-1), {}
                for n, kind in enumerate(r.what):
                    if kind == "q" and n < HG:
                        query_rows(r, n, 0, n)
                    elif kind == "q":
                        if n == len(r.what) - HG:
                            for h in range(2):
                                exps(0, 0, h)
                        query_rows(r, n, 1, n - (len(r.what) - HG))
                    else:
                        emptying(r, -1, n, seen)
                body(0, before=False)
                with act.Fori(1, last - 1) as G:
                    body(G)
                body(last - 1)
                body(last)
                copy_o(last)

            @block.tensor
            def _(pe):
                start(pe, s_put, s_sc, s_pv)

                def query_rows(r, n, G, h):
                    if h == 0:
                        s_rows.wait(pe, G + 1)
                        if not (isinstance(G, int) and G < 2):
                            s_ex.wait(pe, (G - 1) * (2 * STEPS) - 2)
                    bank = r.emptied(pe, n)
                    for t in range(QTILES):
                        ins = pe.transpose(bank[:, t * P:(t + 1) * P], rows[:, t, h, :], k["ident"][:, :])
                    ins.then_inc(s_put.sem, 1)

                def max_scores(r, n, at, b, batch):
                    unit, c = at // CHUNK_PAIRS, at % CHUNK_PAIRS
                    t, h = unit // HG, unit % HG
                    key = batch * S + c * 1024 + 512
                    keys = (kdiff[:, batch * CHUNK_PAIRS + c, :] if r.what[n] == "a" else kT[:, key:key + 512])
                    pe.matmul(r.emptied(pe, n), qT[:, b, h * QT + t * P:h * QT + (t + 1) * P], keys,
                              start=True, stop=True).then_inc(s_put.sem, 1)

                def shifts(r, n, G, at):
                    if at == 0:
                        s_shift.wait(pe, G + 1)
                    bank = r.emptied(pe, n, apart=True)
                    for t in range(QTILES):
                        ins = pe.transpose(bank[0:2 * DH, t * P:(t + 1) * P],
                                           shift[:, t, 2 * at:2 * at + 2, :].rearrange("p h d -> p (h d)"),
                                           k["ident"][:, :])
                    ins.then_inc(s_put.sem, 1)

                def output(r, n, G, g, t):
                    if t == 0:
                        s_oT.wait(pe, G + 1)
                    w_g = wo_sb[:, bass.ds(g, 1), :].rearrange("p g n -> p (g n)")
                    pe.matmul(r.emptied(pe, n), o_sb[:, t * P:(t + 1) * P], w_g, start=True, stop=True
                              ).then_inc(s_put.sem, 1)

                def denominators(r, n, G, quad):
                    s_quad.wait(pe, (G * QUADS + (quad + 1)) * 2)
                    bank = r.emptied(pe, n)
                    for h in range(HG):
                        ins = pe.matmul(bank[h * DH:(h + 1) * DH, :], k["ones32"][:, :],
                                        pair[2 * quad % PAIRS][:, h * QT:(h + 1) * QT], start=True, stop=True)
                    ins.then_inc(s_put.sem, 1)

                def scores(G, t, half, b, batch):
                    if t == 0 and half == 0:
                        s_qT.wait(pe, G + 1)
                    s_ex.wait(pe, G * (2 * STEPS) + (2 * t + half - 1))
                    key = batch * S + t * P
                    for h in (2 * half, 2 * half + 1):
                        ins = pe.matmul(pS[:, h, :], kT[:, key:key + P], qT[:, b, h * QT:(h + 1) * QT],
                                        start=True, stop=True)
                    ins.then_inc(s_sc.sem, 1)

                def values(G, t, batch):
                    s_ex.wait(pe, G * (2 * STEPS) + 2 * (t + 1))
                    if t == 0:
                        s_oc.wait(pe, G)
                    for h in range(HG):
                        ins = pe.matmul(pO[h * DH:(h + 1) * DH, :], v_sb[:, batch * STEPS + t, :],
                                        prob[t // 2 % 2][:, t % 2, h * QT:(h + 1) * QT],
                                        start=t == 0, stop=t == STEPS - 1)
                    ins.then_inc(s_pv.sem, 1)

                def body(G, b, batch, g_before=None, after=None):
                    r, seen = Ring(G), {}
                    for what, *at in events(G):
                        if what == "scores":
                            t, half = at
                            if t < STEPS:
                                scores(G, t, half, b, batch)
                            else:
                                scores(G + 1, 0, half, 1 - b, after)
                        elif what == "values":
                            values(G, at[0], batch)
                        else:
                            n = at[0]
                            kind = r.what[n]
                            i = seen.get(kind, 0)
                            seen[kind] = i + 1
                            if kind == "q":
                                query_rows(r, n, G + 2, i)
                            elif kind in "ab":
                                max_scores(r, n, i, 1 - b, after)
                            elif kind == "o":
                                output(r, n, G - 1, g_before, i)
                            elif kind == "d" and g_before is not None:
                                denominators(r, n, G if i else G - 1, i - 1 if i else QUADS - 1)
                            elif kind == "d":
                                denominators(r, n, G, i)
                            else:
                                shifts(r, n, G + 1, i)

                r = Ring(-1)
                for h in range(HG):
                    query_rows(r, h, 0, h)
                s_diff.wait(pe, DIFF_STEPS)
                s_act.wait(pe, HG)
                seen = {"a": 0, "b": 0}
                for n in range(HG, len(r.what) - HG - 2):
                    max_scores(r, n, seen[r.what[n]], 0, 0)
                    seen[r.what[n]] += 1
                n = len(r.what) - HG
                for h in range(2):
                    shifts(r, n - 2 + h, 0, h)
                for h in range(2):
                    scores(0, 0, h, 0, 0)
                for h in range(HG):
                    query_rows(r, n + h, 1, h)
                s_wo.wait(pe, 16)
                half = GROUPS // B
                body(0, 0, 0, None, 0)
                with pe.Fori(0, half // 2 - 1) as i:
                    for b in (1, 0):
                        body(i * 2 + (2 - b), b, 0, (i % 2) * 2 + (1 - b), 0)
                body(half - 1, 1, 0, PER_CHUNK - 2, 1)
                body(half, 0, 1, PER_CHUNK - 1, 1)
                with pe.Fori(half // 2, half - 2) as i:
                    for b in (1, 0):
                        body(i * 2 + (2 - b), b, 1, (i % 2) * 2 + (1 - b), 1)
                body(last - 2, 1, 1, PER_CHUNK - 4, 1)
                body(last - 1, 0, 1, PER_CHUNK - 3, 1)
                body(last, 1, 1, PER_CHUNK - 2, None)
                r = Ring(GROUPS)
                denominators(r, 0, last, QUADS - 1)
                for t in range(QTILES):
                    output(r, 1 + t, last, PER_CHUNK - 1, t)

            @block.vector
            def _(dve):
                start(dve, s_dve, s_diff, s_shift, s_mx, s_clear, s_quad, s_rec)

                def max_scores(r, n, at):
                    s_act.wait(dve, r.upto("a", r.find("a", at)), apart=True)
                    bank = r.filled(dve, n, apart=True)
                    buf = relus[at % RELUS][:, :]
                    dve.tensor_tensor_reduce(buf, buf, bank, 1.0, LOWEST, ALU.add, ALU.max,
                                             mx[:, at // CHUNK_PAIRS, at % CHUNK_PAIRS:at % CHUNK_PAIRS + 1]
                                             ).then_inc(s_dve.sem, 1)

                def make_shifts(r, G):
                    s_dve.wait(dve, r.upto("d", r.find("b", -1)))
                    s_shift.wait(dve, G)
                    dve.tensor_reduce(nmax[:, :, :].rearrange("p t h -> p (t h)"), mx[:, :, :], X, ALU.max,
                                      negate=True).then_inc(s_mx.sem, 1)
                    s_mx.wait(dve, G * 2 + 1)
                    dve.tensor_copy(shift[:, :, :, 0].bitcast(F32R), nmax[:, :, :]).then_inc(s_mx.sem, 1)
                    s_mx.wait(dve, G * 2 + 2)
                    dve.tensor_tensor(shift[:, :, :, 1], nmax[:, :, :], shift[:, :, :, 0], ALU.subtract
                                      ).then_inc(s_shift.sem, 1)

                def output(r, n, chunk, t):
                    bank = r.filled(dve, n)
                    x = k["x"][:, bass.ds(chunk * QTILES + t, 1), :].rearrange("p a c -> p (a c)")
                    s_dve.wait(dve, r.base["d"])
                    dve.tensor_tensor(x, x, bank, ALU.add).then_inc(s_dve.sem, 1)

                def denominators(r, n, G, quad, earlier):
                    bank = r.filled(dve, n)
                    if quad == 0:
                        s_oT.wait(dve, G)
                        dve.tensor_copy(d_sb[:, :], bank).then_inc(s_dve.sem, 1)
                    else:
                        s_dve.wait(dve, r.upto("d", earlier))
                        dve.tensor_tensor(d_sb[:, :], d_sb[:, :], bank, ALU.add).then_inc(s_dve.sem, 1)

                HALF = HG * QT // 2

                def reciprocals(r, n, half):
                    s_dve.wait(dve, r.upto("d", n))
                    part = d_sb[:, half * (QT // 2):(half + 1) * (QT // 2)]
                    dve.reciprocal(part, part).then_inc(s_rec.sem, 1)

                def add_quad(G, n, half):
                    s_pair.wait(dve, G * (2 * QUADS) + 2 * (n + 1))
                    a, part = 2 * n % PAIRS, slice(half * HALF, (half + 1) * HALF)
                    dve.tensor_tensor(pair[a][:, part], pair[a][:, part], pair[a + 1][:, part], ALU.add
                                      ).then_inc(s_quad.sem, 1)

                def body(G, before=True, prepare=True):
                    r = Ring(G)
                    lead = 1 if prepare else 0
                    extra = {}
                    ds = [n for n, x in enumerate(r.what) if x == "d"]
                    if before:
                        for half in range(2):
                            extra.setdefault(ds[0] + 1 + lead * (1 + 2 * half), []).append((reciprocals, r, ds[0], half))
                    for i, at in enumerate(ds):
                        g, quad = (G - 1, QUADS - 1) if before and i == 0 else (G, i - before)
                        for half in range(2):
                            extra.setdefault(at - lead * 3 * (2 - half), []).append((add_quad, g, quad, half))
                    seen = {}
                    for n, kind in enumerate(r.what):
                        for f, *args in extra.get(n, []):
                            f(*args)
                        i = seen.get(kind, 0)
                        seen[kind] = i + 1
                        if kind == "b":
                            max_scores(r, n, i)
                        elif kind == "o":
                            output(r, n, (G - 1) // PER_CHUNK, i)
                        elif kind == "d":
                            g, quad = (G - 1, QUADS - 1) if before and i == 0 else (G, i - before)
                            earlier = ds[i - 1] if i else (r.find("d", -1, prev=True) if before else None)
                            denominators(r, n, g, quad, earlier)
                    if prepare:
                        make_shifts(r, G + 1)

                kpairs = kT[:, :].bitcast(F32).rearrange("p (g a n) -> p g a n", a=2, n=512)
                exact = pair[0][:, :].rearrange("p (g n) -> p g n", n=512)
                rest = pair[1][:, :].rearrange("p (g n) -> p g n", n=512)
                kd = kdiff[:, :, :]
                lo, hi = slice(2 * DH, 3 * DH), slice(0, 2 * DH)
                dve.memset(kdiff[3 * DH:4 * DH, :, :].bitcast(F32), 0.0).then_inc(s_diff.sem, 1)
                dve.tensor_tensor(exact[0:3 * DH], kpairs[0:3 * DH, :, 0, :], kpairs[0:3 * DH, :, 1, :], ALU.subtract
                                  ).then_inc(s_diff.sem, 1)
                s_diff.wait(dve, 2)
                dve.tensor_copy(kd[hi], exact[hi]).then_inc(s_diff.sem, 1)
                s_diff.wait(dve, 3)
                dve.tensor_tensor(rest[lo], exact[0:DH], kdiff[0:DH, :, :].bitcast(F32), ALU.subtract).then_inc(s_diff.sem, 1)
                s_diff.wait(dve, 4)
                dve.tensor_tensor(kd[lo], exact[lo], rest[lo], ALU.add).then_inc(s_diff.sem, 1)
                dve.memset(shift[:, :, :, :], 0.0).then_inc(s_clear.sem, 1)
                s_clear.wait(dve, 1)
                r = Ring(-1)
                for at in range(number(r.list, "d")):
                    max_scores(r, r.find("b", at), at)
                make_shifts(r, 0)
                body(0, before=False)
                with dve.Fori(1, last - 1) as G:
                    body(G)
                body(last - 1)
                body(last, prepare=False)
                for half in range(2):
                    add_quad(last, QUADS - 1, half)
                r = Ring(GROUPS)
                denominators(r, 0, last, QUADS - 1, r.find("d", -1, prev=True))
                for half in range(2):
                    reciprocals(r, 0, half)
                for t in range(QTILES):
                    output(r, 1 + t, last // PER_CHUNK, t)


def store(nc, tag, k, out):
    m = Memory(nc, None, tag)
    s = m.flag("st")
    with nc.Block() as block:
        @block.sync
        def _(sp):
            start(sp, s)
            sp.dma_start(out.rearrange("b (i p) c -> p (b i) c", p=P), k["x"][:, :, :]).then_inc(s.sem, 16)
            s.wait(sp, 16)


def program(nc, x_in, wq, bq, wk, bk, wv, bv, wo, bo, w_gate, w_su, w_sd, w_up, w_down, out, stages="faf"):
    with ExitStack() as ctx:
        m = Memory(nc, ctx, "g")
        for eng in (nc.gpsimd, nc.tensor, nc.vector):
            Flag.passed[eng.engine] = m.flag(f"passed_{eng.engine.name}").sem
        xn_d = nc.dram_tensor("xn_rows", (N, C), F32).ap()
        out_d = nc.dram_tensor("expert_rows", (ROWS, C), F32).ap()
        q_d = nc.dram_tensor("q_rows", (N, C), F32).ap()
        tables = [nc.dram_tensor(f"slot_table{n}", (ROWS, 1), U32).ap() for n in range(stages.count("f"))]
        k = setup(nc, ctx, x_in, tables)
        keep = {"slot": m.sb("slot", [P, NT, TOPK], U32), "w": m.sb("w", [P, NT, TOPK])}
        for n, stage in enumerate(stages):
            last = n == len(stages) - 1
            if stage == "f":
                tab_d = tables.pop(0)
                route(nc, f"r{n}", k, (w_gate, w_su, w_sd), xn_d, tab_d, keep)
                experts(nc, f"e{n}", k, w_up, w_down, xn_d, tab_d, out_d)
                combine(nc, f"m{n}", k, out_d, keep, out if last else None)
            else:
                attention(nc, f"a{n}", k, (wq, bq, wk, bk, wv, bv, wo, bo), q_d)
                if last:
                    store(nc, f"s{n}", k, out)


_INS = ['L0_attn_x', 'L0_attn_Wq', 'L0_attn_bq', 'L0_attn_Wk', 'L0_attn_bk', 'L0_attn_Wv', 'L0_attn_bv', 'L0_attn_Wo', 'L0_attn_bo', 'L0_ffn_w_gate', 'L0_ffn_w_shared_up', 'L0_ffn_w_shared_down', 'L0_ffn_w_up', 'L0_ffn_w_down']
_OUTS = [((B, S, C), 'float32')]


def kernel(**inputs):
    import numpy as _np
    import concourse.bacc as _bacc
    from concourse import mybir as _mybir
    from concourse.bass_utils import run_bass_kernel_spmd as _run

    nc = _bacc.Bacc("TRN2", target_bir_lowering=False, num_devices=1)
    arrays, args = {}, []
    for name in _INS:
        a = _np.ascontiguousarray(inputs[name])
        arrays[f"in_{name}_dram"] = a
        args.append(nc.dram_tensor(f"in_{name}_dram", a.shape, _mybir.dt.from_np(a.dtype), kind="ExternalInput").ap())
    for i, (shape, dtype) in enumerate(_OUTS):
        dt = _mybir.dt.from_np(_np.dtype(dtype))
        args.append(nc.dram_tensor(f"out_{i}_dram", shape, dt, kind="ExternalOutput").ap())
    program(nc, *args)
    r = _run(nc, [arrays], core_ids=[0])
    got = tuple(r.results[0][f"out_{i}_dram"] for i in range(len(_OUTS)))
    return got[0]
```

```python
from contextlib import ExitStack

import concourse.bass as bass
from concourse import mybir

F32 = mybir.dt.float32
F32R = mybir.dt.float32r
BF16 = mybir.dt.bfloat16
U32 = mybir.dt.uint32
ALU = mybir.AluOpType
ACT = mybir.ActivationFunctionType
X = mybir.AxisListType.X

P = 128
B, S, C = 2, 2048, 512
N = B * S
NT = N // P
CK = C // P
E, H, HS = 64, 64, 128
TOPK, CAP = 6, 256
EPS = 1e-5
SKIP = 65536.0
ROWS = E * CAP
HALVES = CAP // P
TURN = 4
NTURN = NT // TURN


class Flag:

    AHEAD = 32
    passed = {}

    def __init__(self, sem, ahead=AHEAD):
        self.sem, self.ahead = sem, ahead

    def start(self, eng):
        eng.sem_inc(self.sem, self.ahead)

    def wait(self, eng, count, apart=False):
        eng.wait_ge(self.sem, count + self.ahead)
        if apart or eng.engine == mybir.EngineType.Pool:
            eng.sem_inc(self.passed[eng.engine], 1)


class Steps:

    def __init__(self, eng, flag, per_turn=0, before=0):
        self.eng, self.flag, self.per_turn, self.before = eng, flag, per_turn, before
        self.base, self.k = 0, 0

    def turn(self, i):
        self.base, self.k = i * self.per_turn + self.before, 0

    def __call__(self, ins):
        ins.then_inc(self.flag.sem, 1)
        self.k += 1
        return self.k

    def wait(self, k=None, apart=False):
        self.flag.wait(self.eng, self.base + (self.k if k is None else k), apart)

    def end(self):
        assert self.k == self.per_turn, (self.k, self.per_turn)


class Memory:

    def __init__(self, nc, ctx, tag):
        self.nc, self.ctx, self.tag = nc, ctx, tag

    def sb(self, name, shape, dt=F32):
        return self.ctx.enter_context(self.nc.sbuf_tensor(f"{self.tag}_{name}", shape, dt))

    def ps(self, name, shape, dt=F32):
        return self.ctx.enter_context(self.nc.psum_tensor(f"{self.tag}_{name}", shape, dt))

    def flag(self, name):
        return Flag(self.nc.alloc_semaphore(f"{self.tag}_{name}"))

    def flags(self, name, n):
        return [self.flag(f"{name}{i}") for i in range(n)]

    def pool_dmas(self, name):
        return Flag(self.nc.alloc_semaphore(f"{self.tag}_{name}"), ahead=0)


def start(eng, *signals):
    for s in signals:
        s.start(eng)


def setup(nc, ctx, x_in, tables):
    m = Memory(nc, ctx, "c")
    k = {
        "x": m.sb("x", [P, NT, C]),
        "ident": m.sb("ident", [P, P]),
        "tri": m.sb("tri", [P, P], BF16),
        "ones": m.sb("ones", [P, P], BF16),
        "ones32": m.sb("ones32", [P, 32]),
        "half": m.sb("half", [P, TURN]),
        "expert": m.sb("expert", [P, E]),
        "token": m.sb("token", [P, NT], U32),
        "zero": m.sb("zero", [P, P], U32),
    }
    s_zero, s_set, s_tab = (m.flag(n) for n in ("zero", "set", "tab"))
    k["loads"] = m.flags("load", 2)
    first, rest = slice(0, NT // 4), slice(NT // 4, NT)
    x_view = x_in.rearrange("b (i p) c -> p (b i) c", p=P)
    with nc.Block() as block:
        @block.sync
        def _(sp):
            start(sp, s_tab, *k["loads"])
            s_zero.wait(sp, 1)
            for table in tables:
                sp.dma_start(table.rearrange("(p n) a -> p (n a)", p=P), k["zero"][:, :]).then_inc(s_tab.sem, 16)
            sp.dma_start(k["x"][:, first, :], x_view[:, first, :]).then_inc(k["loads"][0].sem, 16)
            k["later"] = [(k["x"][:, rest, :], x_view[:, rest, :], k["loads"][1])]
            s_tab.wait(sp, 16 * len(tables))

        @block.gpsimd
        def _(pool):
            start(pool, s_zero, s_set)
            pool.memset(k["zero"][:, :], 0).then_inc(s_zero.sem, 1)
            pool.memset(k["ident"][:, :], 0.0).then_inc(s_set.sem, 1)
            pool.memset(k["tri"][:, :], 1.0).then_inc(s_set.sem, 1)
            pool.memset(k["ones"][:, :], 1.0).then_inc(s_set.sem, 1)
            pool.memset(k["ones32"][:, :], 1.0).then_inc(s_set.sem, 1)
            pool.memset(k["half"][:, :], -0.5).then_inc(s_set.sem, 1)
            pool.iota(k["expert"][:, :], pattern=[[1, E]], base=0, channel_multiplier=0,
                      allow_small_or_imprecise_dtypes=True).then_inc(s_set.sem, 1)
            pool.iota(k["token"][:, :], pattern=[[P, NT]], base=0, channel_multiplier=1).then_inc(s_set.sem, 1)
            s_set.wait(pool, 7)
            pool.affine_select(out=k["ident"][:, :], in_=k["ident"][:, :], compare_op=ALU.not_equal, fill=1.0,
                               base=0, pattern=[[-1, P]], channel_multiplier=1).then_inc(s_set.sem, 1)
            pool.affine_select(out=k["tri"][:, :], in_=k["tri"][:, :], compare_op=ALU.is_gt, fill=0.0,
                               base=0, pattern=[[1, P]], channel_multiplier=-1).then_inc(s_set.sem, 1)
            s_set.wait(pool, 9)
    return k


def route(nc, tag, k, wts, xn_d, tab_d, keep):
    w_gate, w_su, w_sd = wts
    with ExitStack() as ctx:
        m = Memory(nc, ctx, tag)
        wg = m.sb("wg", [P, CK, E])
        wsu = m.sb("wsu", [P, CK, 2 * HS])
        wsd = m.sb("wsd", [P, C])
        stats = m.sb("stats", [P, TURN, 6])
        mv = [m.sb(f"mv{b}", [P, TURN, 2]) for b in range(2)]
        ve = m.sb("ve", [P, TURN])
        rstd = [m.sb(f"rstd{b}", [P, TURN]) for b in range(2)]
        xn = [m.sb(f"xn{b}", [P, TURN, C]) for b in range(2)]
        xT = m.sb("xT", [P, 2, CK, P])
        sc = [m.sb(f"sc{b}", [P, TURN, E]) for b in range(2)]
        sg = m.sb("sg", [P, 2, P])
        gs = m.sb("gs", [P, 2, P])
        hs = m.sb("hs", [P, 2, P])
        v8 = m.sb("v8", [P, TURN, 8])
        i8 = m.sb("i8", [P, TURN, 8], U32)
        i8f = m.sb("i8f", [P, TURN, 8])
        eq = m.sb("eq", [P, TURN, TOPK, E])
        eqp = m.sb("eqp", [P, TURN, TOPK, E])
        mask = m.sb("mask", [P, TURN, E], BF16)
        msum = m.sb("msum", [P, E], BF16)
        cum = m.sb("cum", [P, E], BF16)
        pos = m.sb("pos", [P, TURN, TOPK])
        far = m.sb("far", [P, TURN, TOPK])
        addr = m.sb("addr", [P, TURN, TOPK])
        over = m.sb("over", [P, TURN, TOPK])
        live = m.sb("live", [P, TURN, TOPK])
        wsum = m.sb("wsum", [P, TURN])
        wrec = m.sb("wrec", [P, TURN])
        slot = [m.sb(f"slot{b}", [P, TURN, TOPK], U32) for b in range(2)]
        tok = [m.sb(f"tok{b}", [P, TURN], U32) for b in range(2)]
        pT = m.ps("pT", [P, 2, CK, P])
        pU = m.ps("pU", [P, 2, 512])
        pD = m.ps("pD", [P, 2, C])
        pP = m.ps("pP", [P, 512])

        s_w = m.flag("w")
        s_ln = m.flag("ln")
        s_dve = m.flag("dve")
        s_gs = m.flag("gs")
        s_ve = m.flag("ve")
        s_rs = m.flag("rs")
        s_xn = m.flag("xn")
        s_st = m.flags("st", 2)
        s_tr = m.flag("tr")
        s_xT = m.flag("xT")
        s_up = m.flag("up")
        s_sg = m.flag("sg")
        s_hs = m.flag("hs")
        s_dn = m.flag("dn")
        s_rd = m.flag("rd")
        s_mask = m.flag("mask")
        s_pos = m.flag("pos")
        s_slot = m.flag("slot")
        s_tok = m.flag("tok")
        s_sc = [m.pool_dmas(f"sc{b}") for b in range(2)]
        s_in = m.flag("in")

        def turns(eng, turn):
            with eng.Fori(0, NTURN // 2 - 1) as i:
                for b in range(2):
                    turn(i * 2 + b, b)
            for b in range(2):
                turn(NTURN - 2 + b, b)

        def follows(i, n=1):
            return not isinstance(i, int) or i + n < NTURN

        with nc.Block() as block:
            @block.sync
            def _(sp):
                start(sp, s_w, *s_st)
                sp.dma_start(wg[:, :, :], w_gate.rearrange("(k p) e -> p k e", p=P)).then_inc(s_w.sem, 16)
                sp.dma_start(wsu[:, :, :], w_su.rearrange("(k p) e -> p k e", p=P)).then_inc(s_w.sem, 16)
                sp.dma_start(wsd[:, :], w_sd).then_inc(s_w.sem, 16)
                for dst, src, flag in k["later"]:
                    sp.dma_start(dst, src).then_inc(flag.sem, 16)
                k["later"] = []

                def turn(i, b):
                    for j in range(TURN):
                        s_xn.wait(sp, i * TURN + (j + 1))
                        sp.dma_start(xn_d[bass.ds(i * (TURN * P) + j * P, P), :], xn[b][:, j, :]).then_inc(s_st[b].sem, 16)

                turns(sp, turn)
                for b in range(2):
                    s_st[b].wait(sp, 16 * TURN * NTURN // 2)

            @block.gpsimd
            def _(pool):
                start(pool, s_rs, s_tok, s_in)

                def rsqrt(i, b):
                    s_ve.wait(pool, i + 1)
                    pool.tensor_tensor(rstd[b][:, :], ve[:, :], k["half"][:, :], ALU.pow).then_inc(s_rs.sem, 1)

                def turn(i, b):
                    if follows(i, 2):
                        rsqrt(i + 2, b)
                    pool.tensor_copy(tok[b][:, :], k["token"][:, bass.ds(i * TURN, TURN)]).then_inc(s_tok.sem, 1)
                    s_tok.wait(pool, i + 1)
                    s_slot.wait(pool, i + 1)
                    for j in range(TURN):
                        for q in range(TOPK):
                            pool.indirect_dma_start(
                                tab_d, bass.IndirectOffsetOnAxis(ap=slot[b][:, j, q:q + 1], axis=0),
                                tok[b][:, j:j + 1], None, bounds_check=ROWS - 1, oob_is_err=False
                            ).then_inc(s_sc[b].sem, 16)
                        if j == 0:
                            s_sc[1 - b].wait(pool, (i + b) * (8 * TURN * TOPK))
                            pool.sem_inc(s_in.sem, 1)

                rsqrt(0, 0)
                rsqrt(1, 1)
                turns(pool, turn)
                s_sc[1].wait(pool, 8 * TURN * TOPK * NTURN)

            @block.tensor
            def _(pe):
                start(pe, s_tr, s_up, s_dn, s_pos)

                def transposes(i, j, b):
                    s_xn.wait(pe, i * TURN + (j + 1))
                    s_xT.wait(pe, i * TURN + (j - 1))
                    for c in range(CK):
                        t = pe.transpose(pT[:, j % 2, c, :], xn[b][:, j, c * P:(c + 1) * P], k["ident"][:, :])
                    t.then_inc(s_tr.sem, 1)

                def products(i, j, b):
                    s_xT.wait(pe, i * TURN + (j + 1))
                    s_hs.wait(pe, i * TURN + (j - 1))
                    h = j % 2
                    for c in range(CK):
                        pe.matmul(pU[:, h, 2 * HS:2 * HS + E], xT[:, h, c, :], wg[:, c, :], start=c == 0,
                                  stop=c == CK - 1)
                    for o in (0, HS):
                        for c in range(CK):
                            t = pe.matmul(pU[:, h, o:o + P], wsu[:, c, o:o + HS], xT[:, h, c, :],
                                          start=c == 0, stop=c == CK - 1)
                    t.then_inc(s_up.sem, 1)

                def down(i, j, b):
                    s_hs.wait(pe, i * TURN + (j + 1))
                    s_rd.wait(pe, i * TURN + (j - 1))
                    pe.matmul(pD[:, j % 2, :], hs[:, j % 2, :], wsd[:, :], start=True, stop=True).then_inc(s_dn.sem, 1)

                def positions(i):
                    s_mask.wait(pe, i + 1)
                    for j in range(TURN):
                        o = pP[:, j * E:(j + 1) * E]
                        pe.matmul(o, k["tri"][:, :], mask[:, j, :], start=True, stop=False)
                        for q in range(j):
                            pe.matmul(o, k["ones"][:, :], mask[:, q, :], start=False, stop=False)
                        t = pe.matmul(o, k["ones"][:, :], cum[:, :], start=False, stop=True)
                    t.then_inc(s_pos.sem, 1)

                def run(i, b, *steps):
                    for f, j in steps:
                        f(i, j, b)

                def turn(i, b):
                    run(i, b, (down, 0), (transposes, 3), (products, 2), (down, 1), (products, 3), (down, 2), (down, 3))
                    if follows(i):
                        run(i + 1, 1 - b, (transposes, 0), (transposes, 1), (products, 0))
                    positions(i)
                    if follows(i):
                        run(i + 1, 1 - b, (transposes, 2), (products, 1))

                s_w.wait(pe, 3 * 16)
                run(0, 0, (transposes, 0), (transposes, 1), (products, 0), (transposes, 2), (products, 1))
                turns(pe, turn)

            @block.scalar
            def _(act):
                start(act, s_xT, s_sg)

                def copy_T(i, j, b):
                    s_tr.wait(act, i * TURN + (j + 1))
                    s_up.wait(act, i * TURN + (j - 1))
                    act.activation(xT[:, j % 2, :, :], pT[:, j % 2, :, :], ACT.Copy).then_inc(s_xT.sem, 1)

                def sigmoids(i, j, b):
                    s_up.wait(act, i * TURN + (j + 1))
                    if j == 0:
                        s_slot.wait(act, i - 1)
                    s_hs.wait(act, i * TURN + (j - 1))
                    act.activation(sc[b][:, j, :], pU[:, j % 2, 2 * HS:2 * HS + E], ACT.Sigmoid)
                    act.activation(sg[:, j % 2, :], pU[:, j % 2, HS:2 * HS], ACT.Sigmoid).then_inc(s_sg.sem, 1)

                def turn(i, b):
                    for f, j in ((copy_T, 0), (copy_T, 1), (sigmoids, 0), (copy_T, 2), (sigmoids, 1), (copy_T, 3),
                                 (sigmoids, 2), (sigmoids, 3)):
                        f(i, j, b)

                turns(act, turn)

            @block.vector
            def _(dve):
                start(dve, s_ln, s_dve, s_gs, s_ve, s_xn, s_hs, s_rd, s_mask, s_slot)
                ln = Steps(dve, s_ln, per_turn=2 * TURN)
                step = Steps(dve, s_dve, per_turn=24, before=1)

                def x_tile(i, j):
                    return k["x"][:, bass.ds(i * TURN + j, 1), :].rearrange("p a c -> p (a c)")

                def variances(i, b):
                    ln.turn(i)
                    for j in range(TURN):
                        ln(dve.bn_stats(stats[:, j, :], x_tile(i, j)))
                    for j in range(TURN):
                        ln.wait(j + 1, apart=True)
                        ln(dve.bn_aggr(mv[b][:, j, :], stats[:, j, :]))
                    ln.wait()
                    s_rs.wait(dve, i)
                    dve.tensor_scalar(ve[:, :], mv[b][:, :, 1], EPS, None, ALU.add).then_inc(s_ve.sem, 1)

                def normalised(i, b):
                    s_rs.wait(dve, i + 1)
                    s_st[b].wait(dve, (i - b) * (8 * TURN))
                    s_tr.wait(dve, (i - 1) * TURN)
                    for j in range(TURN):
                        dve.tensor_scalar(xn[b][:, j, :], x_tile(i, j), mv[b][:, j, 0:1], rstd[b][:, j:j + 1],
                                          ALU.subtract, ALU.mult).then_inc(s_xn.sem, 1)

                def hidden(i, j):
                    s_sg.wait(dve, i * TURN + (j + 1))
                    s_dn.wait(dve, i * TURN + (j - 1))
                    h = j % 2
                    dve.tensor_tensor(gs[:, h, :], sg[:, h, :], pU[:, h, HS:2 * HS], ALU.mult).then_inc(s_gs.sem, 1)
                    s_gs.wait(dve, i * TURN + (j + 1))
                    dve.tensor_tensor(hs[:, h, :], gs[:, h, :], pU[:, h, 0:HS], ALU.mult).then_inc(s_hs.sem, 1)

                def residual(i, j):
                    s_dn.wait(dve, i * TURN + (j + 1))
                    s_xn.wait(dve, (i + 1) * TURN)
                    x = x_tile(i, j)
                    dve.scalar_tensor_tensor(x, pD[:, j % 2, :], 0.5, x, ALU.mult, ALU.add).then_inc(s_rd.sem, 1)

                def select(i, b):
                    for j in range(TURN):
                        step(dve.max(v8[:, j, :], sc[b][:, j, :]))
                        step.wait(apart=True)
                        step(dve.max_index(i8[:, j, :], v8[:, j, :], sc[b][:, j, :]))
                    step.wait()
                    step(dve.tensor_copy(i8f[:, :, :], i8[:, :, :]))
                    step.wait()
                    step(dve.tensor_tensor(
                        eq[:, :, :, :],
                        k["expert"][:, :].unsqueeze(1).unsqueeze(1).to_broadcast([P, TURN, TOPK, E]),
                        i8f[:, :, 0:TOPK].unsqueeze(3).to_broadcast([P, TURN, TOPK, E]), ALU.is_equal))
                    step.wait()
                    s_pos.wait(dve, i)
                    dve.tensor_reduce(mask[:, :, :], eq[:, :, :, :].rearrange("p j q e -> p j e q"), X,
                                      ALU.max).then_inc(s_mask.sem, 1)
                    step(dve.tensor_reduce(wsum[:, :], v8[:, :, 0:TOPK], X, ALU.add))
                    step.wait()
                    step(dve.reciprocal(wrec[:, :], wsum[:, :]))

                def place(i, b):
                    s_mask.wait(dve, i + 1)
                    with nc.allow_low_precision(reason="counts up to 32 are exact in bfloat16"):
                        step(dve.tensor_reduce(msum[:, :], mask[:, :, :].rearrange("p j e -> p e j"), X, ALU.add))
                    s_pos.wait(dve, i + 1)
                    step(dve.tensor_tensor(
                        eqp[:, :, :, :], eq[:, :, :, :],
                        pP[:, 0:TURN * E].rearrange("p (j e) -> p j e", e=E).unsqueeze(2)
                        .to_broadcast([P, TURN, TOPK, E]), ALU.mult))
                    step.wait()
                    step(dve.tensor_reduce(pos[:, :, :], eqp[:, :, :, :], X, ALU.add))
                    step(dve.tensor_tensor(cum[:, :], cum[:, :], msum[:, :], ALU.add))
                    step.wait()
                    step(dve.tensor_scalar(far[:, :, :], pos[:, :, :], float(P), float(1 - P * P), ALU.is_ge, ALU.mult))
                    step(dve.tensor_scalar(over[:, :, :], pos[:, :, :], float(CAP), SKIP, ALU.is_ge, ALU.mult))
                    step(dve.tensor_scalar(live[:, :, :], pos[:, :, :], float(CAP), 0.5, ALU.is_lt, ALU.mult))
                    step.wait()
                    step(dve.scalar_tensor_tensor(addr[:, :, :], i8f[:, :, 0:TOPK], float(HALVES), far[:, :, :],
                                                  ALU.mult, ALU.add))
                    step(dve.tensor_tensor(live[:, :, :], live[:, :, :], v8[:, :, 0:TOPK], ALU.mult))
                    step.wait()
                    step(dve.scalar_tensor_tensor(addr[:, :, :], pos[:, :, :], float(P), addr[:, :, :],
                                                  ALU.mult, ALU.add))
                    step(dve.tensor_tensor(keep["w"][:, bass.ds(i * TURN, TURN), :], live[:, :, :],
                                           wrec[:, :].unsqueeze(2).to_broadcast([P, TURN, TOPK]), ALU.mult))
                    step.wait()
                    s_in.wait(dve, i)
                    dve.tensor_tensor(slot[b][:, :, :], addr[:, :, :], over[:, :, :], ALU.add).then_inc(s_slot.sem, 1)
                    step(dve.tensor_tensor(keep["slot"][:, bass.ds(i * TURN, TURN), :], addr[:, :, :],
                                           over[:, :, :], ALU.add))
                    step.wait()
                    step.end()

                def turn(i, b):
                    step.turn(i)
                    for f, j in ((hidden, 1), (residual, 0), (hidden, 2), (residual, 1), (hidden, 3)):
                        f(i, j)
                    if follows(i):
                        normalised(i + 1, 1 - b)
                    for j in (2, 3):
                        residual(i, j)
                    select(i, b)
                    if follows(i, 2):
                        variances(i + 2, b)
                    if follows(i):
                        hidden(i + 1, 0)
                    place(i, b)

                step(dve.memset(cum[:, :], 0.0))
                k["loads"][0].wait(dve, 16)
                variances(0, 0)
                variances(1, 1)
                normalised(0, 0)
                k["loads"][1].wait(dve, 16)
                hidden(0, 0)
                turns(dve, turn)


def experts(nc, tag, k, w_up, w_down, xn_d, tab_d, out_d):
    PAIRS = E // 2
    Q = 2 * HALVES
    up_view = w_up.rearrange("(g a) (c p) h -> g p a c h", a=2, p=P)
    down_view = w_down.rearrange("(g a) h c -> g h a c", a=2)
    out_view = out_d.rearrange("(p n) c -> p n c", p=P)
    with ExitStack() as ctx:
        m = Memory(nc, ctx, tag)
        table = m.sb("table", [P, P], U32)
        idx = [m.sb(f"idx{b}", [P, Q], U32) for b in range(2)]
        rows = [m.sb(f"rows{b}", [P, Q, C]) for b in range(2)]
        wup = [m.sb(f"wup{b}", [P, 2, CK, 2 * H]) for b in range(2)]
        wdn = [m.sb(f"wdn{b}", [P, 2, C]) for b in range(2)]
        whi = [m.sb(f"whi{b}", [P, 2, C], F32R) for b in range(2)]
        wlo = [m.sb(f"wlo{b}", [P, 2, C], F32R) for b in range(2)]
        xT = [m.sb(f"xT{b}", [P, CK, 2, CAP]) for b in range(2)]
        sg = m.sb("sg", [P, CAP])
        gs = m.sb("gs", [P, CAP])
        hid = m.sb("hid", [P, CAP])
        split = [m.sb(f"split{a}", [P, CAP], F32R) for a in range(2)]
        res = [m.sb(f"res{b}", [P, Q, C]) for b in range(2)]
        pT = m.ps("pT", [P, 2, 2, 512])
        pU = [m.ps(f"pU{b}", [P, 2, CAP]) for b in range(2)]
        pD = m.ps("pD", [P, 2, C])

        s_tab = m.flag("tab")
        s_idx = m.flag("idx")
        s_g = [m.pool_dmas(f"g{b}") for b in range(2)]
        s_w = m.flags("w", 2)
        s_wd = m.flags("wd", 2)
        s_hi = m.flag("hi")
        s_lo = m.flag("lo")
        s_o = m.flags("o", 2)
        s_tr = m.flag("tr")
        s_ca = m.flag("ca")
        s_cd = m.flag("cd")
        s_up = m.flag("up")
        s_sg = m.flag("sg")
        s_gs = m.flag("gs")
        s_hid = m.flag("hid")
        s_dn = m.flag("dn")
        s_ea = m.flag("ea")
        s_ed = m.flag("ed")

        def skewed(eng, *stages):
            def turn(e, b):
                for what, lag in stages:
                    if not isinstance(e, int) or 0 <= e - lag < PAIRS:
                        what(e - lag, (b - lag) % 2)

            for e in range(2):
                turn(e, e)
            with eng.Fori(1, PAIRS // 2) as i:
                for b in range(2):
                    turn(i * 2 + b, b)
            for e in range(2):
                turn(PAIRS + e, e)

        def first(down):
            return lambda e, b: down(e, b, 0)

        def second(down):
            return lambda e, b: down(e, b, 1)

        with nc.Block() as block:
            @block.sync
            def _(sp):
                start(sp, s_tab, *s_w, *s_wd, *s_o)
                sp.dma_start(table[:, :], tab_d.rearrange("(p n) a -> p (n a)", p=P)).then_inc(s_tab.sem, 16)

                def load(e, b):
                    s_up.wait(sp, e - 1)
                    for a in range(2):
                        sp.dma_start(wup[b][:, a, :, :], up_view[bass.ds(e, 1), :, a, :, :]
                                     .rearrange("g p c h -> (g p) c h")).then_inc(s_w[b].sem, 16)
                    s_lo.wait(sp, e - 1)
                    for half in range(2):
                        sp.dma_start(wdn[b][half * H:(half + 1) * H, :, :], down_view[bass.ds(e, 1), :, :, :]
                                     .rearrange("g h a c -> (g h) a c")).then_inc(s_wd[b].sem, 16)

                def store_rows(e, b):
                    s_ea.wait(sp, (e + 1) * 2)
                    s_ed.wait(sp, (e + 1) * 2)
                    sp.dma_start(out_view[:, bass.ds(e * Q, Q), :], res[b][:, :, :]).then_inc(s_o[b].sem, 16)

                skewed(sp, (load, 0), (store_rows, 2))
                for b in range(2):
                    s_w[b].wait(sp, 32 * PAIRS // 2)
                    s_wd[b].wait(sp, 32 * PAIRS // 2)
                    s_o[b].wait(sp, 16 * PAIRS // 2)

            @block.gpsimd
            def _(pool):
                start(pool, s_idx, s_lo)

                def gather(e, b):
                    s_tr.wait(pool, (e - 1) * 2)
                    pool.tensor_copy(idx[b][:, :], table[:, bass.ds(e * Q, Q)]).then_inc(s_idx.sem, 1)
                    s_idx.wait(pool, e + 1)
                    for q in range(Q):
                        pool.indirect_dma_start(
                            rows[b][:, q, :], None, xn_d,
                            bass.IndirectOffsetOnAxis(ap=idx[b][:, q:q + 1], axis=0)).then_inc(s_g[b].sem, 16)

                def low_parts(e, b):
                    s_hi.wait(pool, e + 1)
                    s_dn.wait(pool, (e - 1) * Q)
                    pool.tensor_tensor(wlo[b][:, :, :], wdn[b][:, :, :], whi[b][:, :, :].bitcast(F32),
                                       ALU.subtract).then_inc(s_lo.sem, 1)

                s_tab.wait(pool, 16)
                skewed(pool, (gather, 0), (low_parts, 1))

            @block.tensor
            def _(pe):
                start(pe, s_tr, s_up, s_dn)

                def gathered(e, b):
                    s_g[b].wait(pe, (e + (2 - b)) * (8 * Q))
                    for a in range(2):
                        s_ca.wait(pe, e * 2 + a - 1)
                        s_cd.wait(pe, e * 2 + a - 1)
                        for c in range(CK):
                            for h in range(HALVES):
                                o = (c % 2) * CAP + h * P
                                t = pe.transpose(pT[:, a, c // 2, o:o + P],
                                                 rows[b][:, a * HALVES + h, c * P:(c + 1) * P], k["ident"][:, :])
                        t.then_inc(s_tr.sem, 1)

                def up(e, b):
                    s_w[b].wait(pe, (e + (2 - b)) * 16)
                    s_ca.wait(pe, (e + 1) * 2)
                    s_cd.wait(pe, (e + 1) * 2)
                    s_hid.wait(pe, e - 1)
                    for v in range(2):
                        for c in range(CK):
                            for a in range(2):
                                t = pe.matmul(pU[b][a * H:(a + 1) * H, v, :], wup[b][:, a, c, v * H:(v + 1) * H],
                                              xT[b][:, c, a, :], start=c == 0, stop=c == CK - 1)
                    t.then_inc(s_up.sem, 1)

                def down(e, b, a):
                    if a == 0:
                        s_hid.wait(pe, e + 1)
                        s_lo.wait(pe, e + 1)
                    for h in range(HALVES):
                        (s_ea, s_ed)[h].wait(pe, e * 2 + a)
                        parts = split[a][:, h * P:(h + 1) * P]
                        pe.matmul(pD[:, h, :], parts, whi[b][:, a, :], start=True, stop=False)
                        pe.matmul(pD[:, h, :], parts, wlo[b][:, a, :], start=False, stop=True
                                  ).then_inc(s_dn.sem, 1)

                skewed(pe, (gathered, 0), (second(down), 2), (up, 0), (first(down), 1))

            @block.scalar
            def _(act):
                start(act, s_ca, s_sg, s_hi, s_ea)

                def gathered(e, b):
                    for a in range(2):
                        s_tr.wait(act, e * 2 + a + 1)
                        s_up.wait(act, e - 1)
                        act.activation(xT[b][:, 0:2, a, :], pT[:, a, 0, :].rearrange("p (c n) -> p c n", c=2),
                                       ACT.Copy).then_inc(s_ca.sem, 1)

                def high_parts(e, b):
                    s_wd[b].wait(act, (e + (2 - b)) * 16)
                    s_dn.wait(act, (e - 1) * Q)
                    act.activation(whi[b][:, :, :], wdn[b][:, :, :], ACT.Copy).then_inc(s_hi.sem, 1)

                def up(e, b):
                    s_up.wait(act, e + 1)
                    s_gs.wait(act, e * 3)
                    act.activation(sg[:, :], pU[b][:, 0, :], ACT.Sigmoid).then_inc(s_sg.sem, 1)

                def down(e, b, a):
                    s_o[b].wait(act, (e - b) * 8)
                    s_dn.wait(act, e * Q + (a * HALVES + 1))
                    act.activation(res[b][:, a * HALVES, :], pD[:, 0, :], ACT.Copy).then_inc(s_ea.sem, 1)

                skewed(act, (gathered, 0), (second(down), 2), (high_parts, 0), (up, 1), (first(down), 1))

            @block.vector
            def _(dve):
                start(dve, s_cd, s_gs, s_hid, s_ed)

                def gathered(e, b):
                    for a in range(2):
                        s_tr.wait(dve, e * 2 + a + 1)
                        s_up.wait(dve, e - 1)
                        dve.tensor_copy(xT[b][:, 2:4, a, :], pT[:, a, 1, :].rearrange("p (c n) -> p c n", c=2)
                                        ).then_inc(s_cd.sem, 1)

                def up(e, b):
                    s_sg.wait(dve, e + 1)
                    dve.tensor_tensor(gs[:, :], sg[:, :], pU[b][:, 0, :], ALU.mult).then_inc(s_gs.sem, 1)
                    s_gs.wait(dve, e * 3 + 1)
                    dve.tensor_tensor(hid[:, :], gs[:, :], pU[b][:, 1, :], ALU.mult).then_inc(s_gs.sem, 1)
                    s_gs.wait(dve, e * 3 + 2)
                    s_dn.wait(dve, e * Q)
                    halves = [slice(a * H, (a + 1) * H) for a in range(2)]
                    for a in range(2):
                        ins = dve.tensor_copy(split[a][halves[a], :], hid[halves[a], :])
                    ins.then_inc(s_gs.sem, 1)
                    s_gs.wait(dve, e * 3 + 3)
                    for a in range(2):
                        ins = dve.tensor_tensor(split[a][halves[1 - a], :], hid[halves[a], :],
                                                split[a][halves[a], :].bitcast(F32), ALU.subtract)
                    ins.then_inc(s_hid.sem, 1)

                def down(e, b, a):
                    s_o[b].wait(dve, (e - b) * 8)
                    s_dn.wait(dve, e * Q + (a * HALVES + 2))
                    dve.tensor_copy(res[b][:, a * HALVES + 1, :], pD[:, 1, :]).then_inc(s_ed.sem, 1)

                skewed(dve, (gathered, 0), (second(down), 2), (up, 1), (first(down), 1))


def combine(nc, tag, k, out_d, keep, out):
    with ExitStack() as ctx:
        m = Memory(nc, ctx, tag)
        idx = m.sb("idx", [P, TURN, TOPK], U32)
        got = [m.sb(f"got{j}", [P, TOPK, C]) for j in range(TURN)]
        wst = m.sb("wst", [P, TURN, TOPK])
        s_z = m.flag("z")
        s_idx = m.flag("idx")
        s_g = [m.pool_dmas(f"g{j}") for j in range(TURN)]
        s_ws = m.flag("ws")
        s_add = m.flag("add")
        s_out = m.flag("out")
        out_view = out.rearrange("b (i p) c -> p (b i) c", p=P)

        def tiles(eng, tile):
            with eng.Fori(0, NTURN) as i:
                for j in range(TURN):
                    tile(i, i * TURN + j, j)

        with nc.Block() as block:
            @block.gpsimd
            def _(pool):
                start(pool, s_idx)

                def tile(i, t, j):
                    s_z.wait(pool, j + 1)
                    s_add.wait(pool, (t - TURN + 1) * TOPK)
                    pool.tensor_copy(idx[:, j, :], keep["slot"][:, bass.ds(t, 1), :].rearrange("p a q -> p (a q)")
                                     ).then_inc(s_idx.sem, 1)
                    s_idx.wait(pool, t + 1)
                    for q in range(TOPK):
                        pool.indirect_dma_start(
                            got[j][:, q, :], None, out_d,
                            bass.IndirectOffsetOnAxis(ap=idx[:, j, q:q + 1], axis=0),
                            bounds_check=ROWS - 1, oob_is_err=False).then_inc(s_g[j].sem, 16)

                tiles(pool, tile)

            @block.vector
            def _(dve):
                start(dve, s_z, s_add, s_ws)

                def tile(i, t, j):
                    x = k["x"][:, bass.ds(t, 1), :].rearrange("p a c -> p (a c)")
                    dve.tensor_copy(wst[:, j, :], keep["w"][:, bass.ds(t, 1), :].rearrange("p a q -> p (a q)")
                                    ).then_inc(s_ws.sem, 1)
                    s_ws.wait(dve, t + 1)
                    s_g[j].wait(dve, (i + 1) * (16 * TOPK))
                    for q in range(TOPK):
                        s_add.wait(dve, t * TOPK + q)
                        dve.scalar_tensor_tensor(x, got[j][:, q, :], wst[:, j, q:q + 1], x, ALU.mult,
                                                 ALU.add).then_inc(s_add.sem, 1)

                for j in range(TURN):
                    dve.memset(got[j][:, :, :], 0.0).then_inc(s_z.sem, 1)
                tiles(dve, tile)

            @block.sync
            def _(sp):
                start(sp, s_out)

                def tile(i, t, j):
                    s_add.wait(sp, (t + 1) * TOPK)
                    sp.dma_start(out_view[:, bass.ds(t, 1), :].rearrange("p a c -> p (a c)"),
                                 k["x"][:, bass.ds(t, 1), :].rearrange("p a c -> p (a c)")).then_inc(s_out.sem, 16)

                tiles(sp, tile)
                s_out.wait(sp, 16 * NT)


DH, HQ = 32, 16
HG = 4
QT = 512
QTILES = QT // P
GROUPS = N // QT * (HQ // HG)
STEPS = S // P
PER_CHUNK = HQ // HG
DIFF_STEPS = B + 4
LOWEST = -3.4e38
UNIT = "aabb"
AB = UNIT.count("a")
MX = len(UNIT) - AB


def project(nc, tag, k, w, q_d, kT, v_sb, out_d, keep):
    wq, bq, wk, bk, wv, bv, wo, bo = w
    NORM, OUT = 3, 5
    with ExitStack() as ctx:
        m = Memory(nc, ctx, tag)
        wq_sb = m.sb("wq", [P, CK, C])
        wkv = m.sb("wkv", [P, CK, 2 * DH])
        bo_sb = m.sb("bo", [P, C])
        bkv = m.sb("bkv", [P, 2 * DH])
        idx = m.sb("idx", [P, TURN, TOPK], U32)
        wst = m.sb("wst", [P, TURN, TOPK])
        got = [m.sb(f"got{j}", [P, TOPK, C]) for j in range(TURN)]
        stats = m.sb("stats", [P, TURN, 6])
        mv = m.sb("mv", [P, TURN, 2])
        ve = m.sb("ve", [P, TURN])
        rstd = m.sb("rstd", [P, TURN])
        xn = m.sb("xn", [P, TURN, C])
        xT = m.sb("xT", [P, 2, CK, P])
        q_sb = m.sb("q", [P, 2, C])
        kb = m.sb("kb", [P, 2, DH])
        kst = m.sb("kst", [P, 2, P])
        pT = m.ps("pT", [P, 2, CK, P])
        pQ = m.ps("pQ", [P, 2, C])
        pK = m.ps("pK", [P, 2, 512])
        pS = m.ps("pS", [P, 2, 512])
        s_w = m.flag("w")
        s_clear = m.flag("clear")
        s_idx = m.flag("idx")
        s_g = [m.pool_dmas(f"g{j}") for j in range(TURN)]
        s_ws = m.flag("ws")
        s_add = m.flag("add")
        s_st = m.flag("st")
        s_ve = m.flag("ve")
        s_rs = m.flag("rs")
        s_xn = m.flag("xn")
        s_xb = m.flag("xb")
        s_tr = m.flag("tr")
        s_xT = m.flag("xT")
        s_pr = m.flag("pr")
        s_qb = m.flag("qb")
        s_kb = m.flag("kb")
        s_vb = m.flag("vb")
        s_hi = m.flag("hi")
        s_kst = m.flag("kst")
        s_kt = m.flag("kt")
        s_kc = m.flag("kc")
        s_init = m.flag("init")
        s_q = m.flags("q", 2)
        scale = float(DH) ** -0.5

        def tiles(eng, lag, tile):
            for j in range(2 * TURN):
                tile(j, j % TURN)
            with eng.Fori(2, NTURN) as i:
                for j in range(TURN):
                    tile(i * TURN + j, j)
            for j in range(lag):
                tile(NT + j, j % TURN)

        def real(t):
            return not isinstance(t, int) or 0 <= t < NT

        with nc.Block() as block:
            @block.sync
            def _(sp):
                start(sp, s_w, *s_q)
                sp.dma_start(wq_sb[:, :, :], wq.rearrange("(k p) n -> p k n", p=P)).then_inc(s_w.sem, 16)
                sp.dma_start(wkv[:, :, 0:DH], wk.rearrange("(k p) n -> p k n", p=P)).then_inc(s_w.sem, 16)
                sp.dma_start(wkv[:, :, DH:2 * DH], wv.rearrange("(k p) n -> p k n", p=P)).then_inc(s_w.sem, 16)
                for dst, src in ((bo_sb[:, :], bo), (bkv[:, 0:DH], bk), (bkv[:, DH:2 * DH], bv)):
                    sp.dma_start(dst, src.rearrange("(a n) -> a n", a=1).to_broadcast(list(dst.shape))
                                 ).then_inc(s_w.sem, 16)
                with sp.Fori(0, NTURN) as i:
                    for j in range(TURN):
                        s_qb.wait(sp, i * TURN + (j + 1))
                        sp.dma_start(q_d[bass.ds(i * (TURN * P) + j * P, P), :], q_sb[:, j % 2, :]
                                     ).then_inc(s_q[j % 2].sem, 16)
                for b in range(2):
                    s_q[b].wait(sp, 16 * NT // 2)

            @block.gpsimd
            def _(pool):
                start(pool, s_idx, s_rs)

                def tile(t, j):
                    if real(t):
                        s_add.wait(pool, (t - TURN + 1) * TOPK)
                        pool.tensor_copy(idx[:, j, :], keep["slot"][:, bass.ds(t, 1), :]
                                         .rearrange("p a q -> p (a q)")).then_inc(s_idx.sem, 1)
                        s_idx.wait(pool, t + 1)
                        for q in range(TOPK):
                            pool.indirect_dma_start(
                                got[j][:, q, :], None, out_d,
                                bass.IndirectOffsetOnAxis(ap=idx[:, j, q:q + 1], axis=0),
                                bounds_check=ROWS - 1, oob_is_err=False).then_inc(s_g[j].sem, 16)
                    if real(t - NORM):
                        n = (j - NORM) % TURN
                        s_ve.wait(pool, t - NORM + 1)
                        pool.tensor_tensor(rstd[:, n:n + 1], ve[:, n:n + 1], k["half"][:, 0:1], ALU.pow
                                           ).then_inc(s_rs.sem, 1)

                s_clear.wait(pool, TURN)
                tiles(pool, NORM, tile)

            @block.tensor
            def _(pe):
                start(pe, s_tr, s_pr, s_kt)

                def transposes(t, j):
                    s_xn.wait(pe, t + 1)
                    s_xT.wait(pe, t - 1)
                    for c in range(CK):
                        ins = pe.transpose(pT[:, j % 2, c, :], xn[:, j, c * P:(c + 1) * P], k["ident"][:, :])
                    ins.then_inc(s_tr.sem, 1)

                def products(t, j):
                    h = j % 2
                    s_xT.wait(pe, t + 1)
                    s_qb.wait(pe, t - 1)
                    for c in range(CK):
                        pe.matmul(pQ[:, h, :], xT[:, h, c, :], wq_sb[:, c, :], start=c == 0, stop=c == CK - 1)
                    s_vb.wait(pe, t - 1)
                    for c in range(CK):
                        ins = pe.matmul(pK[:, h, 0:2 * DH], xT[:, h, c, :], wkv[:, c, :], start=c == 0,
                                        stop=c == CK - 1)
                    ins.then_inc(s_pr.sem, 1)

                def keys(t, j):
                    s_kst.wait(pe, t + 1)
                    s_kc.wait(pe, t - 1)
                    pe.transpose(pS[:, j % 2, 0:P], kst[:, j % 2, :], k["ident"][:, :]).then_inc(s_kt.sem, 1)

                def tile(t, j):
                    for f, lag in ((transposes, 0), (products, 1), (keys, OUT - NORM + 1)):
                        if real(t - lag):
                            f(t - lag, (j - lag) % TURN)

                s_w.wait(pe, 6 * 16)
                tiles(pe, OUT - NORM + 1, tile)

            @block.scalar
            def _(act):
                start(act, s_xT, s_qb, s_kc)

                def copy_T(t, j):
                    s_tr.wait(act, t + 1)
                    s_pr.wait(act, t - 1)
                    act.activation(xT[:, j % 2, :, :], pT[:, j % 2, :, :], ACT.Copy).then_inc(s_xT.sem, 1)

                def queries(t, j):
                    s_pr.wait(act, t + 1)
                    s_q[j % 2].wait(act, (t - j + j // 2 * 2) * 8)
                    act.activation(q_sb[:, j % 2, :], pQ[:, j % 2, :], ACT.Copy, scale=scale).then_inc(s_qb.sem, 1)

                def keys(t, j):
                    s_kt.wait(act, t + 1)
                    act.activation(kT[:, bass.ds(t * P, P)], pS[:, j % 2, 0:P], ACT.Copy).then_inc(s_kc.sem, 1)

                def tile(t, j):
                    for f, lag in ((copy_T, 0), (queries, 1), (keys, OUT - NORM + 1)):
                        if real(t - lag):
                            f(t - lag, (j - lag) % TURN)

                tiles(act, OUT - NORM + 1, tile)

            @block.vector
            def _(dve):
                start(dve, s_clear, s_ws, s_add, s_st, s_ve, s_xn, s_xb, s_kb, s_vb, s_hi, s_kst, s_init)

                def x_tile(t):
                    return k["x"][:, bass.ds(t, 1), :].rearrange("p a c -> p (a c)")

                def weights(t, j):
                    dve.tensor_copy(wst[:, j, :], keep["w"][:, bass.ds(t, 1), :].rearrange("p a q -> p (a q)")
                                    ).then_inc(s_ws.sem, 1)

                def add_row(t, j, q):
                    if q == 0:
                        s_ws.wait(dve, t + 1)
                        s_g[j].wait(dve, (t - j + TURN) * (16 * TOPK // TURN))
                    s_add.wait(dve, t * TOPK + q)
                    dve.scalar_tensor_tensor(x_tile(t), got[j][:, q, :], wst[:, j, q:q + 1], x_tile(t), ALU.mult,
                                             ALU.add).then_inc(s_add.sem, 1)

                def moments(t, j):
                    s_add.wait(dve, (t + 1) * TOPK, apart=True)
                    dve.bn_stats(stats[:, j, :], x_tile(t)).then_inc(s_st.sem, 1)

                def aggregate(t, j):
                    s_st.wait(dve, t * 2 + 1, apart=True)
                    dve.bn_aggr(mv[:, j, :], stats[:, j, :]).then_inc(s_st.sem, 1)

                def variance(t, j):
                    s_st.wait(dve, t * 2 + 2)
                    dve.tensor_scalar(ve[:, j:j + 1], mv[:, j, 1:2], EPS, None, ALU.add).then_inc(s_ve.sem, 1)

                def normalise(t, j):
                    s_rs.wait(dve, t + 1)
                    s_tr.wait(dve, t - TURN + 1)
                    dve.tensor_scalar(xn[:, j, :], x_tile(t), mv[:, j, 0:1], rstd[:, j:j + 1],
                                      ALU.subtract, ALU.mult).then_inc(s_xn.sem, 1)

                def output_bias(t, j):
                    s_xn.wait(dve, t + 1)
                    dve.tensor_tensor(x_tile(t), x_tile(t), bo_sb[:, :], ALU.add).then_inc(s_xb.sem, 1)

                def keys(t, j):
                    h = j % 2
                    s_pr.wait(dve, t + 1)
                    s_kst.wait(dve, t - 1)
                    dve.tensor_tensor(kb[:, h, :], pK[:, h, 0:DH], bkv[:, 0:DH], ALU.add).then_inc(s_kb.sem, 1)

                def values(t, j):
                    dve.tensor_tensor(v_sb[:, bass.ds(t, 1), :].rearrange("p a d -> p (a d)"),
                                      pK[:, j % 2, DH:2 * DH], bkv[:, DH:2 * DH], ALU.add).then_inc(s_vb.sem, 1)

                def high_parts(t, j):
                    h = j % 2
                    s_kb.wait(dve, t + 1)
                    s_kt.wait(dve, t - 1)
                    dve.tensor_copy(kst[:, h, 0:2 * DH].rearrange("p (r d) -> p r d", r=2).bitcast(F32R),
                                    kb[:, h, :].unsqueeze(1).to_broadcast([P, 2, DH])).then_inc(s_hi.sem, 1)

                def low_parts(t, j):
                    h = j % 2
                    s_hi.wait(dve, t + 1)
                    dve.tensor_tensor(kst[:, h, 2 * DH:3 * DH], kb[:, h, :], kst[:, h, 0:DH],
                                      ALU.subtract).then_inc(s_kst.sem, 1)

                def tile(t, j):
                    for f, lag in ((weights, 0), (0, 0), (moments, 1), (normalise, NORM), (1, 0), (aggregate, 1),
                                   (keys, OUT), (2, 0), (variance, 1), (values, OUT), (3, 0), (high_parts, OUT),
                                   (4, 0), (low_parts, OUT), (output_bias, NORM), (5, 0)):
                        if real(t - lag):
                            at = (t - lag, (j - lag) % TURN)
                            if isinstance(f, int):
                                add_row(*at, f)
                            else:
                                f(*at)

                for j in range(TURN):
                    dve.memset(got[j][:, :, :], 0.0).then_inc(s_clear.sem, 1)
                dve.memset(kst[:, :, :], 0.0).then_inc(s_init.sem, 1)
                s_init.wait(dve, 1)
                dve.memset(kst[:, :, 3 * DH:3 * DH + 2], 1.0).then_inc(s_init.sem, 1)
                s_init.wait(dve, 2)
                s_w.wait(dve, 6 * 16)
                tiles(dve, OUT, tile)


def attention(nc, tag, k, w, q_d, out_d, keep):
    bq, wo = w[1], w[6]
    with ExitStack() as ctx:
        m = Memory(nc, ctx, tag)
        kT = m.sb("kT", [P, N], F32R)
        kdiff = m.sb("kdiff", [P, B, AB, 512], F32R)
        v_sb = m.sb("v", [P, NT, DH])
        project(nc, tag + "p", k, w, q_d, kT, v_sb, out_d, keep)

        RING = 3
        PR = 4
        PAIRS = 4
        SUMS = 2 * (STEPS // 2 - 1)
        RELUS = 2
        last = GROUPS - 1

        wo_sb = m.sb("wo", [P, PER_CHUNK, C])
        bq_sb = m.sb("bq", [P, C])
        qc = [m.sb(f"qc{b}", [P, QTILES, P]) for b in range(2)]
        rows = m.sb("rows", [P, QTILES, HG, P])
        qT = m.sb("qT", [P, 2, HG * QT], F32R)
        relus = [m.sb(f"relu{b}", [P, 512]) for b in range(RELUS)]
        shift = m.sb("shift", [P, QTILES, HG, DH])
        mx = m.sb("mx", [P, QTILES * HG, MX])
        nmax = m.sb("nmax", [P, QTILES, HG])
        prob = [m.sb(f"prob{b}", [P, 2, HG * QT]) for b in range(PR // 2)]
        pair = [m.sb(f"pair{b}", [P, HG * QT]) for b in range(PAIRS)]
        o_sb, d_sb = (m.sb(n, [P, QT]) for n in ("o", "d"))
        pS = m.ps("pS", [P, HG, 512])
        pO = m.ps("pO", [P, QT])
        pR = m.ps("pR", [P, RING, 512])

        s_wo = m.flag("wo")
        s_bq = m.flag("bq")
        s_qc = m.flags("qc", 2)
        s_init = m.flag("init")
        s_diff = m.flag("diff")
        s_clear = m.flag("clear")
        s_pool = m.flag("pool")
        s_rows = m.flag("rows")
        s_put = m.flag("put")
        s_dve = m.flag("dve")
        s_act = m.flag("act")
        s_shift = m.flag("shift")
        s_mx = m.flag("mx")
        s_sc = m.flag("sc")
        s_ex = m.flag("ex")
        s_pv = m.flag("pv")
        s_pair = m.flag("pair")
        s_sum = m.flag("sum")
        s_oc = m.flag("oc")
        s_rec = m.flag("rec")
        s_oT = m.flag("oT")

        def items(G):
            if G == -1:
                queries = [("q", 0), ("r", 0)] * (HG // 2)
                return queries + [(x, 0) for x in UNIT] * (QTILES * HG) + [("s", 0)] * 2 + queries
            if G == GROUPS:
                return [("d", 0)] + [("o", 0)] * QTILES
            before, after = G > 0, G < last
            if not after:
                return [("d", 3)] + [("o", 7)] * QTILES
            what = list(UNIT) * (QTILES * HG)
            for kind, at in ([("d", 12)] + [("o", 37 + 5 * t) for t in range(QTILES)]) * before:
                what.insert(at, kind)
            steps = STEPS - 2
            placed = [(x, n * steps // len(what)) for n, x in enumerate(what)]
            return placed + [("s", steps)] * 2 + [("q", steps + 1), ("r", steps + 1)] * (HG // 2 * (G < last - 1))

        LISTS = {G: items(G) for G in range(-1, GROUPS + 1)}
        WHO = {"p": "abcdoqrs", "d": "bcdors", "a": "aq"}

        def number(what, who):
            return sum(x in WHO[who] for x, _ in what)

        class Ring:

            def __init__(self, G):
                static = isinstance(G, int)
                at = G if static else 1
                self.list, self.prev = LISTS[at], LISTS.get(at - 1 if static else at, [])
                self.what = [x for x, _ in self.list]
                base = {who: sum(number(LISTS[g], who) for g in range(-1, at)) for who in WHO}
                self.bank0 = base["p"] % RING
                full = {who: number(LISTS[1], who) for who in WHO}
                assert full["p"] % RING == 0
                self.base = base if static else {who: G * full[who] + (base[who] - full[who]) for who in WHO}

            def upto(self, who, n):
                if n >= 0:
                    return self.base[who] + number(self.list[:n + 1], who)
                rest = number(self.prev[len(self.prev) + n + 1:], who)
                return self.base[who] - rest if rest else self.base[who]

            def find(self, kind, at, prev=False):
                what = [x for x, _ in (self.prev if prev else self.list)]
                where = [n for n, x in enumerate(what) if x == kind]
                return where[at] - (len(what) if prev else 0)

            def bank(self, n):
                return pR[:, (self.bank0 + n) % RING, :]

            def filled(self, eng, n, apart=False):
                s_put.wait(eng, self.upto("p", n), apart)
                return self.bank(n)

            def emptied(self, pe, n, apart=False):
                at = n - RING
                if at >= 0 or self.prev:
                    by_dve = (self.list if at >= 0 else self.prev)[at][0] in WHO["d"]
                    if by_dve:
                        s_dve.wait(pe, self.upto("d", at), apart)
                    else:
                        s_act.wait(pe, self.upto("a", at), apart)
                return self.bank(n)

        def events(G):
            placed = LISTS[G if isinstance(G, int) else 1]
            before, after = not isinstance(G, int) or G > 0, not isinstance(G, int) or G < last
            for t in range(STEPS):
                mine = [("item", n) for n, (_, step) in enumerate(placed) if step == t]
                more = t < STEPS - 1 or after
                sc = [("scores", t + 1, 0), ("scores", t + 1, 1)] if more else [None, None]
                if t < STEPS - 2:
                    out = [sc[0]] + mine[0:2] + [sc[1]] + mine[2:3] + [("values", t)] + mine[3:]
                elif t == STEPS - 2:
                    out = sc + [("values", t)] + mine
                else:
                    out = mine[0:2] + [("values", t)] + [sc[0]] + mine[2:3] + [sc[1]] + mine[3:]
                yield from (e for e in out if e is not None)

        with nc.Block() as block:
            @block.sync
            def _(sp):
                start(sp, s_wo, s_bq, *s_qc)
                sp.dma_start(bq_sb[:, :], bq.rearrange("(a n) -> a n", a=1).to_broadcast([P, C])).then_inc(s_bq.sem, 16)
                sp.dma_start(wo_sb[:, :, :], wo.rearrange("(g p) n -> p g n", p=P)).then_inc(s_wo.sem, 16)
                view = q_d.rearrange("(c t p) (g n) -> c g p t n", t=QTILES, p=P, g=PER_CHUNK)
                with sp.Fori(0, GROUPS // 2) as i:
                    for b in range(2):
                        s_rows.wait(sp, i * 2 + (b - 1))
                        c, g = i // (PER_CHUNK // 2), i % (PER_CHUNK // 2) * 2 + b
                        sp.dma_start(qc[b][:, :, :], view[bass.ds(c, 1), bass.ds(g, 1), :, :, :]
                                     .rearrange("c g p t n -> (c g p) t n")).then_inc(s_qc[b].sem, 16)
                for b in range(2):
                    s_qc[b].wait(sp, 16 * (GROUPS // 2))
                s_wo.wait(sp, 16)
                s_bq.wait(sp, 16)

            @block.gpsimd
            def _(pool):
                start(pool, s_init, s_pool, s_rows, s_pair, s_oT)

                def query_rows(G, b, part):
                    q = qc[b][:, :, :].rearrange("p t (h d) -> p t h d", h=HG)
                    if part == 0:
                        s_qc[b].wait(pool, (G - b) * 8 + 16)
                        bias = bq_sb[:, bass.ds(G % PER_CHUNK * P, P)].unsqueeze(1).to_broadcast([P, QTILES, P])
                        pool.tensor_tensor(qc[b][:, :, :], qc[b][:, :, :], bias, ALU.add).then_inc(s_pool.sem, 1)
                    elif part < 3:
                        if part == 1:
                            s_pool.wait(pool, G * 3 + 2)
                            if not (isinstance(G, int) and G == 0):
                                s_put.wait(pool, HG if isinstance(G, int) and G == 1 else
                                           Ring(G - 2).upto("p", -1))
                        o = (part - 1) * 2 * DH
                        pool.tensor_copy(rows[:, :, :, o:o + DH].bitcast(F32R), q).then_inc(s_pool.sem, 1)
                    else:
                        s_pool.wait(pool, (G + 1) * 3 + 1)
                        pool.tensor_tensor(rows[:, :, :, DH:2 * DH], q, rows[:, :, :, 0:DH],
                                           ALU.subtract).then_inc(s_rows.sem, 1)

                def add_pair(r, G, n):
                    s_ex.wait(pool, G * (2 * STEPS) + 4 * (n + 1))
                    if n >= PAIRS:
                        s_sum.wait(pool, G * SUMS + 2 * (n - PAIRS + 1))
                    elif not (isinstance(G, int) and G == 0):
                        if n < PAIRS - 1:
                            s_sum.wait(pool, (G - 1) * SUMS + 2 * (n + STEPS // 2 - PAIRS + 1))
                        else:
                            s_put.wait(pool, r.upto("p", r.find("d", 0)))
                    pool.tensor_tensor(pair[n % PAIRS][:, :], prob[n % 2][:, 0, :], prob[n % 2][:, 1, :],
                                       ALU.add).then_inc(s_pair.sem, 1)

                def normalise(G):
                    s_oc.wait(pool, G + 1)
                    s_rec.wait(pool, (G + 1) * 2)
                    pool.tensor_tensor(o_sb[:, :], o_sb[:, :], d_sb[:, :], ALU.mult).then_inc(s_oT.sem, 1)

                PARTS_AT = (0, 2, 3, 4)

                def body(G, b, before=True, ahead=True):
                    r = Ring(G)
                    for n in range(STEPS // 2):
                        add_pair(r, G, n)
                        if n == 1 and before:
                            normalise(G - 1)
                        if ahead and n in PARTS_AT:
                            query_rows(G + 2, b, PARTS_AT.index(n))

                pool.memset(rows[:, :, :, :], 0.0).then_inc(s_init.sem, 1)
                s_init.wait(pool, 1)
                s_bq.wait(pool, 16)
                pool.tensor_scalar(bq_sb[:, :], bq_sb[:, :], float(DH) ** -0.5, None, ALU.mult).then_inc(s_pool.sem, 1)
                s_pool.wait(pool, 1)
                for part in range(4):
                    query_rows(0, 0, part)
                for part in range(4):
                    query_rows(1, 1, part)
                body(0, 0, before=False)
                with pool.Fori(0, (GROUPS - 4) // 2) as i:
                    for b in (1, 0):
                        body(i * 2 + (2 - b), b)
                body(last - 2, 1)
                body(last - 1, 0, ahead=False)
                body(last, 1, ahead=False)
                normalise(last)

            @block.scalar
            def _(act):
                start(act, s_ex, s_oc, s_act)

                def exps(G, t, h):
                    s_sc.wait(act, G * (2 * STEPS) + (2 * t + h + 1))
                    if h == 0:
                        s_pv.wait(act, G * STEPS + (t - PR + 1))
                        s_pair.wait(act, G * (STEPS // 2) + ((t - PR) // 2 + 1))
                    act.activation(prob[t // 2 % 2][:, t % 2, 2 * h * QT:2 * (h + 1) * QT], pS[:, 2 * h:2 * h + 2, :],
                                   ACT.Exp).then_inc(s_ex.sem, 1)

                def query_rows(r, n, G, h):
                    act.activation(qT[:, bass.ds(G % 2, 1), h * QT:(h + 1) * QT].rearrange("p a n -> p (a n)"),
                                   r.filled(act, n), ACT.Copy).then_inc(s_act.sem, 1)

                def relu(r, n, at):
                    bank = r.filled(act, n)
                    if at >= RELUS:
                        s_dve.wait(act, r.upto("d", r.find("b", at - RELUS)))
                    elif r.prev and "b" in [x for x, _ in r.prev]:
                        s_dve.wait(act, r.upto("d", r.find("b", at - RELUS, prev=True)))
                    act.activation(relus[at % RELUS][:, :], bank, ACT.Relu).then_inc(s_act.sem, 1)

                def copy_o(G):
                    s_pv.wait(act, (G + 1) * STEPS)
                    if not (isinstance(G, int) and G == 0):
                        r = Ring(G + 1)
                        s_put.wait(act, r.upto("p", r.find("o", -1, prev=True)))
                    act.activation(o_sb[:, :], pO[:, :], ACT.Copy).then_inc(s_oc.sem, 1)

                def emptying(r, G, n, seen):
                    kind = r.what[n]
                    at = seen.get(kind, 0)
                    seen[kind] = at + 1
                    if kind == "q":
                        query_rows(r, n, G + 2, 2 * at)
                    elif kind == "a":
                        relu(r, n, at)

                def body(G, before=True):
                    r, seen = Ring(G), {}
                    if before:
                        copy_o(G - 1)
                    for what, *at in events(G):
                        if what == "scores":
                            t, h = at
                            exps(G + t // STEPS, t % STEPS, h)
                        elif what == "item":
                            emptying(r, G, at[0], seen)

                r, seen = Ring(-1), {}
                for n, kind in enumerate(r.what):
                    if n == len(r.what) - HG:
                        for h in range(2):
                            exps(0, 0, h)
                    if kind == "q":
                        query_rows(r, n, int(n > HG), n % HG if n < HG else n - (len(r.what) - HG))
                    elif kind == "a":
                        emptying(r, -1, n, seen)
                body(0, before=False)
                with act.Fori(1, last - 1) as G:
                    body(G)
                body(last - 1)
                body(last)
                copy_o(last)

            @block.tensor
            def _(pe):
                start(pe, s_put, s_sc, s_pv)

                def query_rows(r, n, G, h):
                    if h == 0:
                        s_rows.wait(pe, G + 1)
                        if not (isinstance(G, int) and G < 2):
                            s_ex.wait(pe, (G - 1) * (2 * STEPS) - 2)
                    bank = r.emptied(pe, n)
                    for t in range(QTILES):
                        ins = pe.transpose(bank[:, t * P:(t + 1) * P], rows[:, t, h, :], k["ident"][:, :])
                    ins.then_inc(s_put.sem, 1)

                def max_scores(r, n, at, b, batch):
                    kind = r.what[n]
                    unit, i = at // UNIT.count(kind), at % UNIT.count(kind)
                    t, h = unit // HG, unit % HG
                    key = batch * S + (2 * i + 1 if kind == "b" else 2 * AB + i) * 512
                    keys = kdiff[:, batch, i, :] if kind == "a" else kT[:, key:key + 512]
                    pe.matmul(r.emptied(pe, n), qT[:, b, h * QT + t * P:h * QT + (t + 1) * P], keys,
                              start=True, stop=True).then_inc(s_put.sem, 1)

                def shifts(r, n, G, at):
                    if at == 0:
                        s_shift.wait(pe, G + 1)
                    bank = r.emptied(pe, n, apart=True)
                    for t in range(QTILES):
                        ins = pe.transpose(bank[0:2 * DH, t * P:(t + 1) * P],
                                           shift[:, t, 2 * at:2 * at + 2, :].rearrange("p h d -> p (h d)"),
                                           k["ident"][:, :])
                    ins.then_inc(s_put.sem, 1)

                def output(r, n, G, g, t):
                    if t == 0:
                        s_oT.wait(pe, G + 1)
                    w_g = wo_sb[:, bass.ds(g, 1), :].rearrange("p g n -> p (g n)")
                    pe.matmul(r.emptied(pe, n), o_sb[:, t * P:(t + 1) * P], w_g, start=True, stop=True
                              ).then_inc(s_put.sem, 1)

                def denominators(r, n, G):
                    s_sum.wait(pe, (G + 1) * SUMS)
                    bank = r.emptied(pe, n)
                    for h in range(HG):
                        ins = pe.matmul(bank[h * DH:(h + 1) * DH, :], k["ones32"][:, :],
                                        pair[PAIRS - 1][:, h * QT:(h + 1) * QT], start=True, stop=True)
                    ins.then_inc(s_put.sem, 1)

                def scores(G, t, half, b, batch):
                    if t == 0 and half == 0:
                        r = Ring(G - 1)
                        s_dve.wait(pe, r.upto("d", r.find("s", -1)))
                    s_ex.wait(pe, G * (2 * STEPS) + (2 * t + half - 1))
                    key = batch * S + t * P
                    for h in (2 * half, 2 * half + 1):
                        ins = pe.matmul(pS[:, h, :], kT[:, key:key + P], qT[:, b, h * QT:(h + 1) * QT],
                                        start=True, stop=True)
                    ins.then_inc(s_sc.sem, 1)

                def values(G, t, batch):
                    s_ex.wait(pe, G * (2 * STEPS) + 2 * (t + 1))
                    if t == 0:
                        s_oc.wait(pe, G)
                    for h in range(HG):
                        ins = pe.matmul(pO[h * DH:(h + 1) * DH, :], v_sb[:, batch * STEPS + t, :],
                                        prob[t // 2 % 2][:, t % 2, h * QT:(h + 1) * QT],
                                        start=t == 0, stop=t == STEPS - 1)
                    ins.then_inc(s_pv.sem, 1)

                def body(G, b, batch, g_before=None, after=None):
                    r, seen = Ring(G), {}
                    for what, *at in events(G):
                        if what == "scores":
                            t, half = at
                            if t < STEPS:
                                scores(G, t, half, b, batch)
                            else:
                                scores(G + 1, 0, half, 1 - b, after)
                        elif what == "values":
                            values(G, at[0], batch)
                        else:
                            n = at[0]
                            kind = r.what[n]
                            i = seen.get(kind, 0)
                            seen[kind] = i + 1
                            if kind in "qr":
                                query_rows(r, n, G + 2, 2 * i + (kind == "r"))
                            elif kind in "abc":
                                if (kind, i) == ("a", 0):
                                    s_act.wait(pe, r.upto("a", -1))
                                    s_dve.wait(pe, r.upto("d", -1))
                                max_scores(r, n, i, 1 - b, after)
                            elif kind == "o":
                                output(r, n, G - 1, g_before, i)
                            elif kind == "d":
                                denominators(r, n, G - 1)
                            else:
                                shifts(r, n, G + 1, i)

                r = Ring(-1)
                for h in range(HG):
                    query_rows(r, h, 0, h)
                s_diff.wait(pe, DIFF_STEPS)
                s_act.wait(pe, HG // 2)
                s_dve.wait(pe, HG // 2)
                seen = dict.fromkeys(UNIT, 0)
                for n in range(HG, len(r.what) - HG - 2):
                    max_scores(r, n, seen[r.what[n]], 0, 0)
                    seen[r.what[n]] += 1
                n = len(r.what) - HG
                for h in range(2):
                    shifts(r, n - 2 + h, 0, h)
                for h in range(2):
                    scores(0, 0, h, 0, 0)
                for h in range(HG):
                    query_rows(r, n + h, 1, h)
                s_wo.wait(pe, 16)
                half = GROUPS // B
                body(0, 0, 0, None, 0)
                with pe.Fori(0, half // 2 - 1) as i:
                    for b in (1, 0):
                        body(i * 2 + (2 - b), b, 0, (i % 2) * 2 + (1 - b), 0)
                body(half - 1, 1, 0, PER_CHUNK - 2, 1)
                body(half, 0, 1, PER_CHUNK - 1, 1)
                with pe.Fori(half // 2, half - 2) as i:
                    for b in (1, 0):
                        body(i * 2 + (2 - b), b, 1, (i % 2) * 2 + (1 - b), 1)
                body(last - 2, 1, 1, PER_CHUNK - 4, 1)
                body(last - 1, 0, 1, PER_CHUNK - 3, 1)
                body(last, 1, 1, PER_CHUNK - 2, None)
                r = Ring(GROUPS)
                denominators(r, 0, last)
                for t in range(QTILES):
                    output(r, 1 + t, last, PER_CHUNK - 1, t)

            @block.vector
            def _(dve):
                start(dve, s_dve, s_diff, s_shift, s_mx, s_clear, s_sum, s_rec)

                def max_scores(r, n, at):
                    kind = r.what[n]
                    unit, i = at // UNIT.count(kind), at % UNIT.count(kind)
                    if kind == "c":
                        dve.tensor_reduce(mx[:, unit, AB + i:AB + i + 1], r.filled(dve, n), X, ALU.max
                                          ).then_inc(s_dve.sem, 1)
                        return
                    s_act.wait(dve, r.upto("a", r.find("a", at)), apart=True)
                    bank = r.filled(dve, n, apart=True)
                    buf = relus[at % RELUS][:, :]
                    dve.tensor_tensor_reduce(buf, buf, bank, 1.0, LOWEST, ALU.add, ALU.max, mx[:, unit, i:i + 1]
                                             ).then_inc(s_dve.sem, 1)

                def make_shifts(r, G):
                    s_dve.wait(dve, r.upto("d", max(r.find(x, -1) for x in set(UNIT) - {"a"})))
                    s_shift.wait(dve, G)
                    dve.tensor_reduce(nmax[:, :, :].rearrange("p t h -> p (t h)"), mx[:, :, :], X, ALU.max,
                                      negate=True).then_inc(s_mx.sem, 1)
                    s_mx.wait(dve, G * 2 + 1)
                    dve.tensor_copy(shift[:, :, :, 0].bitcast(F32R), nmax[:, :, :]).then_inc(s_mx.sem, 1)
                    s_mx.wait(dve, G * 2 + 2)
                    dve.tensor_tensor(shift[:, :, :, 1], nmax[:, :, :], shift[:, :, :, 0], ALU.subtract
                                      ).then_inc(s_shift.sem, 1)

                def query_rows(r, n, G, h):
                    dve.tensor_copy(qT[:, bass.ds(G % 2, 1), h * QT:(h + 1) * QT].rearrange("p a n -> p (a n)"),
                                    r.filled(dve, n)).then_inc(s_dve.sem, 1)

                def shifts(r, n, G, at):
                    bank = r.filled(dve, n)
                    for h in range(2):
                        o = (2 * at + h) * QT
                        ins = dve.tensor_copy(
                            qT[3 * DH:4 * DH, bass.ds(G % 2, 1), o:o + QT].rearrange("p a n -> p (a n)"),
                            bank[h * DH:(h + 1) * DH, :])
                    ins.then_inc(s_dve.sem, 1)

                def output(r, n, chunk, t):
                    bank = r.filled(dve, n)
                    x = k["x"][:, bass.ds(chunk * QTILES + t, 1), :].rearrange("p a c -> p (a c)")
                    s_dve.wait(dve, r.base["d"])
                    dve.tensor_tensor(x, x, bank, ALU.add).then_inc(s_dve.sem, 1)

                def denominators(r, n, G):
                    bank = r.filled(dve, n)
                    s_oT.wait(dve, G)
                    dve.tensor_copy(d_sb[:, :], bank).then_inc(s_dve.sem, 1)

                HALF = HG * QT // 2

                def reciprocals(r, n, half):
                    s_dve.wait(dve, r.upto("d", n))
                    part = d_sb[:, half * (QT // 2):(half + 1) * (QT // 2)]
                    dve.reciprocal(part, part).then_inc(s_rec.sem, 1)

                def add_pair(G, n, half):
                    s_pair.wait(dve, G * (STEPS // 2) + (n + 1))
                    s_sum.wait(dve, G * SUMS + 2 * (n - 1))
                    part = slice(half * HALF, (half + 1) * HALF)
                    now, before = pair[n % PAIRS][:, part], pair[(n - 1) % PAIRS][:, part]
                    dve.tensor_tensor(now, now, before, ALU.add).then_inc(s_sum.sem, 1)

                def body(G, before=True, prepare=True):
                    r = Ring(G)
                    extra = {}
                    end = len(r.what)

                    def put(at, f, *args):
                        extra.setdefault(min(at, end), []).append((f, *args))

                    if before:
                        d = r.find("d", 0)
                        for half in range(2):
                            put(prepare * (5 + 3 * half), add_pair, G - 1, STEPS // 2 - 1, half)
                            put(d + 1 + prepare * (2 + 3 * half), reciprocals, r, d, half)
                    for n in range(1, STEPS // 2 - 1):
                        for half in range(2):
                            put(10 * n + 12 + 3 * half if prepare and n < STEPS // 2 - 2 else end, add_pair, G, n, half)
                    seen = {}
                    for n, kind in enumerate(r.what):
                        for f, *args in extra.get(n, []):
                            f(*args)
                        if kind == "s" and "s" not in seen:
                            make_shifts(r, G + 1)
                        i = seen.get(kind, 0)
                        seen[kind] = i + 1
                        if kind in "bc":
                            max_scores(r, n, i)
                        elif kind == "r":
                            query_rows(r, n, G + 2, 2 * i + 1)
                        elif kind == "s":
                            shifts(r, n, G + 1, i)
                        elif kind == "o":
                            output(r, n, (G - 1) // PER_CHUNK, i)
                        elif kind == "d":
                            denominators(r, n, G - 1)
                    for f, *args in extra.get(len(r.what), []):
                        f(*args)
                chunks = kT[:, :].bitcast(F32).rearrange("p (b j a n) -> p b j a n", b=B, a=2, n=512)[:, :, 0:AB]
                exact, rest = (pair[i][:, 0:B * AB * 512].rearrange("p (b j n) -> p b j n", b=B, n=512)
                               for i in range(2))
                hi, lo = slice(0, 2 * DH), slice(2 * DH, 3 * DH)
                dve.memset(kdiff[3 * DH:4 * DH].bitcast(F32), 0.0).then_inc(s_diff.sem, 1)
                for g in range(B):
                    dve.tensor_tensor(exact[0:3 * DH, g], chunks[0:3 * DH, g, :, 0, :], chunks[0:3 * DH, g, :, 1, :],
                                      ALU.subtract).then_inc(s_diff.sem, 1)
                s_diff.wait(dve, 1 + B)
                dve.tensor_copy(kdiff[hi], exact[hi]).then_inc(s_diff.sem, 1)
                s_diff.wait(dve, 2 + B)
                dve.tensor_tensor(rest[lo], exact[0:DH], kdiff[0:DH].bitcast(F32), ALU.subtract
                                  ).then_inc(s_diff.sem, 1)
                s_diff.wait(dve, 3 + B)
                dve.tensor_tensor(kdiff[lo], exact[lo], rest[lo], ALU.add).then_inc(s_diff.sem, 1)
                dve.memset(shift[:, :, :, :], 0.0).then_inc(s_clear.sem, 1)
                s_clear.wait(dve, 1)
                r = Ring(-1)
                seen = dict.fromkeys(r.what, 0)
                for n, kind in enumerate(r.what):
                    i = seen[kind]
                    seen[kind] += 1
                    if kind in "bc":
                        max_scores(r, n, i)
                    elif kind == "r":
                        query_rows(r, n, int(n > HG), 2 * (i % (HG // 2)) + 1)
                    elif kind == "s":
                        if i == 0:
                            make_shifts(r, 0)
                        shifts(r, n, 0, i)
                body(0, before=False)
                with dve.Fori(1, last - 1) as G:
                    body(G)
                body(last - 1)
                body(last, prepare=False)
                for half in range(2):
                    add_pair(last, STEPS // 2 - 1, half)
                r = Ring(GROUPS)
                denominators(r, 0, last)
                for half in range(2):
                    reciprocals(r, 0, half)
                for t in range(QTILES):
                    output(r, 1 + t, last // PER_CHUNK, t)


def program(nc, x_in, wq, bq, wk, bk, wv, bv, wo, bo, w_gate, w_su, w_sd, w_up, w_down, out):
    with ExitStack() as ctx:
        m = Memory(nc, ctx, "g")
        for eng in (nc.gpsimd, nc.tensor, nc.vector):
            Flag.passed[eng.engine] = m.flag(f"passed_{eng.engine.name}").sem
        xn_d = nc.dram_tensor("xn_rows", (N, C), F32).ap()
        out_d = nc.dram_tensor("expert_rows", (ROWS, C), F32).ap()
        q_d = nc.dram_tensor("q_rows", (N, C), F32).ap()
        tables = [nc.dram_tensor(f"slot_table{n}", (ROWS, 1), U32).ap() for n in range(2)]
        k = setup(nc, ctx, x_in, tables)
        keep = {"slot": m.sb("slot", [P, NT, TOPK], U32), "w": m.sb("w", [P, NT, TOPK])}
        for n, table in enumerate(tables):
            route(nc, f"route{n}", k, (w_gate, w_su, w_sd), xn_d, table, keep)
            experts(nc, f"experts{n}", k, w_up, w_down, xn_d, table, out_d)
            if n == 0:
                attention(nc, "attention", k, (wq, bq, wk, bk, wv, bv, wo, bo), q_d, out_d, keep)
            else:
                combine(nc, "combine", k, out_d, keep, out)


_INS = ['L0_attn_x', 'L0_attn_Wq', 'L0_attn_bq', 'L0_attn_Wk', 'L0_attn_bk', 'L0_attn_Wv', 'L0_attn_bv', 'L0_attn_Wo', 'L0_attn_bo', 'L0_ffn_w_gate', 'L0_ffn_w_shared_up', 'L0_ffn_w_shared_down', 'L0_ffn_w_up', 'L0_ffn_w_down']
_OUTS = [((B, S, C), 'float32')]


def kernel(**inputs):
    import numpy as _np
    import concourse.bacc as _bacc
    from concourse import mybir as _mybir
    from concourse.bass_utils import run_bass_kernel_spmd as _run

    nc = _bacc.Bacc("TRN2", target_bir_lowering=False, num_devices=1)
    arrays, args = {}, []
    for name in _INS:
        a = _np.ascontiguousarray(inputs[name])
        arrays[f"in_{name}_dram"] = a
        args.append(nc.dram_tensor(f"in_{name}_dram", a.shape, _mybir.dt.from_np(a.dtype), kind="ExternalInput").ap())
    for i, (shape, dtype) in enumerate(_OUTS):
        dt = _mybir.dt.from_np(_np.dtype(dtype))
        args.append(nc.dram_tensor(f"out_{i}_dram", shape, dt, kind="ExternalOutput").ap())
    program(nc, *args)
    r = _run(nc, [arrays], core_ids=[0])
    got = tuple(r.results[0][f"out_{i}_dram"] for i in range(len(_OUTS)))
    return got[0]
```
